# Optimizing a Trainium2 kernel written in Bass

```python
import numpy as np
import jax
import jax.numpy as jnp

def _softmax(x, axis=-1):
    return jax.nn.softmax(x, axis=axis)

def _gelu(x):
    return jax.nn.gelu(x, approximate=True)

def _silu(x):
    return jax.nn.silu(x)

def _sigmoid(x):
    return jax.nn.sigmoid(x)

def _layernorm(x, axis=-1, eps=1e-05):
    m = jnp.mean(x, axis=axis, keepdims=True)
    v = jnp.var(x, axis=axis, keepdims=True)
    return (x - m) / jnp.sqrt(v + eps)

def _scatter_add(tgt, idx, src, axis=0):
    return tgt.at[idx].add(src)

def _segment_sum(src, seg, n):
    return jax.ops.segment_sum(src, seg, n)
kernel_name = 'mk_flamingo_gated_d1_seqx_r4_629428'

def setup_inputs(seed: int=0):
    np.random.seed(seed)
    _w = jnp.asarray

    def _rec_inputs():
        import jax
        import jax.numpy as jnp
        _rk = jax.random.key(seed)
        x = -0.0002928 + 1 * jax.random.normal(jax.random.fold_in(_rk, 1), (32, 256, 256), jnp.float32)
        _lenS = 256 - jax.random.randint(jax.random.fold_in(_rk, 7), (32,), 0, max(1, 256 // 4) + 1, jnp.int32)
        _lenS2 = 77 - jax.random.randint(jax.random.fold_in(_rk, 8), (32,), 0, max(1, 77 // 4) + 1, jnp.int32)
        _ctx_2048P = jax.random.normal(jax.random.fold_in(_rk, 11), (32, 16, 512), jnp.float32)
        _ctx_2048c = jax.random.dirichlet(jax.random.fold_in(_rk, 511), 0.3 * jnp.ones((16,), jnp.float32), (32, 77))
        _ctx_2048t = jnp.einsum('bsk,bkd->bsd', _ctx_2048c, _ctx_2048P)
        _ctx_2048t = _ctx_2048t * jax.lax.rsqrt(jnp.mean(jnp.square(_ctx_2048t)) + 1e-12) * 0.953939
        ctx_2048 = -0.000514642 + 1.00011 * (_ctx_2048t + 0.3 * jax.random.normal(jax.random.fold_in(_rk, 611), (32, 77, 512), jnp.float32))
        _g = jax.random.normal(jax.random.fold_in(_rk, 9001), (2, 1), jnp.float32)
        _g = jnp.sign(_g) * jnp.maximum(jnp.abs(_g), 1.0) + (_g == 0) * 1.0
        g_xattn = _g[0]
        g_ffn = _g[1]
        return (x, ctx_2048, g_xattn, g_ffn)
    x, ctx_2048, g_xattn, g_ffn = _rec_inputs()

    def _L0_xattn_setup():
        import jax, jax.numpy as jnp
        import numpy as np
        NUM_HEADS = 16
        key = jax.random.key(seed)
        ks = jax.random.split(key, 5)
        dim = 256
        B, N, N_c = (4, 256, 64)
        x = jax.random.normal(ks[0], (B, N, dim), dtype=jnp.float32)
        context = jax.random.normal(ks[1], (B, N_c, 2 * dim), dtype=jnp.float32)
        w_qkv = jax.random.normal(ks[2], (3 * dim, dim), dtype=jnp.float32) * 0.02
        w_proj = jax.random.normal(ks[3], (dim, dim), dtype=jnp.float32) * 0.02
        b_proj = jax.random.normal(ks[4], (dim,), dtype=jnp.float32) * 0.02
        return {'x': x, 'context': context, 'w_qkv': w_qkv, 'w_proj': w_proj, 'b_proj': b_proj}
    _L0_xattn_all = _L0_xattn_setup()
    _L0_xattn_in = {k: v for k, v in _L0_xattn_all.items() if k in ('w_qkv', 'w_proj', 'b_proj')}
    del _L0_xattn_all

    def _L0_ffn_setup():
        import jax, jax.numpy as jnp
        import numpy as np
        NUM_EXPERTS = 8
        TOP_K = 2
        CAPACITY_FACTOR = 1.25
        key = jax.random.key(seed)
        k1, k2, k3, k4, k5 = jax.random.split(key, 5)
        B, S, H, I, E = (4, 512, 256, 1024, NUM_EXPERTS)
        return {'hidden_states': jax.random.normal(k1, (B, S, H), dtype=jnp.float32), 'router_gate': jax.random.normal(k2, (H, E), dtype=jnp.float32) * 0.02, 'gate_w': jax.random.normal(k3, (E, H, I), dtype=jnp.float32) * 0.02, 'up_w': jax.random.normal(k4, (E, H, I), dtype=jnp.float32) * 0.02, 'down_w': jax.random.normal(k5, (E, I, H), dtype=jnp.float32) * 0.02}
    _L0_ffn_all = _L0_ffn_setup()
    _L0_ffn_in = {k: v for k, v in _L0_ffn_all.items() if k in ('router_gate', 'gate_w', 'up_w', 'down_w')}
    del _L0_ffn_all
    return {'x': x, 'ctx_2048': ctx_2048, 'g_xattn': g_xattn, 'g_ffn': g_ffn, 'L0_xattn_w_qkv': _L0_xattn_in['w_qkv'], 'L0_xattn_w_proj': _L0_xattn_in['w_proj'], 'L0_xattn_b_proj': _L0_xattn_in['b_proj'], 'L0_ffn_router_gate': _L0_ffn_in['router_gate'], 'L0_ffn_gate_w': _L0_ffn_in['gate_w'], 'L0_ffn_up_w': _L0_ffn_in['up_w'], 'L0_ffn_down_w': _L0_ffn_in['down_w']}

def reference(x, ctx_2048, g_xattn, g_ffn, L0_xattn_w_qkv, L0_xattn_w_proj, L0_xattn_b_proj, L0_ffn_router_gate, L0_ffn_gate_w, L0_ffn_up_w, L0_ffn_down_w):
    import jax
    import jax.numpy as jnp

    def _L0_xattn_ref(x, context, w_qkv, w_proj, b_proj):
        import jax, jax.numpy as jnp
        import numpy as np
        NUM_HEADS = 16
        B, N, C = x.shape
        H = NUM_HEADS
        D = C // H
        scale = D ** (-0.5)
        qkv = (x @ w_qkv.T).reshape(B, N, 3, H, D).transpose(2, 0, 3, 1, 4)
        q, k, v = (qkv[0], qkv[1], qkv[2])
        N_c = context.shape[1]
        kv = context.reshape(B, N_c, 2, H, D).transpose(2, 0, 3, 1, 4)
        extra_k, extra_v = (kv[0], kv[1])
        k = jnp.concatenate([extra_k, k], axis=2)
        v = jnp.concatenate([extra_v, v], axis=2)
        dtype = q.dtype
        attn = jnp.einsum('bhnd,bhmd->bhnm', q * scale, k).astype(jnp.float32)
        attn = jax.nn.softmax(attn, axis=-1).astype(dtype)
        out = jnp.einsum('bhnm,bhmd->bhnd', attn, v)
        out = out.transpose(0, 2, 1, 3).reshape(B, N, C)
        return out @ w_proj.T + b_proj

    def _L0_ffn_ref(hidden_states, router_gate, gate_w, up_w, down_w):
        import jax, jax.numpy as jnp
        import numpy as np
        NUM_EXPERTS = 8
        TOP_K = 2
        CAPACITY_FACTOR = 1.25
        B, S, H = hidden_states.shape
        E = router_gate.shape[1]
        K = TOP_K
        x = hidden_states.reshape(-1, H)
        T = x.shape[0]
        cap = int(CAPACITY_FACTOR * ((T * K + E - 1) // E))
        probs = jax.nn.softmax(x @ router_gate, axis=-1)
        topw, topi = jax.lax.top_k(probs, K)
        topw = topw / (topw.sum(-1, keepdims=True) + 1e-09)
        gates = jnp.zeros((T, E), x.dtype).at[jnp.arange(T)[:, None], topi].set(topw)
        top_g, tok_idx = jax.lax.top_k(gates.T, cap)
        xe = x[tok_idx]
        h = jax.nn.silu(jnp.einsum('ech,ehi->eci', xe, gate_w)) * jnp.einsum('ech,ehi->eci', xe, up_w)
        ye = jnp.einsum('eci,eih->ech', h, down_w) * top_g[..., None]
        out = jnp.zeros_like(x).at[tok_idx.reshape(-1)].add(ye.reshape(-1, H))
        return out.reshape(B, S, H)
    x = x + jnp.tanh(g_xattn[0]) * _L0_xattn_ref(_layernorm(x, axis=-1), ctx_2048, L0_xattn_w_qkv, L0_xattn_w_proj, L0_xattn_b_proj)
    x = x + jnp.tanh(g_ffn[0]) * _L0_ffn_ref(_layernorm(x, axis=-1), L0_ffn_router_gate, L0_ffn_gate_w, L0_ffn_up_w, L0_ffn_down_w)
    return x

_drawn_inputs = setup_inputs


def setup_inputs(seed=0):
    import zlib

    import numpy as np

    out = dict(_drawn_inputs(seed))
    spreads = {}
    factors = {'L0_xattn_w_qkv': 8.0,
     'L0_xattn_b_proj': 3.784,
     'L0_ffn_router_gate': 8.693,
     'ctx_2048': 8.0,
     'L0_ffn_gate_w': 2.671}
    for name, (base, spread) in spreads.items():
        noise = np.random.default_rng([zlib.crc32(name.encode()), seed]).standard_normal(out[name].shape)
        drawn = base * np.exp(spread * noise) if base else spread * noise
        out[name] = jnp.asarray(drawn.astype(out[name].dtype))
    for name, factor in factors.items():
        out[name] = (out[name] * factor).astype(out[name].dtype)
    return out
```

```python
import concourse.bass as bass
from concourse import mybir
from contextlib import ExitStack

F32, F16, I32 = mybir.dt.float32, mybir.dt.float16, mybir.dt.int32
ALU = mybir.AluOpType
ACT = mybir.ActivationFunctionType
AX = mybir.AxisListType.X

B, N, C, NC = 32, 256, 256, 77
H, D = 16, 16
NK = NC + N
T = B * N
E, I, K = 8, 1024, 2
CAP = int(1.25 * ((T * K + E - 1) // E))
TS = 256
REGION = T + TS
NT = T * K // TS + E - 1
ROW = C + 4
WPIECE = 6 * 512
WS = 64.0
EPS = 1e-5
KT = (NC, 128, 128)


class At:
    def __init__(self, n, half, par):
        self.n, self.half, self.par = n, half, par

    def next(self):
        return At(self.n + 1, self.half + self.par, 1 - self.par)

    def prev(self):
        return At(self.n - 1, self.half - (1 - self.par), 1 - self.par)


def at(n):
    return At(n, n // 2, n % 2)


def settle(eng, waits_over):
    eng.sem_inc(waits_over, 1)


def wait(eng, sem, value):
    if isinstance(value, int) and value <= 0:
        return
    eng.wait_ge(sem, value)


def flamingo_block(nc, x, ctx_kT, ctx, g_xattn, g_ffn, wqkvT, wprojT, b_proj, router_w, gate_w, up_w, down_w, out):
    slots = nc.dram_tensor("slots", [E * REGION + TS, ROW], F32).ap()
    wsplit = nc.dram_tensor("wsplit", [E, 4, 128, WPIECE], F16).ap()

    ctx_stack = ExitStack()
    with ctx_stack:
        def sb(name, shape, dt=F32):
            return ctx_stack.enter_context(nc.sbuf_tensor(name, shape, dt))

        def sem(name):
            return ctx_stack.enter_context(nc.semaphore(name))

        bank = [ctx_stack.enter_context(nc.psum_tensor(f"pair{i}", [128, 2, 512], F32)) for i in range(2)]
        ptx_ps = ctx_stack.enter_context(nc.psum_tensor("ptx_ps", [128, 512], F32))
        ptc_ps = ctx_stack.enter_context(nc.psum_tensor("ptc_ps", [128, 512], F32))
        o_ps = ctx_stack.enter_context(nc.psum_tensor("o_ps", [128, 512], F32))
        misc = ctx_stack.enter_context(nc.psum_tensor("misc", [128, 512], F32))

        ident = sb("ident", [128, 128])
        tri = sb("tri", [128, 128], F16)
        ones16 = sb("ones16", [128, 128], F16)
        ones32 = sb("ones32", [128, 128])
        same_expert = sb("same_expert", [128, 128])
        iscr = sb("iscr", [128, 512], I32)
        low_rows = sb("low_rows", [128, 1])
        iota8 = sb("iota8", [128, 8])
        region_at = sb("region_at", [128, 8])
        before = sb("before", [128, 8, 8])
        slot_num = sb("slot_num", [128, 2])
        tok_of = sb("tok_of", [128, 2])
        tokTi = sb("tokTi", [128, 512], I32)
        mhalf = sb("mhalf", [128, 2])
        wraw = sb("wraw", [128, 2, 768])
        praw = sb("praw", [128, 2, 256])
        braw = sb("braw", [1, 256])
        rout = sb("rout", [128, 2, 8])
        wq = sb("wq", [128, 2, 2, 512], F16)
        wk = sb("wk", [128, 2, 2, 512], F16)
        wv = sb("wv", [128, 2, 2, 256], F16)
        wp = sb("wp", [128, 2, 2, 256], F16)
        bp = sb("bp", [1, 2, 256], F16)
        tgx = sb("tgx", [128, 1])
        tgf = sb("tgf", [128, 1])

        xb = sb("xb", [128, 2, 2, 256])
        xr = sb("xr", [128, 2, 2, 256])
        ckraw = sb("ckraw", [128, 2, 4, NC])
        cvraw = sb("cvraw", [NC, 2, 256])
        stats = sb("stats", [128, 2, 6])
        mv1 = sb("mv1", [128, 2, 2])
        mv2 = sb("mv2", [128, 2, 2])
        ve1 = sb("ve1", [128, 2])
        ve2 = sb("ve2", [128, 2])
        rs1 = sb("rs1", [128, 2])
        rs2 = sb("rs2", [128, 2])
        xn = sb("xn", [128, 2, 256])
        xTh = sb("xTh", [128, 2, 256], F16)
        xTl = sb("xTl", [128, 2, 256], F16)
        qhi = sb("qhi", [128, 512], F16)
        qst = sb("qst", [128, 2, 4, 256], F16)
        kh = sb("kh", [128, 2, 4, NK], F16)
        kl = sb("kl", [128, 2, 4, NK], F16)
        v = sb("v", [128, 2, 3, H, D + 1])
        negmax = sb("negmax", [128, 2, 2])
        p = sb("p", [128, 2, 2, NK])
        ptx = sb("ptx", [128, 2, 2, 2, 128])
        ptc = sb("ptc", [NC, 2, 2, 128])
        rden = sb("rden", [128, 16])
        o = sb("o", [128, 2, 256])
        oTh = sb("oTh", [128, 2, 256], F16)
        oTl = sb("oTl", [128, 2, 256], F16)
        row = sb("row", [128, 2, 2, ROW])
        xn2T = sb("xn2T", [128, 2, 256])
        lmax = sb("lmax", [128, 2])
        lg = sb("lg", [128, 2, 8])
        ex = sb("ex", [128, 2, 8])
        esum = sb("esum", [128, 2])
        pr = sb("pr", [128, 2, 8])
        gt = sb("gt", [128, 2, 8, 8])
        eq = sb("eq", [128, 2, 8, 8])
        rank = sb("rank", [128, 2, 8])
        oh = sb("oh", [128, 2, 2, 8])
        ohp = sb("ohp", [128, 2, 2, 8])
        pg = sb("pg", [128, 2, 2])
        den = sb("den", [128, 2])
        gsel = sb("gsel", [128, 2, 2])
        sel = sb("sel", [128, 2, 8], F16)
        seen = sb("seen", [128, 8], F16)
        pos = sb("pos", [128, 2, 8])
        idxf = sb("idxf", [128, 2, 2])
        idx = sb("idx", [128, 2, 2, 2], I32)
        gall = sb("gall", [128, 2 * B, 8])
        wst = sb("wst", [128, 2, 3, 512])
        wout = sb("wout", [128, 2, 6, 512], F16)

        cnt = sb("cnt", [128, 8])
        nti = sb("nti", [128, 8], I32)
        ntf = sb("ntf", [128, 8])
        tend = sb("tend", [128, 8])
        tnum = sb("tnum", [128, NT + 1])
        tcmp = sb("tcmp", [128, NT + 1, 8])
        tcmp2 = sb("tcmp2", [128, NT + 1, 8])
        texp = sb("texp", [128, NT + 1])
        tbase = sb("tbase", [128, NT + 1])
        tscr = sb("tscr", [128, NT + 1])
        tabs = sb("tabs", [128, 3, NT + 1], I32)
        thr_t = sb("thr_t", [128, NT + 1])
        cut_t = sb("cut_t", [128, NT + 1])
        padf = sb("padf", [128, 2, 8])
        padi = sb("padi", [128, 2, 8], I32)
        padrow = sb("padrow", [128, 2, ROW])
        gT = sb("gT", [128, 512])
        tokT = sb("tokT", [128, 512])
        gcmp = sb("gcmp", [128, 512])
        thr = sb("thr", [128, 1], I32)
        cand = sb("cand", [128, 1], I32)
        bit = sb("bit", [128, 1], I32)
        bitf = sb("bitf", [128, 1])
        keep_i = sb("keep_i", [128, 1], I32)
        count = sb("count", [128, 1])
        need = sb("need", [128, 1])
        cut = sb("cut", [128, 1])
        candf = sb("candf", [128, 1])
        stepf = sb("stepf", [128, 1])
        diag = sb("diag", [8, 2, 8])
        lim = sb("lim", [128, 2, 8])

        wb = sb("wb", [128, 2, 4, WPIECE], F16)
        xe = sb("xe", [128, 2, 2, ROW])
        eTh = sb("eTh", [128, 2, 2, TS], F16)
        eTl = sb("eTl", [128, 2, 2, TS], F16)
        sg = sb("sg", [128, 2, TS])
        h32 = sb("h32", [128, 2, TS])
        hh = sb("hh", [128, 4, TS], F16)
        hl = sb("hl", [128, 4, TS], F16)
        gf = sb("gf", [128, 2, 2])
        ga = sb("ga", [128, 2])
        gb = sb("gb", [128, 2])
        gg = sb("gg", [128, 2])
        gk = sb("gk", [128, 2])
        toki = sb("toki", [128, 2, 2], I32)
        y = sb("y", [128, 2, 2, 256])

        s_const = sem("const_loaded")
        s_made = sem("const_made")
        s_pmade = sem("pool_const_made")
        s_tanh = sem("tanh_done")
        pool_waits_over, dve_waits_over = sem("pool_waits_over"), sem("dve_waits_over")
        s_padrow = sem("pad_rows_made")
        s_kh = sem("ctx_key_high")
        s_dve = sem("dve_order")
        s_pool = sem("pool_order")
        s_x = [sem("x_loaded0"), sem("x_loaded1")]
        s_ck = [sem("ctxk_loaded0"), sem("ctxk_loaded1")]
        s_cv = [sem("ctxv_loaded0"), sem("ctxv_loaded1")]
        s_w = [sem("w_loaded0"), sem("w_loaded1")]
        s_xr = [sem("residual_loaded0"), sem("residual_loaded1")]
        s_xst = [sem("x1_stored0"), sem("x1_stored1")]
        s_wst = [sem("w_stored0"), sem("w_stored1")]
        s_scat = [sem("rows_scattered0"), sem("rows_scattered1")]
        ve1_ready, rs1_ready, ve2_ready, rs2_ready = sem("ve1_ready"), sem("rs1_ready"), sem("ve2_ready"), sem("rs2_ready")
        xn_ready, x1_ready, row_ready = sem("xn_ready"), sem("x1_ready"), sem("row_ready")
        ctx_split, w_split = sem("ctx_split"), sem("w_split")
        filled, emptied = sem("misc_filled"), sem("misc_emptied")
        pre_hi, ot_hi = sem("pre_high"), sem("ot_high")
        scored, maxed, expd = sem("scored"), sem("maxed"), sem("exp_done")
        turned, ptx_out, ptc_out = sem("probs_turned"), sem("ptx_out"), sem("ptc_out")
        pv_done, o_out = sem("pv_done"), sem("o_out")
        xn2t_ready, lg_ready, ex_ready, sel_ready, idx_ready = (
            sem("xn2t_ready"), sem("logits_ready"), sem("router_exp"), sem("sel_ready"), sem("idx_ready"))
        s_cnt, s_gt, s_gtc, s_count, s_cnt_in, s_lim, s_limin = (
            sem("counts_done"), sem("gates_turned"), sem("gates_copied"), sem("count_summed"), sem("count_in"),
            sem("limits_done"), sem("limits_in"))
        s_tabs, s_padi, s_pads = sem("tables_ready"), sem("pads_ready"), sem("pads_stored")
        s_dummy = sem("dummy_rows_stored")
        s_limits_ok = sem("limits_ready")
        s_wl = [sem("expert_w0"), sem("expert_w1")]
        s_xe = [sem("slots_loaded0"), sem("slots_loaded1")]
        gu_filled, silu_done, mult_done, hhi_done, hlo_done = (
            sem("gu_filled"), sem("silu_done"), sem("mult_done"), sem("hhi_done"), sem("hlo_done"))
        et_filled, et_hi, et_lo = sem("et_filled"), sem("et_high"), sem("et_low")
        y_filled, y_out, gf_ready, s_add = sem("y_filled"), sem("y_out"), sem("gf_ready"), sem("rows_added")

        def pre_use(b, k):
            return k if isinstance(b.n, int) and b.n == 0 else 11 * b.n - 5 + k

        def post_use(b, k):
            last = 6 if isinstance(b.n, int) and b.n == B - 1 else 0
            return 12 + 11 * b.n - last + k

        class Chain:
            def __init__(self, eng, s, after=None):
                self.eng, self.s, self.base, self.n, self.after = eng, s, 0, 0, after

            def __call__(self, ins):
                self.n += 1
                ins.then_inc(self.s, 1)
                self.eng.wait_ge(self.s, self.base + self.n)
                if self.after:
                    settle(self.eng, self.after)

            def rest(self):
                self.base, self.n = self.base + self.n, 0

        def batches(eng, body, chain=None):
            def part(*a):
                if chain:
                    chain.rest()
                body(*a)
            part(at(-1), False, False, True)
            part(at(0), True, False, True)
            part(at(1), True, True, True)
            part(at(2), True, True, True)
            if chain:
                chain.rest()
                start = chain.base
            with eng.Fori(1, (B - 2) // 2) as i:
                for j in (1, 2):
                    if chain:
                        chain.n = 0
                        chain.base = start + (i - 1) * (2 * chain.per) + (j - 1) * chain.per
                    body(At(2 * i + j, i + j // 2, j % 2), True, True, True)
                    if chain:
                        assert chain.n == chain.per, (chain.n, chain.per)
            if chain:
                chain.base, chain.n = start + (B - 4) * chain.per, 0
            part(at(B - 1), True, True, False)
            part(at(B), False, True, False)

        def tiles(eng, body, chain=None):
            def part(*a):
                if chain:
                    chain.rest()
                body(*a)
            part(at(-1))
            part(at(0))
            part(at(1))
            part(at(2))
            if chain:
                chain.rest()
                start = chain.base
            with eng.Fori(1, (NT - 1) // 2) as i:
                for j in (1, 2):
                    if chain:
                        chain.n = 0
                        chain.base = start + (i - 1) * (2 * chain.per) + (j - 1) * chain.per
                    body(At(2 * i + j, i + j // 2, j % 2))
                    if chain:
                        assert chain.n == chain.per, (chain.n, chain.per)
            if chain:
                chain.base, chain.n = start + (NT - 3) * chain.per, 0
            part(at(NT))

        block = ctx_stack.enter_context(nc.Block())

        @block.sync
        def _(sp):
            def load_batch(b):
                par = b.par
                wait(sp, xn_ready, b.n - 1)
                sp.dma_start(xb[:, par], x[bass.ds(b.n, 1)].rearrange("a (t p) c -> p (a t) c", p=128)).then_inc(s_x[par], 16)
                wait(sp, ctx_split, b.n - 1)
                sp.dma_start(ckraw[:, par], ctx_kT[bass.ds(b.n, 1)].rearrange("a p c k -> p (a c) k")).then_inc(s_ck[par], 16)
                sp.dma_start(cvraw[:, par], ctx[bass.ds(b.n, 1), :, C:].rearrange("a k c -> k (a c)")).then_inc(s_cv[par], 16)

            def load_weights(b, e, q):
                wait(sp, w_split, b.n - 1)
                for k, w in enumerate((gate_w, up_w)):
                    sp.dma_start(wst[:, b.par, k].rearrange("p (k c) -> p k c", k=2),
                                 w[bass.ds(e, 1), :, bass.ds(q * 256, 256)].rearrange("a (k p) c -> p (a k) c", p=128)
                                 ).then_inc(s_w[b.par], 16)
                sp.dma_start(wst[:, b.par, 2].rearrange("p (k c) -> p k c", k=2),
                             down_w[bass.ds(e, 1), bass.ds(q * 256, 256), :].rearrange("a (k p) c -> p (a k) c", p=128)
                             ).then_inc(s_w[b.par], 16)

            def load_residual(b):
                wait(sp, s_xst[b.par], 16 * b.half)
                wait(sp, row_ready, b.n - 1)
                sp.dma_start(xr[:, b.par], x[bass.ds(b.n, 1)].rearrange("a (t p) c -> p (a t) c", p=128)).then_inc(s_xr[b.par], 16)

            def store_x1(b):
                sp.wait_ge(x1_ready, b.n + 1)
                sp.dma_start(out[bass.ds(b.n * N, N)].rearrange("(t p) c -> p t c", p=128), xr[:, b.par]).then_inc(s_xst[b.par], 16)

            load_batch(at(0))
            sp.dma_start(wraw[:], wqkvT.rearrange("(k p) n -> p k n", p=128)).then_inc(s_const, 16)
            sp.dma_start(praw[:], wprojT.rearrange("(k p) n -> p k n", p=128)).then_inc(s_const, 16)
            sp.dma_start(braw[:], b_proj.rearrange("(a n) -> a n", a=1)).then_inc(s_const, 16)
            sp.dma_start(rout[:], router_w.rearrange("(k p) n -> p k n", p=128)).then_inc(s_const, 16)
            sp.dma_start(tgx[:], g_xattn.rearrange("(a n) -> a n", a=1).to_broadcast([128, 1])).then_inc(s_const, 16)
            sp.dma_start(tgf[:], g_ffn.rearrange("(a n) -> a n", a=1).to_broadcast([128, 1])).then_inc(s_const, 16)
            load_batch(at(1))
            for b in (0, 1):
                load_weights(at(b), 0, b)
                load_residual(at(b))

            with sp.Fori(0, (B - 2) // 2) as i:
                for j in (0, 1):
                    b = At(2 * i + j, i, j)
                    nxt = At(2 * i + j + 2, i + 1, j)
                    load_batch(nxt)
                    load_weights(nxt, (i + 1) // 2, ((i + 1) % 2) * 2 + j)
                    store_x1(b)
                    load_residual(nxt)
            store_x1(at(B - 2))
            store_x1(at(B - 1))

            sp.wait_ge(s_padrow, 1)
            sp.dma_start(out[T:T + TS].rearrange("(s p) c -> p s c", p=128), padrow[:, :, 0:C]).then_inc(s_dummy, 16)
            sp.dma_start(slots[E * REGION:].rearrange("(s p) c -> p s c", p=128), padrow[:]).then_inc(s_dummy, 16)
            sp.wait_ge(s_dummy, 32)
            for par in (0, 1):
                sp.wait_ge(s_scat[par], 64 * B // 2)
                sp.wait_ge(s_wst[par], 16 * B // 2)
                sp.wait_ge(s_xst[par], 16 * B // 2)
            sp.wait_ge(s_tabs, 1)
            sp.wait_ge(s_pads, 16 * 2 * E)

            def load_tile(t):
                e = nc.values_load(tabs[0:1, 0, bass.ds(t.n, 1)], engines=(mybir.EngineType.SP,), min_val=0, max_val=E - 1,
                                   skip_runtime_bounds_check_because="the table is clipped")
                r0 = nc.values_load(tabs[0:1, 1, bass.ds(t.n, 1)], engines=(mybir.EngineType.SP,), min_val=0, max_val=E * REGION,
                                    skip_runtime_bounds_check_because="the table is clipped")
                new = nc.values_load(tabs[0:1, 2, bass.ds(t.n, 1)], engines=(mybir.EngineType.SP,), min_val=0, max_val=1,
                                     skip_runtime_bounds_check_because="it is a comparison's result")
                wait(sp, gf_ready, t.n - 1)
                sp.dma_start(xe[:, t.par], slots[bass.ds(r0, TS)].rearrange("(s p) c -> p s c", p=128)).then_inc(s_xe[t.par], 16)
                wait(sp, y_filled, t.n - 1)
                sp.dma_start(wb[:, t.par], wsplit[bass.ds(e, 1)].rearrange("a q p c -> p (a q) c"),
                             cond=new).then_inc(s_wl[t.par], 16)

            for n in range(3):
                load_tile(at(n))
            with sp.Fori(1, (NT - 1) // 2) as i:
                for j in (1, 2):
                    load_tile(At(2 * i + j, i + j // 2, j % 2))
            load_tile(at(NT))
            sp.wait_ge(s_wl[1], 16 * ((NT + 1) // 2))
            sp.wait_ge(s_wl[0], 16 * ((NT + 1) // 2))
            sp.wait_ge(s_add, 32 * NT)

        @block.gpsimd
        def _(pool):
            chain = Chain(pool, s_pool)
            pool.memset(ident[:], 0.0).then_inc(s_pmade, 1)
            chain(pool.memset(tri[:], 1.0))
            pool.wait_ge(s_pmade, 1)
            chain(pool.affine_select(out=ident[:], in_=ident[:], compare_op=ALU.not_equal, fill=1.0, base=0,
                                     pattern=[[-1, 128]], channel_multiplier=1))
            chain(pool.affine_select(out=tri[:], in_=tri[:], compare_op=ALU.is_gt, fill=0.0, base=0,
                                     pattern=[[1, 128]], channel_multiplier=-1))
            chain(pool.memset(ones16[:], 1.0))
            chain(pool.memset(ones32[:], 1.0))
            chain(pool.memset(mhalf[:], -0.5))
            chain(pool.memset(seen[:], 0.0))
            for par in (0, 1):
                chain(pool.memset(v[:, par, :, :, D:D + 1], 1.0))
            chain(pool.memset(before[:], 1.0))
            chain(pool.affine_select(out=before[:], in_=before[:], compare_op=ALU.is_gt, fill=0.0, base=0,
                                     pattern=[[1, 8], [-1, 8]], channel_multiplier=0))
            chain(pool.iota(iscr[:, 0:1], [[0, 1]], base=0, channel_multiplier=1))
            chain(pool.iota(iscr[:, 1:9], [[1, 8]], base=0, channel_multiplier=0))
            chain(pool.iota(iscr[:, 16:16 + NT + 1], [[1, NT + 1]], base=0, channel_multiplier=0))
            chain(pool.iota(iscr[:, 128:256], [[-1, 128]], base=128, channel_multiplier=1))
            chain(pool.iota(tokTi[:], [[16 * 128, 4], [1, 128]], base=0, channel_multiplier=0))
            pool.memset(padrow[:], 0.0).then_inc(s_pmade, 1)

            def piece_weights(b):
                par = b.par
                pool.wait_ge(s_w[par], 48 * (b.half + 1))
                wait(pool, s_wst[par], 16 * b.half)
                settle(pool, pool_waits_over)
                chain(pool.tensor_scalar(wst[:, par], wst[:, par], WS, None, ALU.mult))
                chain(pool.tensor_copy(wout[:, par, 0:3], wst[:, par]))
                pool.tensor_tensor(wout[:, par, 3:6], wst[:, par], wout[:, par, 0:3], ALU.subtract).then_inc(w_split, 1)
                pool.wait_ge(w_split, b.n + 1)
                settle(pool, pool_waits_over)

            def store_weights(b, e, q):
                pool.dma_start(wsplit[bass.ds(e, 1), bass.ds(q, 1)].rearrange("a q p c -> p (a q c)"),
                               wout[:, b.par].rearrange("p s c -> p (s c)")).then_inc(s_wst[b.par], 16)

            def body(b, heads, post, pre):
                nb, lb = b.next(), b.prev()
                if pre:
                    pool.wait_ge(ve1_ready, nb.n + 1)
                    pool.tensor_tensor(rs1[:], ve1[:], mhalf[:], ALU.pow).then_inc(rs1_ready, 1)
                    wait(pool, pv_done, 16 * (nb.n - 1))
                    pool.wait_ge(s_ck[nb.par], 16 * (nb.half + 1))
                    pool.wait_ge(s_cv[nb.par], 16 * (nb.half + 1))
                    settle(pool, pool_waits_over)
                    pool.tensor_copy(v[0:NC, nb.par, 0, :, 0:D], cvraw[:, nb.par].rearrange("p (h d) -> p h d", h=H))
                    pool.tensor_copy(kh[:, nb.par, :, 0:NC], ckraw[:, nb.par]).then_inc(s_kh, 1)
                    pool.wait_ge(s_kh, nb.n + 1)
                    pool.tensor_tensor(kl[:, nb.par, :, 0:NC], ckraw[:, nb.par], kh[:, nb.par, :, 0:NC],
                                       ALU.subtract).then_inc(ctx_split, 1)
                if post:
                    pool.wait_ge(ve2_ready, lb.n + 1)
                    pool.tensor_tensor(rs2[:], ve2[:], mhalf[:], ALU.pow).then_inc(rs2_ready, 1)
                if heads:
                    piece_weights(b)
                    if isinstance(b.n, int):
                        store_weights(b, b.n // 4, b.n % 4)
                    else:
                        store_weights(b, b.half // 2, (b.half % 2) * 2 + b.par)
                if post:
                    pool.wait_ge(idx_ready, lb.n + 1)
                    settle(pool, pool_waits_over)
                    for c in (0, 1):
                        for t in (0, 1):
                            pool.indirect_dma_start(out=slots[:], out_offset=bass.IndirectOffsetOnAxis(ap=idx[:, lb.par, c, t:t + 1], axis=0),
                                                    in_=row[:, lb.par, t], in_offset=None).then_inc(s_scat[lb.par], 16)

            chain.per, chain.after = 2, pool_waits_over
            batches(pool, body, chain)

            pool.wait_ge(s_padi, 2)
            for e in range(E):
                for s in (0, 1):
                    pool.indirect_dma_start(out=slots[:], out_offset=bass.IndirectOffsetOnAxis(ap=padi[:, s, e:e + 1], axis=0),
                                            in_=padrow[:, s], in_offset=None).then_inc(s_pads, 16)
            pool.wait_ge(s_dummy, 32)
            for par in (0, 1):
                pool.wait_ge(s_xst[par], 16 * B // 2)

            def add_tile(t):
                pool.wait_ge(y_out, t.n + 1)
                wait(pool, s_add, 32 * t.n)
                settle(pool, pool_waits_over)
                for s in (0, 1):
                    pool.indirect_dma_start(out=out[:], out_offset=bass.IndirectOffsetOnAxis(ap=toki[:, t.par, s:s + 1], axis=0),
                                            in_=y[:, t.par, s], in_offset=None, compute_op=ALU.add).then_inc(s_add, 16)

            for n in range(3):
                add_tile(at(n))
            with pool.Fori(1, (NT - 1) // 2) as i:
                for j in (1, 2):
                    add_tile(At(2 * i + j, i + j // 2, j % 2))

        @block.scalar
        def _(act):
            act.wait_ge(s_const, 96)
            act.activation(tgx[:], tgx[:], ACT.Tanh).then_inc(s_tanh, 1)
            act.activation(tgf[:], tgf[:], ACT.Tanh).then_inc(s_tanh, 1)

            def ctx_out(b, h):
                g = b.n * H + h
                act.wait_ge(turned, g + 1)
                wait(act, pv_done, g - 1)
                act.copy(ptc[:, h % 2], ptc_ps[0:NC, 0:256].rearrange("p (t q) -> p t q", t=2)).then_inc(ptc_out, 1)

            def body(b, heads, post, pre):
                nb, lb = b.next(), b.prev()
                for h in range(H):
                    if h == 0 and post:
                        ctx_out(lb, H - 1)
                    if heads:
                        if h:
                            ctx_out(b, h - 1)
                        g = b.n * H + h
                        act.wait_ge(maxed, g + 1)
                        wait(act, turned, g - 1)
                        for t in (0, 1):
                            last = act.activation(p[:, h % 2, t], bank[h % 2][:, t, 0:NK], ACT.Exp,
                                                  bias=negmax[:, h % 2, t:t + 1])
                        last.then_inc(expd, 1)
                    if post and h == 2:
                        act.wait_ge(filled, post_use(lb, 0) + 1)
                        act.copy(oTh[:].rearrange("p k t -> p (k t)"), misc[:]).then_inc(ot_hi, 1)
                    if post and h == 5:
                        act.wait_ge(filled, post_use(lb, 2) + 1)
                        act.copy(xn2T[:].rearrange("p k t -> p (k t)"), misc[:]).then_inc(emptied, 1)
                    if post and h == 6:
                        act.wait_ge(lg_ready, lb.n + 1)
                        act.activation(ex[:], lg[:], ACT.Exp).then_inc(ex_ready, 1)
                    if pre and h == 9:
                        act.wait_ge(filled, pre_use(nb, 0) + 1)
                        act.copy(xTh[:].rearrange("p k t -> p (k t)"), misc[:]).then_inc(pre_hi, 1)
                    if pre and h in (10, 11):
                        act.wait_ge(filled, pre_use(nb, h - 9) + 1)
                        act.copy(qhi[:], misc[:]).then_inc(pre_hi, 1)
                    if pre and h in (12, 13):
                        act.wait_ge(filled, pre_use(nb, h - 9) + 1)
                        c = 2 * (h - 12)
                        act.copy(kh[:, nb.par, c:c + 2, NC:NK], misc[:].rearrange("p (c t) -> p c t", c=2)).then_inc(pre_hi, 1)
                    if pre and h == 14:
                        act.wait_ge(filled, pre_use(nb, 5) + 1)
                        act.copy(v[:, nb.par, 1:3, :, 0:D], misc[:].rearrange("p (t h d) -> p t h d", t=2, h=H)).then_inc(emptied, 1)

            batches(act, body)

            def turned_high(t):
                act.wait_ge(et_filled, t.n + 1)
                act.copy(eTh[:, t.par].rearrange("p k t -> p (k t)"), misc[:]).then_inc(et_hi, 1)

            def high(t, c):
                u = t.n * 8 + c
                act.wait_ge(mult_done, u + 1)
                act.copy(hh[:, c % 4], h32[:, c % 2]).then_inc(hhi_done, 1)

            def tile(t):
                first = isinstance(t.n, int) and t.n < 0
                last = isinstance(t.n, int) and t.n == NT
                if first:
                    return turned_high(t.next())
                for c in range(8):
                    if not last:
                        u = t.n * 8 + c
                        act.wait_ge(gu_filled, u + 1)
                        wait(act, mult_done, u - 1)
                        act.activation(sg[:, c % 2], bank[c % 4 // 2][:, c % 2, 0:TS], ACT.Silu, scale=1.0 / WS).then_inc(silu_done, 1)
                    if c == 0 and not (isinstance(t.n, int) and t.n == 0):
                        high(t.prev(), 7)
                    if c and not last:
                        high(t, c - 1)
                    if c == 4 and not last:
                        turned_high(t.next())

            tiles(act, tile)

        @block.tensor
        def _(pe):
            def mm(out_, l, r, start, stop, **kw):
                return pe.matmul(out_, l, r, start=start, stop=stop, **kw)

            def three(dst, lh, ll, rh, rl):
                for n, (l, r) in enumerate(((lh, rh), (ll, rh), (lh, rl))):
                    for k in (0, 1):
                        last = mm(dst, l(k), r(k), n == 0 and k == 0, n == 2 and k == 1)
                return last

            def turn(src, width=128):
                for k in (0, 1):
                    for t in (0, 1):
                        last = pe.transpose(misc[:, k * 256 + t * 128:k * 256 + t * 128 + 128],
                                            src(t, k), ident[:])
                return last

            def scores(b, h):
                g = b.n * H + h
                wait(pe, expd, g - 1)
                j, c = h % 4, h // 4
                rows = slice(32 * j, 32 * j + 32)
                for t in (0, 1):
                    dst = bank[h % 2][:, t, 0:NK]
                    q = qst[rows, b.par, c, t * 128:t * 128 + 128]
                    mm(dst, q, kh[rows, b.par, c, :], True, False)
                    last = mm(dst, q, kl[rows, b.par, c, :], False, True)
                last.then_inc(scored, 1)

            def turn_probs(b, h):
                g = b.n * H + h
                pe.wait_ge(expd, g + 1)
                wait(pe, ptx_out, g)
                wait(pe, ptc_out, g)
                for t in (0, 1):
                    pe.transpose(ptc_ps[0:NC, t * 128:t * 128 + 128], p[:, h % 2, t, 0:NC], ident[:])
                    for k in (0, 1):
                        last = pe.transpose(ptx_ps[:, (k * 2 + t) * 128:(k * 2 + t) * 128 + 128],
                                            p[:, h % 2, t, NC + k * 128:NC + k * 128 + 128], ident[:])
                last.then_inc(turned, 1)

            def values(b, h):
                g = b.n * H + h
                pe.wait_ge(ptx_out, g + 1)
                pe.wait_ge(ptc_out, g + 1)
                if h % 8 == 0:
                    wait(pe, o_out, 2 * b.n + h // 8)
                for t in (0, 1):
                    dst = o_ps[:, ((h % 8) * 2 + t) * 17:((h % 8) * 2 + t) * 17 + 17]
                    mm(dst, ptc[:, h % 2, t], v[0:NC, b.par, 0, h], True, False)
                    mm(dst, ptx[:, h % 2, 0, t], v[:, b.par, 1, h], False, False)
                    last = mm(dst, ptx[:, h % 2, 1, t], v[:, b.par, 2, h], False, True)
                last.then_inc(pv_done, 1)

            def pre_step(b, k):
                wait(pe, emptied, pre_use(b, k))
                if k == 0:
                    pe.wait_ge(xn_ready, b.n + 1)
                    last = turn(lambda t, c: xn[:, t, c * 128:c * 128 + 128])
                elif k < 5:
                    w = wq if k < 3 else wk
                    for c in (0, 1):
                        chunk = ((k - 1) % 2) * 2 + c
                        last = three(misc[:, c * 256:c * 256 + 256],
                                     lambda kk: w[:, 0, kk, chunk * 128:chunk * 128 + 128],
                                     lambda kk: w[:, 1, kk, chunk * 128:chunk * 128 + 128],
                                     lambda kk: xTh[:, kk, :], lambda kk: xTl[:, kk, :])
                else:
                    for t in (0, 1):
                        last = three(misc[:, t * 256:t * 256 + 256],
                                     lambda kk: xTh[:, kk, t * 128:t * 128 + 128],
                                     lambda kk: xTl[:, kk, t * 128:t * 128 + 128],
                                     lambda kk: wv[:, 0, kk, :], lambda kk: wv[:, 1, kk, :])
                last.then_inc(filled, 1)

            def post_step(b, k):
                wait(pe, emptied, post_use(b, k))
                if k == 0:
                    pe.wait_ge(o_out, 2 * b.n + 2)
                    last = turn(lambda t, c: o[:, t, c * 128:c * 128 + 128])
                elif k == 1:
                    for t in (0, 1):
                        dst = misc[:, t * 256:t * 256 + 256]
                        for n, (l, s) in enumerate(((oTh, 0), (oTl, 0), (oTh, 1))):
                            for c in (0, 1):
                                mm(dst, l[:, c, t * 128:t * 128 + 128], wp[:, s, c, :], n == 0 and c == 0, False)
                        mm(dst, ones16[0:1, :], bp[:, 0, :], False, False)
                        last = mm(dst, ones16[0:1, :], bp[:, 1, :], False, True)
                elif k == 2:
                    pe.wait_ge(row_ready, b.n + 1)
                    last = turn(lambda t, c: row[:, b.par, t, c * 128:c * 128 + 128])
                elif k == 3:
                    for t in (0, 1):
                        for c in (0, 1):
                            last = mm(misc[:, t * 8:t * 8 + 8], xn2T[:, c, t * 128:t * 128 + 128], rout[:, c, :], c == 0, c == 1)
                else:
                    pe.wait_ge(sel_ready, b.n + 1)
                    mm(misc[:, 0:8], tri[:], sel[:, 0], True, False)
                    mm(misc[:, 0:8], ones16[:], seen[:], False, True)
                    mm(misc[:, 8:16], tri[:], sel[:, 1], True, False)
                    mm(misc[:, 8:16], ones16[:], seen[:], False, False)
                    last = mm(misc[:, 8:16], ones16[:], sel[:, 0], False, True)
                last.then_inc(filled, 1)

            pe.wait_ge(s_made, 1)
            pe.wait_ge(s_pmade, 2)

            def body(b, heads, post, pre):
                nb, lb = b.next(), b.prev()
                for h in range(H):
                    if heads and h + 1 < H:
                        scores(b, h + 1)
                    if pre and h + 1 == H:
                        pe.wait_ge(emptied, pre_use(nb, 5))
                        pe.wait_ge(ctx_split, nb.n + 1)
                        scores(nb, 0)
                    if pre and 9 <= h <= 14:
                        pre_step(nb, h - 9)
                    if post and h in (2, 3, 5, 6, 8):
                        post_step(lb, {2: 0, 3: 1, 5: 2, 6: 3, 8: 4}[h])
                    if heads and h:
                        values(b, h - 1)
                    if post and h == 0:
                        values(lb, H - 1)
                    if heads:
                        if h == 0:
                            pe.wait_ge(emptied, pre_use(b, 6))
                        turn_probs(b, h)

            batches(pe, body)

            pe.wait_ge(s_cnt_in, 1)
            mm(misc[:, 0:8], ones16[:], seen[:], True, True).then_inc(s_cnt, 1)
            pe.wait_ge(idx_ready, B)
            for i in range(4):
                last = pe.transpose(o_ps[:, i * 128:i * 128 + 128], gall[:, i * 16:i * 16 + 16, :].rearrange("p t e -> p (t e)"), ident[:])
            last.then_inc(s_gt, 1)

            def summed(n):
                pe.wait_ge(s_cnt_in, n + 2)
                mm(ptx_ps[:, 0:1], same_expert[:], count[:], True, True).then_inc(s_count, 1)
            with pe.Fori(0, 30) as i:
                summed(i)
            summed(30)
            with pe.Fori(0, 14) as i:
                summed(i + 31)
            pe.wait_ge(s_limin, 1)
            mm(ptx_ps[:, 8:24], ones32[0:8, :], diag[:].rearrange("p a e -> p (a e)"), True, True).then_inc(s_lim, 1)

            def turn_tile(t):
                pe.wait_ge(s_xe[t.par], 16 * (t.half + 1))
                wait(pe, et_lo, t.n)
                turn(lambda s, c: xe[:, t.par, s, c * 128:c * 128 + 128]).then_inc(et_filled, 1)

            def weights(t, part, low, c, k=0):
                off = (low * 3 + part) * 512
                if part < 2:
                    off += k * 256 + (c % 2) * 128
                    return wb[:, t.par, c // 2, off:off + 128]
                off += (c % 2) * 256
                return wb[:, t.par, c // 2, off:off + 256]

            def gate_up(t, c):
                u = t.n * 8 + c
                wait(pe, mult_done, u - 3)
                for part in (0, 1):
                    last = three(bank[c % 4 // 2][:, c % 2, part * TS:part * TS + TS],
                                 lambda k: weights(t, part, 0, c, k), lambda k: weights(t, part, 1, c, k),
                                 lambda k: eTh[:, t.par, k, :], lambda k: eTl[:, t.par, k, :])
                last.then_inc(gu_filled, 1)

            y_ps = (ptc_ps, o_ps)

            def down(t, c):
                u = t.n * 8 + c
                pe.wait_ge(hhi_done, u + 1)
                pe.wait_ge(hlo_done, u + 1)
                if c == 0:
                    wait(pe, y_out, t.n - 1)
                for s in (0, 1):
                    rows = slice(s * 128, s * 128 + 128)
                    dst = y_ps[t.par][:, s * 256:s * 256 + 256]
                    mm(dst, hh[:, c % 4, rows], weights(t, 2, 0, c), c == 0 and s == 0, False, skip_group_check=True)
                    mm(dst, hl[:, c % 4, rows], weights(t, 2, 0, c), False, False, skip_group_check=True)
                    last = mm(dst, hh[:, c % 4, rows], weights(t, 2, 1, c), False, c == 7, skip_group_check=True)
                if c == 7:
                    last.then_inc(y_filled, 1)

            def tile(t):
                first = isinstance(t.n, int) and t.n < 0
                last = isinstance(t.n, int) and t.n == NT
                zero = isinstance(t.n, int) and t.n == 0
                if first:
                    pe.wait_ge(s_limits_ok, 1)
                    return turn_tile(t.next())
                for c in range(8):
                    if not last:
                        if c == 0:
                            pe.wait_ge(et_lo, t.n + 1)
                            pe.wait_ge(s_wl[t.par], 16 * (t.half + 1))
                        gate_up(t, c)
                    if c < 2 and not zero:
                        down(t.prev(), c + 6)
                    if c >= 2 and not last:
                        down(t, c - 2)
                    if c == 4 and not last:
                        turn_tile(t.next())

            tiles(pe, tile)

        @block.vector
        def _(dve):
            link = Chain(dve, s_dve)
            bc = lambda a, n, shape: a.unsqueeze(n).to_broadcast(shape)
            dve.wait_ge(s_pmade, 2)
            for s in (0, 1):
                link(dve.tensor_scalar(slot_num[:, s:s + 1], iscr[:, 0:1], float(128 * s), None, ALU.add))
            link(dve.tensor_copy(tok_of[:], slot_num[:]))
            link(dve.tensor_scalar(iscr[:, 11:12], iscr[:, 0:1], 3, None, ALU.logical_shift_right))
            link(dve.tensor_copy(candf[:], iscr[:, 11:12]))
            link(dve.tensor_scalar(candf[:], candf[:], 128.0, None, ALU.mult))
            link(dve.tensor_copy(tokT[:], tokTi[:]))
            link(dve.tensor_scalar(tokT[:], tokT[:], candf[:, 0:1], None, ALU.add))
            link(dve.tensor_copy(iota8[:], iscr[:, 1:9]))
            link(dve.tensor_copy(tnum[:], iscr[:, 16:16 + NT + 1]))
            link(dve.tensor_scalar(iscr[:, 256:384], iscr[:, 128:256], 7, None, ALU.bitwise_and))
            link(dve.tensor_scalar(same_expert[:], iscr[:, 256:384], 0.0, None, ALU.is_equal))
            link(dve.tensor_scalar(iscr[:, 10:11], iscr[:, 0:1], 16, None, ALU.bitwise_and))
            link(dve.tensor_scalar(low_rows[:], iscr[:, 10:11], -1.0 / 16, None, ALU.mult))
            link(dve.tensor_scalar(region_at[:], iota8[:], float(REGION), None, ALU.mult))
            dve.tensor_scalar(padrow[:, :, C], slot_num[:], float(T), None, ALU.add).then_inc(s_padrow, 1)
            dve.wait_ge(s_const, 96)
            link(dve.tensor_scalar(wraw[:, :, 0:256], wraw[:, :, 0:256], D ** -0.5, None, ALU.mult))
            for w, c0 in ((wq, 0), (wk, 256)):
                for r in (0, 1):
                    src = wraw[:, :, c0:c0 + 256].rearrange("p k (h d) -> p k h d", h=H)
                    hi, lo = (w[:, s].rearrange("p k (h r d) -> p k h r d", h=H, r=2)[:, :, :, r, :] for s in (0, 1))
                    for k in (0, 1):
                        link(dve.tensor_copy(hi[:, k], src[:, k]))
                        link(dve.tensor_tensor(lo[:, k], src[:, k], hi[:, k], ALU.subtract))
            for w, src in ((wv, wraw[:, :, 512:768]), (wp, praw[:])):
                link(dve.tensor_copy(w[:, 0], src))
                link(dve.tensor_tensor(w[:, 1], src, w[:, 0], ALU.subtract))
            link(dve.tensor_copy(bp[:, 0], braw[:]))
            dve.tensor_tensor(bp[:, 1], braw[:], bp[:, 0], ALU.subtract).then_inc(s_made, 1)
            dve.wait_ge(s_tanh, 2)
            link(dve.tensor_scalar(bitf[:], tgf[:], 1.0 / (WS * WS), None, ALU.mult))
            link(dve.tensor_copy(tgf[:], bitf[:]))

            def norm_stats(src, mv, ve, ready):
                for t in (0, 1):
                    link(dve.bn_stats(stats[:, t], src[:, t]))
                    settle(dve, dve_waits_over)
                for t in (0, 1):
                    link(dve.bn_aggr(mv[:, t], stats[:, t]))
                    settle(dve, dve_waits_over)
                dve.tensor_scalar(ve[:], mv[:, :, 1], EPS, None, ALU.add).then_inc(ready, 1)

            def ptx_evac(b, h):
                g = b.n * H + h
                dve.wait_ge(turned, g + 1)
                wait(dve, pv_done, g - 1)
                dve.tensor_copy(ptx[:, h % 2].rearrange("p k t q -> p (k t q)"), ptx_ps[:]).then_inc(ptx_out, 1)

            def row_max(b, h):
                g = b.n * H + h
                dve.wait_ge(scored, g + 1)
                wait(dve, expd, g - 1)
                dve.tensor_reduce(negmax[:, h % 2], bank[h % 2][:, :, 0:NK], AX, ALU.max, negate=True).then_inc(maxed, 1)

            def o_evac(b, half):
                dve.wait_ge(pv_done, b.n * H + 8 * half + 8)
                src = o_ps[:, 0:272].rearrange("p (u d) -> p u d", d=17)
                link(dve.reciprocal(rden[:].unsqueeze(2), src[:, :, 16:17]))
                dst = o[:].rearrange("p t (h d) -> p h t d", h=H)[:, 8 * half:8 * half + 8]
                dve.tensor_tensor(dst, src[:, :, 0:16].rearrange("p (h t) d -> p h t d", t=2),
                                  bc(rden[:].rearrange("p (h t) -> p h t", t=2), 3, [128, 8, 2, 16]), ALU.mult).then_inc(o_out, 1)

            def low(k, b, hi, lo):
                dve.wait_ge(pre_hi, b.n * 5 + k + 1)
                dve.tensor_tensor(lo, misc[:].rearrange("p (c t) -> p c t", c=2), hi, ALU.subtract).then_inc(emptied, 1)

            def route(b):
                par = b.par
                dve.wait_ge(ex_ready, b.n + 1)
                link(dve.tensor_reduce(esum[:], ex[:], AX, ALU.add))
                link(dve.reciprocal(esum[:], esum[:]))
                link(dve.tensor_tensor(pr[:], ex[:], bc(esum[:], 2, [128, 2, 8]), ALU.mult))
                mine, other = bc(pr[:], 3, [128, 2, 8, 8]), bc(pr[:], 2, [128, 2, 8, 8])
                dve.tensor_tensor(gt[:], other, mine, ALU.is_gt)
                link(dve.tensor_tensor(eq[:], other, mine, ALU.is_equal))
                link(dve.tensor_tensor(eq[:], eq[:], bc(before[:], 1, [128, 2, 8, 8]), ALU.mult))
                link(dve.tensor_tensor(gt[:], gt[:], eq[:], ALU.add))
                link(dve.tensor_reduce(rank[:], gt[:], AX, ALU.add))
                for c in (0, 1):
                    dve.tensor_scalar(oh[:, c], rank[:], float(c), None, ALU.is_equal)
                link(dve.tensor_scalar(sel[:], rank[:], 1.0, None, ALU.is_le))
                dve.tensor_tensor(ohp[:, 0], oh[:, 0], pr[:], ALU.mult).then_inc(sel_ready, 1)
                link(dve.tensor_tensor(ohp[:, 1], oh[:, 1], pr[:], ALU.mult))
                link(dve.tensor_reduce(pg[:], ohp[:], AX, ALU.add))
                link(dve.tensor_tensor(den[:], pg[:, 0], pg[:, 1], ALU.add))
                link(dve.tensor_scalar(den[:], den[:], 1e-9, None, ALU.add))
                link(dve.reciprocal(den[:], den[:]))
                link(dve.tensor_tensor(gsel[:], pg[:], bc(den[:], 1, [128, 2, 2]), ALU.mult))
                dve.tensor_copy(row[:, par, :, C + 1:C + 3].rearrange("p t c -> p c t"), gsel[:])
                link(dve.tensor_tensor(ohp[:, 0], ohp[:, 0], ohp[:, 1], ALU.add))
                link(dve.tensor_tensor(gall[:, bass.ds(2 * b.n, 2)], ohp[:, 0], bc(den[:], 2, [128, 2, 8]), ALU.mult))
                link(dve.tensor_tensor(ohp[:, 1], oh[:, 0], bc(iota8[:], 1, [128, 2, 8]), ALU.mult))
                link(dve.tensor_reduce(row[:, par, :, C + 3:C + 4].rearrange("p t a -> p (t a)"), ohp[:, 1], AX, ALU.add))
                link(dve.tensor_copy(row[:, par, :, C], tok_of[:]))

            def place(b):
                dve.wait_ge(filled, post_use(b, 4) + 1)
                link(dve.tensor_tensor(pos[:], misc[:, 0:16].rearrange("p (t e) -> p t e", t=2), bc(region_at[:], 1, [128, 2, 8]), ALU.add))
                link(dve.tensor_tensor(seen[:], seen[:], sel[:, 0], ALU.add))
                link(dve.tensor_tensor(seen[:], seen[:], sel[:, 1], ALU.add))
                for c in (0, 1):
                    link(dve.tensor_tensor(ohp[:, c], oh[:, c], pos[:], ALU.mult))
                link(dve.tensor_reduce(idxf[:], ohp[:], AX, ALU.add))
                dve.tensor_copy(idx[:, b.par], idxf[:]).then_inc(idx_ready, 1)
                link(dve.tensor_scalar(tok_of[:], tok_of[:], float(N), None, ALU.add))

            def body(b, heads, post, pre):
                nb, lb = b.next(), b.prev()
                for h in range(H):
                    if h == 0 and post:
                        ptx_evac(lb, H - 1)
                    if heads and h:
                        ptx_evac(b, h - 1)
                    if post and h == 1:
                        o_evac(lb, 1)
                    if heads and h == 9:
                        o_evac(b, 0)
                    if heads and h + 1 < H:
                        row_max(b, h + 1)
                    if pre and h + 1 == H:
                        row_max(nb, 0)
                    if pre and h == 0:
                        dve.wait_ge(s_x[nb.par], 16 * (nb.half + 1))
                        norm_stats(xb[:, nb.par], mv1, ve1, ve1_ready)
                    if pre and h == 2:
                        dve.wait_ge(rs1_ready, nb.n + 1)
                        for t in (0, 1):
                            last = dve.tensor_scalar(xn[:, t], xb[:, nb.par, t], mv1[:, t, 0:1], rs1[:, t:t + 1], ALU.subtract, ALU.mult)
                        last.then_inc(xn_ready, 1)
                    if post and h == 2:
                        dve.wait_ge(ot_hi, lb.n + 1)
                        dve.tensor_tensor(oTl[:].rearrange("p k t -> p (k t)"), misc[:], oTh[:].rearrange("p k t -> p (k t)"),
                                          ALU.subtract).then_inc(emptied, 1)
                    if post and h == 3:
                        dve.wait_ge(filled, post_use(lb, 1) + 1)
                        dve.wait_ge(s_xr[lb.par], 16 * (lb.half + 1))
                        xrow = xr[:, lb.par].rearrange("p t c -> p (t c)")
                        dve.scalar_tensor_tensor(xrow, misc[:], tgx[:, 0:1], xrow, ALU.mult, ALU.add).then_inc(x1_ready, 1)
                        dve.wait_ge(x1_ready, lb.n + 1)
                        dve.sem_inc(emptied, 1)
                        norm_stats(xr[:, lb.par], mv2, ve2, ve2_ready)
                    if post and h == 4:
                        dve.wait_ge(rs2_ready, lb.n + 1)
                        wait(dve, s_scat[lb.par], 64 * lb.half)
                        for t in (0, 1):
                            last = dve.tensor_scalar(row[:, lb.par, t, 0:C], xr[:, lb.par, t], mv2[:, t, 0:1], rs2[:, t:t + 1], ALU.subtract, ALU.mult)
                        last.then_inc(row_ready, 1)
                    if post and h == 6:
                        dve.wait_ge(filled, post_use(lb, 3) + 1)
                        mlg = misc[:, 0:16].rearrange("p (t e) -> p t e", t=2)
                        link(dve.tensor_reduce(lmax[:], mlg, AX, ALU.max))
                        dve.tensor_tensor(lg[:], mlg, bc(lmax[:], 2, [128, 2, 8]), ALU.subtract).then_inc(lg_ready, 1)
                        dve.wait_ge(lg_ready, lb.n + 1)
                        dve.sem_inc(emptied, 1)
                    if post and h == 7:
                        route(lb)
                    if post and h == 9:
                        place(lb)
                        dve.sem_inc(emptied, 1)
                    if pre and h == 9:
                        low(0, nb, xTh[:], xTl[:])
                    if pre and h in (10, 11):
                        c = 2 * (h - 10)
                        dve.wait_ge(pre_hi, nb.n * 5 + h - 8)
                        dve.scalar_tensor_tensor(qst[:, nb.par, c:c + 2].rearrange("p c t -> p (c t)"), qhi[:], low_rows[:, 0:1], misc[:],
                                                 ALU.mult, ALU.add).then_inc(emptied, 1)
                    if pre and h in (12, 13):
                        c = 2 * (h - 12)
                        low(h - 9, nb, kh[:, nb.par, c:c + 2, NC:NK], kl[:, nb.par, c:c + 2, NC:NK])

            link.per = 37
            batches(dve, body, link)
            link.rest()

            dve.sem_inc(s_cnt_in, 1)
            dve.wait_ge(s_cnt, 1)
            link(dve.tensor_copy(cnt[:], misc[:, 0:8]))
            for s in (0, 1):
                link(dve.tensor_tensor(padf[:, s], cnt[:], region_at[:], ALU.add))
                link(dve.tensor_scalar(padf[:, s], padf[:, s], slot_num[:, s:s + 1], None, ALU.add))
                dve.tensor_copy(padi[:, s], padf[:, s]).then_inc(s_padi, 1)
            link(dve.tensor_scalar(nti[:], cnt[:], float(TS - 1), None, ALU.add))
            link(dve.tensor_scalar(nti[:], nti[:], TS.bit_length() - 1, None, ALU.logical_shift_right))
            link(dve.tensor_copy(ntf[:], nti[:]))
            link(dve.tensor_tensor_scan(tend[:], ones32[:, 0:8], ntf[:], 0.0, ALU.mult, ALU.add))
            shape = [128, NT + 1, 8]
            link(dve.tensor_tensor(tcmp[:], bc(tnum[:], 2, shape), bc(tend[:], 1, shape), ALU.is_ge))
            link(dve.tensor_tensor(tcmp2[:], tcmp[:], bc(ntf[:], 1, shape), ALU.mult))
            link(dve.tensor_reduce(texp[:], tcmp[:], AX, ALU.add))
            link(dve.tensor_reduce(tbase[:], tcmp2[:], AX, ALU.add))
            link(dve.tensor_tensor(tbase[:], tnum[:], tbase[:], ALU.subtract))
            link(dve.tensor_scalar(tbase[:], tbase[:], float(TS), None, ALU.mult))
            link(dve.tensor_scalar(tscr[:], texp[:], float(REGION), None, ALU.mult))
            link(dve.tensor_tensor(tbase[:], tbase[:], tscr[:], ALU.add))
            link(dve.tensor_scalar(tabs[:, 1], tbase[:], float(E * REGION), None, ALU.min))
            link(dve.tensor_scalar(tscr[:], texp[:], float(E - 1), None, ALU.min))
            link(dve.tensor_copy(tabs[:, 0], tscr[:]))
            link(dve.memset(tabs[:, 2, 0:2], 1))
            dve.tensor_tensor(tabs[:, 2, 2:], tscr[:, 2:], tscr[:, :NT - 1], ALU.not_equal).then_inc(s_tabs, 1)

            dve.wait_ge(s_gt, 1)
            link(dve.tensor_copy(gT[:], o_ps[:]))
            link(dve.memset(thr[:], 0))
            link(dve.memset(bit[:], 1 << 29))
            link(dve.memset(cut[:], 0.0))
            link(dve.memset(stepf[:], float(1 << 13)))
            link.rest()
            start = link.base
            with dve.Fori(0, 30) as i:
                link.base, link.n = start + i * 5, 0
                link(dve.tensor_tensor(cand[:], thr[:], bit[:], ALU.bitwise_or))
                dve.tensor_scalar(gcmp[:], gT[:], cand[:, 0:1].bitcast(F32), 0.0, ALU.is_ge, ALU.add, accum_out=count[:]).then_inc(s_cnt_in, 1)
                dve.wait_ge(s_count, i + 1)
                link(dve.tensor_scalar(keep_i[:], ptx_ps[:, 0:1], float(CAP), -1.0, ALU.is_ge, ALU.mult))
                link(dve.tensor_tensor(keep_i[:], keep_i[:], bit[:], ALU.bitwise_and))
                link(dve.tensor_tensor(thr[:], thr[:], keep_i[:], ALU.bitwise_or))
                link(dve.tensor_scalar(bit[:], bit[:], 1, None, ALU.logical_shift_right))
                assert link.n == 5
            link.base, link.n = start + 150, 0
            thrf = thr[:, 0:1].bitcast(F32)
            dve.tensor_scalar(gcmp[:], gT[:], thrf, 0.0, ALU.is_gt, ALU.add, accum_out=count[:]).then_inc(s_cnt_in, 1)
            dve.wait_ge(s_count, 31)
            link(dve.tensor_scalar(need[:], ptx_ps[:, 0:1], -1.0, float(CAP), ALU.mult, ALU.add))
            link(dve.tensor_scalar(gcmp[:], gT[:], thrf, float(4 * T), ALU.not_equal, ALU.mult))
            link(dve.tensor_tensor(tokT[:], tokT[:], gcmp[:], ALU.add))
            link.rest()
            start = link.base
            with dve.Fori(0, 14) as i:
                link.base, link.n = start + i * 4, 0
                link(dve.tensor_tensor(candf[:], cut[:], stepf[:], ALU.add))
                dve.tensor_scalar(gcmp[:], tokT[:], candf[:, 0:1], 0.0, ALU.is_lt, ALU.add, accum_out=count[:]).then_inc(s_cnt_in, 1)
                dve.wait_ge(s_count, i + 32)
                link(dve.tensor_scalar(candf[:], ptx_ps[:, 0:1], need[:, 0:1], stepf[:, 0:1], ALU.is_le, ALU.mult))
                link(dve.tensor_tensor(cut[:], cut[:], candf[:], ALU.add))
                link(dve.tensor_scalar(stepf[:], stepf[:], 0.5, None, ALU.mult))
                assert link.n == 4
            link.base, link.n = start + 56, 0
            dve.tensor_scalar(diag[:, 0], ident[0:8, 0:8], thr[0:8, 0:1].bitcast(F32), None, ALU.mult)
            dve.tensor_scalar(diag[:, 1], ident[0:8, 0:8], cut[0:8, 0:1], None, ALU.mult).then_inc(s_limin, 1)
            dve.wait_ge(s_lim, 1)
            link(dve.tensor_copy(lim[:].rearrange("p a e -> p (a e)"), ptx_ps[:, 8:24]))
            link(dve.tensor_tensor(tcmp[:], bc(texp[:], 2, shape), bc(iota8[:], 1, shape), ALU.is_equal))
            for a, dst in ((0, thr_t), (1, cut_t)):
                link(dve.tensor_tensor(tcmp2[:], tcmp[:], bc(lim[:, a], 1, shape), ALU.mult))
                link(dve.tensor_reduce(dst[:], tcmp2[:], AX, ALU.add))
            dve.sem_inc(s_limits_ok, 1)
            link.rest()

            def turned_low(t):
                dve.wait_ge(et_hi, t.n + 1)
                dve.tensor_tensor(eTl[:, t.par].rearrange("p k t -> p (k t)"), misc[:], eTh[:, t.par].rearrange("p k t -> p (k t)"),
                                  ALU.subtract).then_inc(et_lo, 1)

            def low_h(t, c):
                dve.wait_ge(hhi_done, t.n * 8 + c + 1)
                dve.tensor_tensor(hl[:, c % 4], h32[:, c % 2], hh[:, c % 4], ALU.subtract).then_inc(hlo_done, 1)

            def y_evac(t):
                dve.wait_ge(y_filled, t.n + 1)
                for s in (0, 1):
                    last = dve.tensor_scalar(y[:, t.par, s], y_ps[t.par][:, s * 256:s * 256 + 256], gf[:, t.par, s:s + 1], None, ALU.mult)
                last.then_inc(y_out, 1)

            y_ps = (ptc_ps, o_ps)

            def gates(t):
                par = t.par
                e_t, th, ct = (a[:, bass.ds(t.n, 1)] for a in (texp, thr_t, cut_t))
                tok, g0, g1, e0 = (xe[:, par, :, C + k] for k in range(4))
                wait(dve, s_add, 32 * (t.n - 1))
                link(dve.tensor_scalar(ga[:], e0, e_t, None, ALU.is_equal))
                dve.tensor_scalar(gb[:], e0, e_t, None, ALU.not_equal)
                link(dve.tensor_tensor(ga[:], ga[:], g0, ALU.mult))
                link(dve.tensor_tensor(gb[:], gb[:], g1, ALU.mult))
                link(dve.tensor_tensor(gg[:], ga[:], gb[:], ALU.add))
                dve.tensor_copy(toki[:, par], tok)
                link(dve.tensor_scalar(ga[:], gg[:], th, None, ALU.is_gt))
                dve.tensor_scalar(gb[:], gg[:], th, None, ALU.is_equal)
                link(dve.tensor_scalar(gk[:], tok, ct, None, ALU.is_lt))
                link(dve.tensor_tensor(gb[:], gb[:], gk[:], ALU.mult))
                link(dve.tensor_tensor(ga[:], ga[:], gb[:], ALU.add))
                link(dve.tensor_tensor(ga[:], ga[:], gg[:], ALU.mult))
                dve.tensor_scalar(gf[:, par], ga[:], tgf[:, 0:1], None, ALU.mult).then_inc(gf_ready, 1)

            def tile(t):
                first = isinstance(t.n, int) and t.n < 0
                last = isinstance(t.n, int) and t.n == NT
                zero = isinstance(t.n, int) and t.n == 0
                if first:
                    return turned_low(t.next())
                for c in range(8):
                    if not last:
                        u = t.n * 8 + c
                        dve.wait_ge(silu_done, u + 1)
                        wait(dve, hlo_done, u - 1)
                        dve.tensor_tensor(h32[:, c % 2], sg[:, c % 2], bank[c % 4 // 2][:, c % 2, TS:2 * TS], ALU.mult).then_inc(mult_done, 1)
                    if c == 0 and not zero:
                        low_h(t.prev(), 7)
                    if c and not last:
                        low_h(t, c - 1)
                    if c == 2 and not zero:
                        y_evac(t.prev())
                    if c == 3 and not last:
                        gates(t)
                    if c == 4 and not last:
                        turned_low(t.next())

            link.per = 9
            tiles(dve, tile, link)


def kernel(x, ctx_2048, g_xattn, g_ffn, L0_xattn_w_qkv, L0_xattn_w_proj, L0_xattn_b_proj,
           L0_ffn_router_gate, L0_ffn_gate_w, L0_ffn_up_w, L0_ffn_down_w):
    import numpy as np
    import concourse.bacc as bacc
    from concourse.bass_utils import run_bass_kernel_spmd as run

    ctx = np.asarray(ctx_2048)
    kT = ctx[:, :, :C].reshape(B, NC, 4, 4, D).transpose(0, 3, 4, 2, 1)
    kT = np.repeat(kT[:, :, None], 2, axis=2).reshape(B, 128, 4, NC)
    arrays = {
        "x": np.asarray(x), "ctx_kT": kT, "ctx": ctx, "g_xattn": np.asarray(g_xattn), "g_ffn": np.asarray(g_ffn),
        "wqkvT": np.asarray(L0_xattn_w_qkv).T, "wprojT": np.asarray(L0_xattn_w_proj).T, "b_proj": np.asarray(L0_xattn_b_proj),
        "router_w": np.asarray(L0_ffn_router_gate), "gate_w": np.asarray(L0_ffn_gate_w), "up_w": np.asarray(L0_ffn_up_w),
        "down_w": np.asarray(L0_ffn_down_w),
    }
    arrays = {n: np.ascontiguousarray(a) for n, a in arrays.items()}
    nc = bacc.Bacc("TRN2", target_bir_lowering=False, num_devices=1)
    args = [nc.dram_tensor(n, a.shape, mybir.dt.from_np(a.dtype), kind="ExternalInput").ap() for n, a in arrays.items()]
    out = nc.dram_tensor("out", (T + TS, C), F32, kind="ExternalOutput").ap()
    flamingo_block(nc, *args, out)
    r = run(nc, [arrays], core_ids=[0])
    return r.results[0]["out"][:T].reshape(B, N, C)
```

```python
import concourse.bass as bass
from concourse import mybir
from contextlib import ExitStack

F32, F16, BF16, I32, U16 = mybir.dt.float32, mybir.dt.float16, mybir.dt.bfloat16, mybir.dt.int32, mybir.dt.uint16
ALU = mybir.AluOpType
ACT = mybir.ActivationFunctionType
AX = mybir.AxisListType.X

B, N, C, NC = 32, 256, 256, 77
H, D = 16, 16
NK = NC + N
T = B * N
E, I, K = 8, 1024, 2
CAP = int(1.25 * ((T * K + E - 1) // E))
TS = 256
REGION = T + TS
NT = T * K // TS + E - 1
ROW = C + 4
WPIECE = 6 * 512
WS = 64.0
EPS = 1e-5
USES = [(3, "pre", 0), (4, "post", 0), (5, "post", 1), (6, "pre", 1), (7, "post", 2), (8, "post", 3),
        (9, "pre", 2), (10, "post", 4), (11, "pre", 3)]
PRE = sum(u[1] == "pre" for u in USES)


W_SLOTS = (1, 12, 13)


def uses_of(body):
    return [u for u in USES if (body >= 1 if u[1] == "post" else body < B - 1)]


def use(body, kind, k):
    if isinstance(body, int):
        before = sum(len(uses_of(b)) for b in range(-1, body))
        return before + [u[1:] for u in uses_of(body)].index((kind, k))
    return (body - 1) * len(USES) + len(uses_of(-1)) + len(uses_of(0)) + [u[1:] for u in USES].index((kind, k))


class At:
    def __init__(self, n, half, par):
        self.n, self.half, self.par = n, half, par

    def next(self):
        return At(self.n + 1, self.half + self.par, 1 - self.par)

    def prev(self):
        return At(self.n - 1, self.half - (1 - self.par), 1 - self.par)


def at(n):
    return At(n, n // 2, n % 2)


def settle(eng, waits_over):
    eng.sem_inc(waits_over, 1)


def wait(eng, sem, value):
    if isinstance(value, int) and value <= 0:
        return
    eng.wait_ge(sem, value)


def flamingo_block(nc, x, ctx_kT, ctx, g_xattn, g_ffn, wqkvT, wprojT, b_proj, router_w, gate_w, up_w, down_w, out):
    slots = nc.dram_tensor("slots", [E * REGION + TS, ROW], F32).ap()
    wsplit = nc.dram_tensor("wsplit", [E, 4, 128, WPIECE], F16).ap()
    q_turn = nc.dram_tensor("q_turn", [2, 8, D, 2, 2, 2 * N], F16).ap()
    k_turn = nc.dram_tensor("k_turn", [2, 8, D, 2, 2, 2 * NK], F16).ap()

    ctx_stack = ExitStack()
    with ctx_stack:
        def sb(name, shape, dt=F32):
            return ctx_stack.enter_context(nc.sbuf_tensor(name, shape, dt))

        def sem(name):
            return ctx_stack.enter_context(nc.semaphore(name))

        bank = [ctx_stack.enter_context(nc.psum_tensor(f"pair{i}", [128, 2, 512], F32)) for i in range(2)]
        ptx_ps = ctx_stack.enter_context(nc.psum_tensor("ptx_ps", [128, 512], F32))
        ptc_ps = ctx_stack.enter_context(nc.psum_tensor("ptc_ps", [128, 512], F32))
        o_ps = ctx_stack.enter_context(nc.psum_tensor("o_ps", [128, 512], F32))
        misc = ctx_stack.enter_context(nc.psum_tensor("misc", [128, 512], F32))

        ident = sb("ident", [128, 128])
        tri = sb("tri", [128, 128], F16)
        ones16 = sb("ones16", [128, 128], F16)
        ones32 = sb("ones32", [128, 128])
        same_expert = sb("same_expert", [128, 128])
        iscr = sb("iscr", [128, 512], I32)
        iota8 = sb("iota8", [128, 8])
        region_at = sb("region_at", [128, 8])
        before = sb("before", [128, 8, 8])
        slot_num = sb("slot_num", [128, 2])
        tok_of = sb("tok_of", [128, 2])
        tokTi = sb("tokTi", [128, 512], I32)
        mhalf = sb("mhalf", [128, 2])
        wraw = sb("wraw", [128, 2, 768])
        praw = sb("praw", [128, 2, 256])
        braw = sb("braw", [1, 256])
        rout = sb("rout", [128, 2, 8])
        wq = sb("wq", [128, 2, 2, 256], F16)
        wk = sb("wk", [128, 2, 2, 256], F16)
        wv = sb("wv", [128, 2, 2, 256], F16)
        wp = sb("wp", [128, 2, 2, 256], F16)
        bp = sb("bp", [1, 2, 256], F16)
        tgx = sb("tgx", [128, 1])
        tgf = sb("tgf", [128, 1])

        xb = sb("xb", [128, 2, 2, 256])
        xr = sb("xr", [128, 2, 2, 256])
        ckraw = sb("ckraw", [128, 2, 2, NC])
        cvraw = sb("cvraw", [NC, 2, 256])
        stats = sb("stats", [128, 2, 6])
        mv1 = sb("mv1", [128, 2, 2])
        mv2 = sb("mv2", [128, 2, 2])
        ve1 = sb("ve1", [128, 2])
        ve2 = sb("ve2", [128, 2])
        rs1 = sb("rs1", [128, 2])
        rs2 = sb("rs2", [128, 2])
        xn = sb("xn", [128, 2, 256])
        xTh = sb("xTh", [128, 2, 256], F16)
        xTl = sb("xTl", [128, 2, 256], F16)
        qs = sb("qs", [128, 2, 2, N], F16)
        ks = sb("ks", [128, 2, 2, NK], F16)
        qst = sb("qst", [128, 2, 4, 2, N], F16)
        kst = sb("kst", [128, 2, 4, 2, NK], F16)
        vh = sb("vh", [128, 2, 3, H, D + 1], F16)
        vl = sb("vl", [128, 2, 3, H, D], F16)
        negmax = sb("negmax", [128, 2, 2])
        p = sb("p", [128, 2, 2, NK])
        p_high = p[:].bitcast(BF16)[:, :, :, 1:2 * NK:2]
        pl = sb("pl", [128, 2, 2, NK], F16)
        ptx = sb("ptx", [128, 2, 2, 2, 2, 128], U16)
        ptc = sb("ptc", [NC, 2, 2, 2, 128], U16)
        ident_b = sb("ident_b", [128, 128], BF16)
        ident_h = sb("ident_h", [128, 128], F16)
        rden = sb("rden", [128, 16])
        o = sb("o", [128, 2, 256])
        oTh = sb("oTh", [128, 2, 256], F16)
        oTl = sb("oTl", [128, 2, 256], F16)
        row = sb("row", [128, 2, 2, ROW])
        xn2T = sb("xn2T", [128, 2, 256])
        lmax = sb("lmax", [128, 2])
        lg = sb("lg", [128, 2, 8])
        ex = sb("ex", [128, 2, 8])
        esum = sb("esum", [128, 2])
        pr = sb("pr", [128, 2, 8])
        gt = sb("gt", [128, 2, 8, 8])
        eq = sb("eq", [128, 2, 8, 8])
        rank = sb("rank", [128, 2, 8])
        oh = sb("oh", [128, 2, 2, 8])
        ohp = sb("ohp", [128, 2, 2, 8])
        pg = sb("pg", [128, 2, 2])
        den = sb("den", [128, 2])
        gsel = sb("gsel", [128, 2, 2])
        sel = sb("sel", [128, 2, 8], F16)
        seen = sb("seen", [128, 8], F16)
        pos = sb("pos", [128, 2, 8])
        idxf = sb("idxf", [128, 2, 2])
        idx = sb("idx", [128, 2, 2, 2], I32)
        ohq = sb("ohq", [128, 2, 2, 8])
        gall = sb("gall", [128, 2 * B, 8])
        wst = sb("wst", [128, 2, 3, 512])
        wout = sb("wout", [128, 2, 6, 512], F16)

        cnt = sb("cnt", [128, 8])
        nti = sb("nti", [128, 8], I32)
        ntf = sb("ntf", [128, 8])
        tend = sb("tend", [128, 8])
        tnum = sb("tnum", [128, NT + 1])
        tcmp = sb("tcmp", [128, NT + 1, 8])
        tcmp2 = sb("tcmp2", [128, NT + 1, 8])
        texp = sb("texp", [128, NT + 1])
        tbase = sb("tbase", [128, NT + 1])
        tscr = sb("tscr", [128, NT + 1])
        tabs = sb("tabs", [128, 3, NT + 1], I32)
        thr_t = sb("thr_t", [128, NT + 1])
        cut_t = sb("cut_t", [128, NT + 1])
        padf = sb("padf", [128, 2, 8])
        padi = sb("padi", [128, 2, 8], I32)
        padrow = sb("padrow", [128, 2, ROW])
        gT = sb("gT", [128, 512])
        tokT = sb("tokT", [128, 512])
        gcmp = sb("gcmp", [128, 512])
        thr = sb("thr", [128, 1], I32)
        cand = sb("cand", [128, 1], I32)
        bit = sb("bit", [128, 1], I32)
        bitf = sb("bitf", [128, 1])
        keep_i = sb("keep_i", [128, 1], I32)
        count = sb("count", [128, 1])
        need = sb("need", [128, 1])
        cut = sb("cut", [128, 1])
        candf = sb("candf", [128, 1])
        stepf = sb("stepf", [128, 1])
        diag = sb("diag", [8, 2, 8])
        lim = sb("lim", [128, 2, 8])

        wb = sb("wb", [128, 2, 4, WPIECE], F16)
        xe = sb("xe", [128, 2, 2, ROW])
        eTh = sb("eTh", [128, 2, 2, TS], F16)
        eTl = sb("eTl", [128, 2, 2, TS], F16)
        sg = sb("sg", [128, 2, TS])
        h32 = sb("h32", [128, 2, TS])
        hh = sb("hh", [128, 4, TS], F16)
        hl = sb("hl", [128, 4, TS], F16)
        gf = sb("gf", [128, 2, 2])
        ga = sb("ga", [128, 2])
        gb = sb("gb", [128, 2])
        gg = sb("gg", [128, 2])
        gk = sb("gk", [128, 2])
        toki = sb("toki", [128, 2, 2], I32)
        y = sb("y", [128, 2, 2, 256])

        s_const = sem("const_loaded")
        s_made = sem("const_made")
        s_pmade = sem("pool_const_made")
        s_tanh = sem("tanh_done")
        sp_waits_over, pool_waits_over, dve_waits_over = sem("sp_waits_over"), sem("pool_waits_over"), sem("dve_waits_over")
        s_padrow = sem("pad_rows_made")
        s_kh, s_vh = sem("ctx_key_high"), sem("ctx_value_high")
        plow = sem("probs_low")
        w_high = sem("w_high")
        s_dve = sem("dve_order")
        s_pool = sem("pool_order")
        s_x = [sem("x_loaded0"), sem("x_loaded1")]
        s_ck = [sem("ctxk_loaded0"), sem("ctxk_loaded1")]
        s_cv = [sem("ctxv_loaded0"), sem("ctxv_loaded1")]
        q_saved, k_saved = sem("q_saved"), sem("k_saved")
        q_stacked = [sem("q_stacked0"), sem("q_stacked1")]
        k_stacked = [sem("k_stacked0"), sem("k_stacked1")]
        s_w = [sem("w_loaded0"), sem("w_loaded1")]
        s_xr = [sem("residual_loaded0"), sem("residual_loaded1")]
        s_xst = [sem("x1_stored0"), sem("x1_stored1")]
        s_wst = [sem("w_stored0"), sem("w_stored1")]
        s_scat = [sem("rows_scattered0"), sem("rows_scattered1")]
        ve1_ready, rs1_ready, ve2_ready, rs2_ready = sem("ve1_ready"), sem("rs1_ready"), sem("ve2_ready"), sem("rs2_ready")
        xn_ready, x1_ready, row_ready = sem("xn_ready"), sem("x1_ready"), sem("row_ready")
        ctx_split, w_split = sem("ctx_split"), sem("w_split")
        filled, emptied = sem("misc_filled"), sem("misc_emptied")
        pre_hi, ot_hi = sem("pre_high"), sem("ot_high")
        scored, maxed, expd = sem("scored"), sem("maxed"), sem("exp_done")
        turned, ptx_out, ptc_out = sem("probs_turned"), sem("ptx_out"), sem("ptc_out")
        pv_done, o_out = sem("pv_done"), sem("o_out")
        xn2t_ready, lg_ready, ex_ready, sel_ready, idx_ready = (
            sem("xn2t_ready"), sem("logits_ready"), sem("router_exp"), sem("sel_ready"), sem("idx_ready"))
        s_cnt, s_gt, s_gtc, s_count, s_cnt_in, s_lim, s_limin = (
            sem("counts_done"), sem("gates_turned"), sem("gates_copied"), sem("count_summed"), sem("count_in"),
            sem("limits_done"), sem("limits_in"))
        s_tabs, s_padi, s_pads = sem("tables_ready"), sem("pads_ready"), sem("pads_stored")
        s_dummy = sem("dummy_rows_stored")
        s_limits_ok = sem("limits_ready")
        s_wl = [sem("expert_w0"), sem("expert_w1")]
        s_xe = [sem("slots_loaded0"), sem("slots_loaded1")]
        gu_filled, silu_done, mult_done, hhi_done, hlo_done = (
            sem("gu_filled"), sem("silu_done"), sem("mult_done"), sem("hhi_done"), sem("hlo_done"))
        et_filled, et_hi, et_lo = sem("et_filled"), sem("et_high"), sem("et_low")
        y_filled, y_out, gf_ready, s_add = sem("y_filled"), sem("y_out"), sem("gf_ready"), sem("rows_added")

        def pre_use(b, k):
            return use(b.n - 1, "pre", k)

        def post_use(b, k):
            return use(b.n + 1, "post", k)

        def head_at(b, h, lag, heads, post, pre):
            n = h - lag
            if n < 0:
                return (b.prev(), n + H) if post else None
            if n >= H:
                return (b.next(), n - H) if pre else None
            return (b, n) if heads else None

        class Chain:
            def __init__(self, eng, s, after=None):
                self.eng, self.s, self.base, self.n, self.after = eng, s, 0, 0, after

            def __call__(self, ins):
                self.n += 1
                ins.then_inc(self.s, 1)
                self.eng.wait_ge(self.s, self.base + self.n)
                if self.after:
                    settle(self.eng, self.after)

            def rest(self):
                self.base, self.n = self.base + self.n, 0

        def batches(eng, body, chain=None):
            def part(*a):
                if chain:
                    chain.rest()
                body(*a)
            part(at(-1), False, False, True)
            part(at(0), True, False, True)
            part(at(1), True, True, True)
            part(at(2), True, True, True)
            if chain:
                chain.rest()
                start = chain.base
            with eng.Fori(1, (B - 2) // 2) as i:
                for j in (1, 2):
                    if chain:
                        chain.n = 0
                        chain.base = start + (i - 1) * (2 * chain.per) + (j - 1) * chain.per
                    body(At(2 * i + j, i + j // 2, j % 2), True, True, True)
                    if chain:
                        assert chain.n == chain.per, (chain.n, chain.per)
            if chain:
                chain.base, chain.n = start + (B - 4) * chain.per, 0
            part(at(B - 1), True, True, False)
            part(at(B), False, True, False)

        def tiles(eng, body, chain=None):
            def part(*a):
                if chain:
                    chain.rest()
                body(*a)
            part(at(-1))
            part(at(0))
            part(at(1))
            part(at(2))
            if chain:
                chain.rest()
                start = chain.base
            with eng.Fori(1, (NT - 1) // 2) as i:
                for j in (1, 2):
                    if chain:
                        chain.n = 0
                        chain.base = start + (i - 1) * (2 * chain.per) + (j - 1) * chain.per
                    body(At(2 * i + j, i + j // 2, j % 2))
                    if chain:
                        assert chain.n == chain.per, (chain.n, chain.per)
            if chain:
                chain.base, chain.n = start + (NT - 3) * chain.per, 0
            part(at(NT))

        block = ctx_stack.enter_context(nc.Block())

        @block.sync
        def _(sp):
            def load_batch(b):
                par = b.par
                wait(sp, xn_ready, b.n - 1)
                sp.dma_start(xb[:, par], x[bass.ds(b.n, 1)].rearrange("a (t p) c -> p (a t) c", p=128)).then_inc(s_x[par], 16)
                wait(sp, ctx_split, 2 * (b.n - 1))
                sp.dma_start(ckraw[:, par], ctx_kT[bass.ds(b.n, 1)].rearrange("a p c k -> p (a c) k")).then_inc(s_ck[par], 16)
                sp.dma_start(cvraw[:, par], ctx[bass.ds(b.n, 1), :, C:].rearrange("a k c -> k (a c)")).then_inc(s_cv[par], 16)

            def load_weights(b, e, q):
                wait(sp, w_split, 3 * (b.n - 1))
                for k, w in enumerate((gate_w, up_w)):
                    sp.dma_start(wst[:, b.par, k].rearrange("p (k c) -> p k c", k=2),
                                 w[bass.ds(e, 1), :, bass.ds(q * 256, 256)].rearrange("a (k p) c -> p (a k) c", p=128)
                                 ).then_inc(s_w[b.par], 16)
                sp.dma_start(wst[:, b.par, 2].rearrange("p (k c) -> p k c", k=2),
                             down_w[bass.ds(e, 1), bass.ds(q * 256, 256), :].rearrange("a (k p) c -> p (a k) c", p=128)
                             ).then_inc(s_w[b.par], 16)

            def stack(b):
                for step, turn_, made, stacks, saved, stacked in ((1, q_turn, qs, qst, q_saved, q_stacked),
                                                                  (2, k_turn, ks, kst, k_saved, k_stacked)):
                    sp.wait_ge(emptied, pre_use(b, step) + 1)
                    if step == 2:
                        settle(sp, sp_waits_over)
                        sp.wait_ge(ctx_split, 2 * (b.n + 1))
                    for s in (0, 1):
                        copies = turn_[b.par].rearrange("h d i j n -> (h d) i j n")
                        copies = copies[:, :, s] if step == 1 else copies[:, s]
                        sp.dma_start(copies, made[:, s].rearrange("p c n -> p (c n)").unsqueeze(1).to_broadcast(
                            [128, 2, 2 * (N if step == 1 else NK)])).then_inc(saved, 16)
                    wait(sp, pv_done, 16 * (b.n - 1))
                    settle(sp, sp_waits_over)
                    sp.wait_ge(saved, 32 * (b.n + 1))
                    sp.dma_start(stacks[:, b.par].rearrange("p a c n -> p a (c n)"),
                                 turn_[b.par].rearrange("(a h) d i j n -> (h d i j) a n", h=2)).then_inc(stacked[b.par], 16)

            def store_weights(b, e, q):
                sp.wait_ge(w_split, 3 * (b.n + 1))
                sp.dma_start(wsplit[bass.ds(e, 1), bass.ds(q, 1)].rearrange("a q p c -> p (a q c)"),
                             wout[:, b.par].rearrange("p s c -> p (s c)")).then_inc(s_wst[b.par], 16)

            def load_residual(b):
                wait(sp, s_xst[b.par], 16 * b.half)
                wait(sp, row_ready, b.n - 1)
                sp.dma_start(xr[:, b.par], x[bass.ds(b.n, 1)].rearrange("a (t p) c -> p (a t) c", p=128)).then_inc(s_xr[b.par], 16)

            def store_x1(b):
                sp.wait_ge(x1_ready, b.n + 1)
                sp.dma_start(out[bass.ds(b.n * N, N)].rearrange("(t p) c -> p t c", p=128), xr[:, b.par]).then_inc(s_xst[b.par], 16)

            load_batch(at(0))
            sp.dma_start(wraw[:], wqkvT.rearrange("(k p) n -> p k n", p=128)).then_inc(s_const, 16)
            sp.dma_start(praw[:], wprojT.rearrange("(k p) n -> p k n", p=128)).then_inc(s_const, 16)
            sp.dma_start(braw[:], b_proj.rearrange("(a n) -> a n", a=1)).then_inc(s_const, 16)
            sp.dma_start(rout[:], router_w.rearrange("(k p) n -> p k n", p=128)).then_inc(s_const, 16)
            sp.dma_start(tgx[:], g_xattn.rearrange("(a n) -> a n", a=1).to_broadcast([128, 1])).then_inc(s_const, 16)
            sp.dma_start(tgf[:], g_ffn.rearrange("(a n) -> a n", a=1).to_broadcast([128, 1])).then_inc(s_const, 16)
            load_batch(at(1))
            stack(at(0))
            for n in (0, 1):
                load_weights(at(n), 0, n)
                load_residual(at(n))
            load_batch(at(2))
            stack(at(1))
            store_weights(at(0), 0, 0)
            load_weights(at(2), 0, 2)

            def step(b, q0, q2):
                load_batch(b.next().next())
                store_x1(b.prev())
                load_residual(b.next())
                stack(b.next())
                store_weights(b, *q0)
                load_weights(b.next().next(), *q2)
            step(at(1), (0, 1), (0, 3))
            with sp.Fori(1, B // 2 - 1) as i:
                step(At(2 * i, i, 0), (i // 2, (i % 2) * 2), ((i + 1) // 2, ((i + 1) % 2) * 2))
                step(At(2 * i + 1, i, 1), (i // 2, (i % 2) * 2 + 1), ((i + 1) // 2, ((i + 1) % 2) * 2 + 1))
            store_x1(at(B - 3))
            load_residual(at(B - 1))
            stack(at(B - 1))
            for n in (B - 2, B - 1):
                store_weights(at(n), n // 4, n % 4)
                store_x1(at(n))

            sp.wait_ge(s_padrow, 1)
            sp.dma_start(out[T:T + TS].rearrange("(s p) c -> p s c", p=128), padrow[:, :, 0:C]).then_inc(s_dummy, 16)
            sp.dma_start(slots[E * REGION:].rearrange("(s p) c -> p s c", p=128), padrow[:]).then_inc(s_dummy, 16)
            sp.wait_ge(s_dummy, 32)
            for par in (0, 1):
                sp.wait_ge(s_scat[par], 64 * B // 2)
                sp.wait_ge(s_wst[par], 16 * B // 2)
                sp.wait_ge(s_xst[par], 16 * B // 2)
            sp.wait_ge(s_tabs, 1)
            sp.wait_ge(s_pads, 16 * 2 * E)

            def load_tile(t):
                e = nc.values_load(tabs[0:1, 0, bass.ds(t.n, 1)], engines=(mybir.EngineType.SP,), min_val=0, max_val=E - 1,
                                   skip_runtime_bounds_check_because="the table is clipped")
                r0 = nc.values_load(tabs[0:1, 1, bass.ds(t.n, 1)], engines=(mybir.EngineType.SP,), min_val=0, max_val=E * REGION,
                                    skip_runtime_bounds_check_because="the table is clipped")
                new = nc.values_load(tabs[0:1, 2, bass.ds(t.n, 1)], engines=(mybir.EngineType.SP,), min_val=0, max_val=1,
                                     skip_runtime_bounds_check_because="it is a comparison's result")
                wait(sp, gf_ready, t.n - 1)
                sp.dma_start(xe[:, t.par], slots[bass.ds(r0, TS)].rearrange("(s p) c -> p s c", p=128)).then_inc(s_xe[t.par], 16)
                wait(sp, y_filled, t.n - 1)
                sp.dma_start(wb[:, t.par], wsplit[bass.ds(e, 1)].rearrange("a q p c -> p (a q) c"),
                             cond=new).then_inc(s_wl[t.par], 16)

            for n in range(3):
                load_tile(at(n))
            with sp.Fori(1, (NT - 1) // 2) as i:
                for j in (1, 2):
                    load_tile(At(2 * i + j, i + j // 2, j % 2))
            load_tile(at(NT))
            sp.wait_ge(s_wl[1], 16 * ((NT + 1) // 2))
            sp.wait_ge(s_wl[0], 16 * ((NT + 1) // 2))
            sp.wait_ge(s_add, 32 * NT)

        @block.gpsimd
        def _(pool):
            chain = Chain(pool, s_pool)
            pool.memset(ident[:], 0.0).then_inc(s_pmade, 1)
            chain(pool.memset(tri[:], 1.0))
            pool.wait_ge(s_pmade, 1)
            chain(pool.affine_select(out=ident[:], in_=ident[:], compare_op=ALU.not_equal, fill=1.0, base=0,
                                     pattern=[[-1, 128]], channel_multiplier=1))
            chain(pool.affine_select(out=tri[:], in_=tri[:], compare_op=ALU.is_gt, fill=0.0, base=0,
                                     pattern=[[1, 128]], channel_multiplier=-1))
            chain(pool.memset(ones16[:], 1.0))
            chain(pool.memset(ones32[:], 1.0))
            chain(pool.memset(mhalf[:], -0.5))
            chain(pool.memset(seen[:], 0.0))
            for par in (0, 1):
                chain(pool.memset(vh[:, par, :, :, D:D + 1], 1.0))
            chain(pool.memset(before[:], 1.0))
            chain(pool.affine_select(out=before[:], in_=before[:], compare_op=ALU.is_gt, fill=0.0, base=0,
                                     pattern=[[1, 8], [-1, 8]], channel_multiplier=0))
            chain(pool.iota(iscr[:, 0:1], [[0, 1]], base=0, channel_multiplier=1))
            chain(pool.iota(iscr[:, 1:9], [[1, 8]], base=0, channel_multiplier=0))
            chain(pool.iota(iscr[:, 16:16 + NT + 1], [[1, NT + 1]], base=0, channel_multiplier=0))
            chain(pool.iota(iscr[:, 128:256], [[-1, 128]], base=128, channel_multiplier=1))
            chain(pool.iota(tokTi[:], [[16 * 128, 4], [1, 128]], base=0, channel_multiplier=0))
            pool.memset(padrow[:], 0.0).then_inc(s_pmade, 1)

            def body(b, heads, post, pre):
                nb, lb = b.next(), b.prev()
                for h in range(H):
                    if heads:
                        g = b.n * H + h
                        pool.wait_ge(expd, g + 1)
                        wait(pool, turned, g - 1)
                        pool.tensor_tensor(pl[:, h % 2], p[:, h % 2], p_high[:, h % 2], ALU.subtract).then_inc(plow, 1)
                    if pre and h == 0:
                        pool.wait_ge(ve1_ready, nb.n + 1)
                        pool.tensor_tensor(rs1[:], ve1[:], mhalf[:], ALU.pow).then_inc(rs1_ready, 1)
                    if pre and h in (2, 3):
                        if h == 2:
                            wait(pool, k_saved, 32 * nb.n)
                        else:
                            wait(pool, pv_done, 16 * (nb.n - 1))
                        src, high, low_, loaded, made = (
                            (ckraw[:, nb.par], ks[:, 0, :, 0:NC], ks[:, 1, :, 0:NC], s_ck, s_kh) if h == 2 else
                            (cvraw[:, nb.par].rearrange("p (h d) -> p h d", h=H), vh[0:NC, nb.par, 0, :, 0:D],
                             vl[0:NC, nb.par, 0], s_cv, s_vh))
                        pool.wait_ge(loaded[nb.par], 16 * (nb.half + 1))
                        settle(pool, pool_waits_over)
                        pool.tensor_copy(high, src).then_inc(made, 1)
                        pool.wait_ge(made, nb.n + 1)
                        pool.tensor_tensor(low_, src, high, ALU.subtract).then_inc(ctx_split, 1)
                    if post and h == 5:
                        pool.wait_ge(ve2_ready, lb.n + 1)
                        pool.tensor_tensor(rs2[:], ve2[:], mhalf[:], ALU.pow).then_inc(rs2_ready, 1)
                    if post and h >= 12:
                        c, t = (h - 12) // 2, h % 2
                        pool.wait_ge(idx_ready, lb.n + 1)
                        settle(pool, pool_waits_over)
                        pool.indirect_dma_start(out=slots[:], out_offset=bass.IndirectOffsetOnAxis(ap=idx[:, lb.par, c, t:t + 1], axis=0),
                                                in_=row[:, lb.par, t], in_offset=None).then_inc(s_scat[lb.par], 16)

            batches(pool, body)

            pool.wait_ge(s_padi, 2)
            for e in range(E):
                for s in (0, 1):
                    pool.indirect_dma_start(out=slots[:], out_offset=bass.IndirectOffsetOnAxis(ap=padi[:, s, e:e + 1], axis=0),
                                            in_=padrow[:, s], in_offset=None).then_inc(s_pads, 16)
            pool.wait_ge(s_dummy, 32)
            for par in (0, 1):
                pool.wait_ge(s_xst[par], 16 * B // 2)

            def add_tile(t):
                pool.wait_ge(y_out, t.n + 1)
                wait(pool, s_add, 32 * t.n)
                settle(pool, pool_waits_over)
                for s in (0, 1):
                    pool.indirect_dma_start(out=out[:], out_offset=bass.IndirectOffsetOnAxis(ap=toki[:, t.par, s:s + 1], axis=0),
                                            in_=y[:, t.par, s], in_offset=None, compute_op=ALU.add).then_inc(s_add, 16)

            for n in range(3):
                add_tile(at(n))
            with pool.Fori(1, (NT - 1) // 2) as i:
                for j in (1, 2):
                    add_tile(At(2 * i + j, i + j // 2, j % 2))

        @block.scalar
        def _(act):
            act.wait_ge(s_const, 96)
            act.activation(tgx[:], tgx[:], ACT.Tanh).then_inc(s_tanh, 1)
            act.activation(tgf[:], tgf[:], ACT.Tanh).then_inc(s_tanh, 1)

            def ctx_out(b, h):
                g = b.n * H + h
                act.wait_ge(turned, g + 1)
                wait(act, pv_done, g - 1)
                act.copy(ptc[:, h % 2].rearrange("p s t q -> p (s t q)"), ptc_ps[0:NC].bitcast(U16)[:, 0:512]).then_inc(ptc_out, 1)

            def body(b, heads, post, pre):
                nb, lb = b.next(), b.prev()
                for h in range(H):
                    if bh := head_at(b, h, 2, heads, post, pre):
                        ctx_out(*bh)
                    if heads:
                        g = b.n * H + h
                        act.wait_ge(maxed, g + 1)
                        wait(act, turned, g - 1)
                        for t in (0, 1):
                            last = act.activation(p[:, h % 2, t], bank[h % 2][:, t, 0:NK], ACT.Exp,
                                                  bias=negmax[:, h % 2, t:t + 1])
                        last.then_inc(expd, 1)
                    for slot, kind, k in USES:
                        if slot != h or not (post if kind == "post" else pre):
                            continue
                        if kind == "post" and k in (0, 2):
                            act.wait_ge(filled, post_use(lb, k) + 1)
                        if kind == "post" and k == 0:
                            act.copy(oTh[:].rearrange("p k t -> p (k t)"), misc[:]).then_inc(ot_hi, 1)
                        if kind == "post" and k == 2:
                            act.copy(xn2T[:].rearrange("p k t -> p (k t)"), misc[:]).then_inc(emptied, 1)
                        if kind == "post" and k == 3:
                            act.wait_ge(lg_ready, lb.n + 1)
                            act.activation(ex[:], lg[:], ACT.Exp).then_inc(ex_ready, 1)
                        if kind == "pre":
                            act.wait_ge(filled, pre_use(nb, k) + 1)
                            if k == 1:
                                wait(act, q_saved, 32 * nb.n)
                            if k == 2:
                                wait(act, k_saved, 32 * nb.n)
                            dst, src = (
                                (xTh[:].rearrange("p k t -> p (k t)"), misc[:]) if k == 0 else
                                (qs[:, 0].rearrange("p c t -> p (c t)"), misc[:]) if k == 1 else
                                (ks[:, 0, :, NC:NK], misc[:].rearrange("p (c t) -> p c t", c=2)) if k == 2 else
                                (vh[:, nb.par, 1:3, :, 0:D], misc[:].rearrange("p (t h d) -> p t h d", t=2, h=H)))
                            act.copy(dst, src).then_inc(pre_hi, 1)
                    if heads and h in W_SLOTS:
                        n = W_SLOTS.index(h)
                        if n == 0:
                            act.wait_ge(s_w[b.par], 48 * (b.half + 1))
                            wait(act, s_wst[b.par], 16 * b.half)
                        act.mul(wout[:, b.par, n], wst[:, b.par, n], WS).then_inc(w_high, 1)

            batches(act, body)

            def turned_high(t):
                act.wait_ge(et_filled, t.n + 1)
                act.copy(eTh[:, t.par].rearrange("p k t -> p (k t)"), misc[:]).then_inc(et_hi, 1)

            def high(t, c):
                u = t.n * 8 + c
                act.wait_ge(mult_done, u + 1)
                act.copy(hh[:, c % 4], h32[:, c % 2]).then_inc(hhi_done, 1)

            def tile(t):
                first = isinstance(t.n, int) and t.n < 0
                last = isinstance(t.n, int) and t.n == NT
                if first:
                    return turned_high(t.next())
                for c in range(8):
                    if not last:
                        u = t.n * 8 + c
                        act.wait_ge(gu_filled, u + 1)
                        wait(act, mult_done, u - 1)
                        act.activation(sg[:, c % 2], bank[c % 4 // 2][:, c % 2, 0:TS], ACT.Silu, scale=1.0 / WS).then_inc(silu_done, 1)
                    if c == 0 and not (isinstance(t.n, int) and t.n == 0):
                        high(t.prev(), 7)
                    if c and not last:
                        high(t, c - 1)
                    if c == 4 and not last:
                        turned_high(t.next())

            tiles(act, tile)

        @block.tensor
        def _(pe):
            def mm(out_, l, r, start, stop, **kw):
                return pe.matmul(out_, l, r, start=start, stop=stop, **kw)

            def three(dst, lh, ll, rh, rl):
                for n, (l, r) in enumerate(((lh, rh), (ll, rh), (lh, rl))):
                    for k in (0, 1):
                        last = mm(dst, l(k), r(k), n == 0 and k == 0, n == 2 and k == 1)
                return last

            def turn(src, width=128):
                for k in (0, 1):
                    for t in (0, 1):
                        last = pe.transpose(misc[:, k * 256 + t * 128:k * 256 + t * 128 + 128],
                                            src(t, k), ident[:])
                return last

            def scores(b, h):
                g = b.n * H + h
                wait(pe, expd, g - 1)
                c, pair, rows = h // 8, h % 8 // 2, slice(64 * (h % 2), 64 * (h % 2) + 64)
                for t in (0, 1):
                    last = mm(bank[h % 2][:, t, 0:NK], qst[rows, b.par, pair, c, t * 128:t * 128 + 128],
                              kst[rows, b.par, pair, c], True, True)
                last.then_inc(scored, 1)

            def turn_probs(b, h):
                g = b.n * H + h
                pe.wait_ge(plow, g + 1)
                wait(pe, ptx_out, g)
                wait(pe, ptc_out, g)
                for s, (src, i_, dt) in enumerate(((p_high, ident_b, BF16), (pl[:], ident_h, F16))):
                    cdst, xdst = ptc_ps[0:NC].bitcast(dt), ptx_ps[:].bitcast(dt)
                    for t in (0, 1):
                        pe.transpose(cdst[:, (s * 2 + t) * 128:(s * 2 + t) * 128 + 128], src[:, h % 2, t, 0:NC], i_[:])
                        for k in (0, 1):
                            at_ = ((s * 2 + k) * 2 + t) * 128
                            last = pe.transpose(xdst[:, at_:at_ + 128], src[:, h % 2, t, NC + k * 128:NC + k * 128 + 128], i_[:])
                last.then_inc(turned, 1)

            def values(b, h):
                g = b.n * H + h
                pe.wait_ge(ptx_out, g + 1)
                pe.wait_ge(ptc_out, g + 1)
                if h % 8 == 0:
                    wait(pe, o_out, 2 * b.n + h // 8)
                if h == 0:
                    pe.wait_ge(emptied, pre_use(b, 3) + 1)
                par = h % 2
                for t in (0, 1):
                    at_ = ((h % 8) * 2 + t) * 17
                    whole, plain = o_ps[:, at_:at_ + 17], o_ps[:, at_:at_ + 16]
                    for k in range(3):
                        n = NC if k == 0 else 128
                        hi, lo = ((ptc[:, par, s, t] if k == 0 else ptx[:, par, s, k - 1, t]).bitcast(dt)
                                  for s, dt in ((0, BF16), (1, F16)))
                        mm(whole, hi, vh[0:n, b.par, k, h], k == 0, False)
                        mm(plain, hi, vl[0:n, b.par, k, h], False, False)
                        last = mm(whole, lo, vh[0:n, b.par, k, h], False, k == 2)
                last.then_inc(pv_done, 1)

            def pre_step(b, k):
                wait(pe, emptied, pre_use(b, k))
                if k == 0:
                    pe.wait_ge(xn_ready, b.n + 1)
                    last = turn(lambda t, c: xn[:, t, c * 128:c * 128 + 128])
                elif k < 3:
                    w = wq if k == 1 else wk
                    for c in (0, 1):
                        last = three(misc[:, c * 256:c * 256 + 256],
                                     lambda kk: w[:, 0, kk, c * 128:c * 128 + 128],
                                     lambda kk: w[:, 1, kk, c * 128:c * 128 + 128],
                                     lambda kk: xTh[:, kk, :], lambda kk: xTl[:, kk, :])
                else:
                    for t in (0, 1):
                        last = three(misc[:, t * 256:t * 256 + 256],
                                     lambda kk: xTh[:, kk, t * 128:t * 128 + 128],
                                     lambda kk: xTl[:, kk, t * 128:t * 128 + 128],
                                     lambda kk: wv[:, 0, kk, :], lambda kk: wv[:, 1, kk, :])
                last.then_inc(filled, 1)

            def post_step(b, k):
                wait(pe, emptied, post_use(b, k))
                if k == 0:
                    pe.wait_ge(o_out, 2 * b.n + 2)
                    last = turn(lambda t, c: o[:, t, c * 128:c * 128 + 128])
                elif k == 1:
                    for t in (0, 1):
                        dst = misc[:, t * 256:t * 256 + 256]
                        for n, (l, s) in enumerate(((oTh, 0), (oTl, 0), (oTh, 1))):
                            for c in (0, 1):
                                mm(dst, l[:, c, t * 128:t * 128 + 128], wp[:, s, c, :], n == 0 and c == 0, False)
                        mm(dst, ones16[0:1, :], bp[:, 0, :], False, False)
                        last = mm(dst, ones16[0:1, :], bp[:, 1, :], False, True)
                elif k == 2:
                    pe.wait_ge(row_ready, b.n + 1)
                    last = turn(lambda t, c: row[:, b.par, t, c * 128:c * 128 + 128])
                elif k == 3:
                    for t in (0, 1):
                        for c in (0, 1):
                            last = mm(misc[:, t * 8:t * 8 + 8], xn2T[:, c, t * 128:t * 128 + 128], rout[:, c, :], c == 0, c == 1)
                else:
                    pe.wait_ge(sel_ready, b.n + 1)
                    mm(misc[:, 0:8], tri[:], sel[:, 0], True, False)
                    mm(misc[:, 0:8], ones16[:], seen[:], False, True)
                    mm(misc[:, 8:16], tri[:], sel[:, 1], True, False)
                    mm(misc[:, 8:16], ones16[:], seen[:], False, False)
                    last = mm(misc[:, 8:16], ones16[:], sel[:, 0], False, True)
                last.then_inc(filled, 1)

            pe.wait_ge(s_made, 1)
            pe.wait_ge(s_pmade, 2)

            def body(b, heads, post, pre):
                nb, lb = b.next(), b.prev()
                for h in range(H):
                    if bh := head_at(b, h, -1, heads, post, pre):
                        if h + 1 == H:
                            pe.wait_ge(q_stacked[nb.par], 16 * (nb.half + 1))
                            pe.wait_ge(k_stacked[nb.par], 16 * (nb.half + 1))
                            pe.wait_ge(ctx_split, 2 * (nb.n + 1))
                        scores(*bh)
                    for slot, kind, k in USES:
                        if slot == h and kind == "post" and post:
                            post_step(lb, k)
                        if slot == h and kind == "pre" and pre:
                            pre_step(nb, k)
                    if bh := head_at(b, h, 3, heads, post, False):
                        values(*bh)
                    if bh := head_at(b, h, 1, heads, post, False):
                        turn_probs(*bh)

            batches(pe, body)

            pe.wait_ge(s_cnt_in, 1)
            mm(misc[:, 0:8], ones16[:], seen[:], True, True).then_inc(s_cnt, 1)
            pe.wait_ge(idx_ready, B)
            for i in range(4):
                last = pe.transpose(o_ps[:, i * 128:i * 128 + 128], gall[:, i * 16:i * 16 + 16, :].rearrange("p t e -> p (t e)"), ident[:])
            last.then_inc(s_gt, 1)

            def summed(n):
                pe.wait_ge(s_cnt_in, n + 2)
                mm(ptx_ps[:, 0:1], same_expert[:], count[:], True, True).then_inc(s_count, 1)
            with pe.Fori(0, 30) as i:
                summed(i)
            summed(30)
            with pe.Fori(0, 14) as i:
                summed(i + 31)
            pe.wait_ge(s_limin, 1)
            mm(ptx_ps[:, 8:24], ones32[0:8, :], diag[:].rearrange("p a e -> p (a e)"), True, True).then_inc(s_lim, 1)

            def turn_tile(t):
                pe.wait_ge(s_xe[t.par], 16 * (t.half + 1))
                wait(pe, et_lo, t.n)
                turn(lambda s, c: xe[:, t.par, s, c * 128:c * 128 + 128]).then_inc(et_filled, 1)

            def weights(t, part, low, c, k=0):
                off = (low * 3 + part) * 512
                if part < 2:
                    off += k * 256 + (c % 2) * 128
                    return wb[:, t.par, c // 2, off:off + 128]
                off += (c % 2) * 256
                return wb[:, t.par, c // 2, off:off + 256]

            def gate_up(t, c):
                u = t.n * 8 + c
                wait(pe, mult_done, u - 3)
                for part in (0, 1):
                    last = three(bank[c % 4 // 2][:, c % 2, part * TS:part * TS + TS],
                                 lambda k: weights(t, part, 0, c, k), lambda k: weights(t, part, 1, c, k),
                                 lambda k: eTh[:, t.par, k, :], lambda k: eTl[:, t.par, k, :])
                last.then_inc(gu_filled, 1)

            y_ps = (ptc_ps, o_ps)

            def down(t, c):
                u = t.n * 8 + c
                pe.wait_ge(hhi_done, u + 1)
                pe.wait_ge(hlo_done, u + 1)
                if c == 0:
                    wait(pe, y_out, t.n - 1)
                for s in (0, 1):
                    rows = slice(s * 128, s * 128 + 128)
                    dst = y_ps[t.par][:, s * 256:s * 256 + 256]
                    mm(dst, hh[:, c % 4, rows], weights(t, 2, 0, c), c == 0 and s == 0, False, skip_group_check=True)
                    mm(dst, hl[:, c % 4, rows], weights(t, 2, 0, c), False, False, skip_group_check=True)
                    last = mm(dst, hh[:, c % 4, rows], weights(t, 2, 1, c), False, c == 7, skip_group_check=True)
                if c == 7:
                    last.then_inc(y_filled, 1)

            def tile(t):
                first = isinstance(t.n, int) and t.n < 0
                last = isinstance(t.n, int) and t.n == NT
                zero = isinstance(t.n, int) and t.n == 0
                if first:
                    pe.wait_ge(s_limits_ok, 1)
                    return turn_tile(t.next())
                for c in range(8):
                    if not last:
                        if c == 0:
                            pe.wait_ge(et_lo, t.n + 1)
                            pe.wait_ge(s_wl[t.par], 16 * (t.half + 1))
                        gate_up(t, c)
                    if c < 2 and not zero:
                        down(t.prev(), c + 6)
                    if c >= 2 and not last:
                        down(t, c - 2)
                    if c == 4 and not last:
                        turn_tile(t.next())

            tiles(pe, tile)

        @block.vector
        def _(dve):
            link = Chain(dve, s_dve)
            bc = lambda a, n, shape: a.unsqueeze(n).to_broadcast(shape)
            dve.wait_ge(s_pmade, 2)
            link(dve.tensor_copy(ident_b[:], ident[:]))
            link(dve.tensor_copy(ident_h[:], ident[:]))
            for s in (0, 1):
                link(dve.tensor_scalar(slot_num[:, s:s + 1], iscr[:, 0:1], float(128 * s), None, ALU.add))
            link(dve.tensor_copy(tok_of[:], slot_num[:]))
            link(dve.tensor_scalar(iscr[:, 11:12], iscr[:, 0:1], 3, None, ALU.logical_shift_right))
            link(dve.tensor_copy(candf[:], iscr[:, 11:12]))
            link(dve.tensor_scalar(candf[:], candf[:], 128.0, None, ALU.mult))
            link(dve.tensor_copy(tokT[:], tokTi[:]))
            link(dve.tensor_scalar(tokT[:], tokT[:], candf[:, 0:1], None, ALU.add))
            link(dve.tensor_copy(iota8[:], iscr[:, 1:9]))
            link(dve.tensor_copy(tnum[:], iscr[:, 16:16 + NT + 1]))
            link(dve.tensor_scalar(iscr[:, 256:384], iscr[:, 128:256], 7, None, ALU.bitwise_and))
            link(dve.tensor_scalar(same_expert[:], iscr[:, 256:384], 0.0, None, ALU.is_equal))
            link(dve.tensor_scalar(region_at[:], iota8[:], float(REGION), None, ALU.mult))
            dve.tensor_scalar(padrow[:, :, C], slot_num[:], float(T), None, ALU.add).then_inc(s_padrow, 1)
            dve.wait_ge(s_const, 96)
            link(dve.tensor_scalar(wraw[:, :, 0:256], wraw[:, :, 0:256], D ** -0.5, None, ALU.mult))
            for w, src in ((wq, wraw[:, :, 0:256]), (wk, wraw[:, :, 256:512]), (wv, wraw[:, :, 512:768]), (wp, praw[:])):
                link(dve.tensor_copy(w[:, 0], src))
                link(dve.tensor_tensor(w[:, 1], src, w[:, 0], ALU.subtract))
            link(dve.tensor_copy(bp[:, 0], braw[:]))
            dve.tensor_tensor(bp[:, 1], braw[:], bp[:, 0], ALU.subtract).then_inc(s_made, 1)
            dve.wait_ge(s_tanh, 2)
            link(dve.tensor_scalar(bitf[:], tgf[:], 1.0 / (WS * WS), None, ALU.mult))
            link(dve.tensor_copy(tgf[:], bitf[:]))

            def norm_stats(src, mv, ve, ready):
                for t in (0, 1):
                    link(dve.bn_stats(stats[:, t], src[:, t]))
                    settle(dve, dve_waits_over)
                for t in (0, 1):
                    link(dve.bn_aggr(mv[:, t], stats[:, t]))
                    settle(dve, dve_waits_over)
                dve.tensor_scalar(ve[:], mv[:, :, 1], EPS, None, ALU.add).then_inc(ready, 1)

            def ptx_evac(b, h):
                g = b.n * H + h
                dve.wait_ge(turned, g + 1)
                wait(dve, pv_done, g - 1)
                dve.tensor_copy(ptx[:, h % 2].rearrange("p s k t q -> p (s k t q)"), ptx_ps[:].bitcast(U16)).then_inc(ptx_out, 1)

            def row_max(b, h):
                g = b.n * H + h
                dve.wait_ge(scored, g + 1)
                wait(dve, expd, g - 1)
                dve.tensor_reduce(negmax[:, h % 2], bank[h % 2][:, :, 0:NK], AX, ALU.max, negate=True).then_inc(maxed, 1)

            def o_evac(b, g):
                dve.wait_ge(pv_done, b.n * H + 8 * g + 8)
                src = o_ps[:, 0:272].rearrange("p (u d) -> p u d", d=17)
                link(dve.reciprocal(rden[:].unsqueeze(2), src[:, :, 16:17]))
                dst = o[:].rearrange("p t (h d) -> p h t d", h=H)[:, 8 * g:8 * g + 8]
                dve.tensor_tensor(dst, src[:, :, 0:16].rearrange("p (h t) d -> p h t d", t=2),
                                  bc(rden[:].rearrange("p (h t) -> p h t", t=2), 3, [128, 8, 2, 16]), ALU.mult).then_inc(o_out, 1)

            def low(b, k):
                dve.wait_ge(pre_hi, b.n * PRE + k + 1)
                pair = misc[:].rearrange("p (c t) -> p c t", c=2)
                lo, src, hi = (
                    (xTl[:], pair, xTh[:]) if k == 0 else
                    (qs[:, 1], pair, qs[:, 0]) if k == 1 else
                    (ks[:, 1, :, NC:NK], pair, ks[:, 0, :, NC:NK]) if k == 2 else
                    (vl[:, b.par, 1:3], misc[:].rearrange("p (t h d) -> p t h d", t=2, h=H), vh[:, b.par, 1:3, :, 0:D]))
                dve.tensor_tensor(lo, src, hi, ALU.subtract).then_inc(emptied, 1)

            def route(b):
                par = b.par
                dve.wait_ge(ex_ready, b.n + 1)
                link(dve.tensor_reduce(esum[:], ex[:], AX, ALU.add))
                link(dve.reciprocal(esum[:], esum[:]))
                link(dve.tensor_tensor(pr[:], ex[:], bc(esum[:], 2, [128, 2, 8]), ALU.mult))
                mine, other = bc(pr[:], 3, [128, 2, 8, 8]), bc(pr[:], 2, [128, 2, 8, 8])
                dve.tensor_tensor(gt[:], other, mine, ALU.is_gt)
                link(dve.tensor_tensor(eq[:], other, mine, ALU.is_equal))
                link(dve.tensor_tensor(eq[:], eq[:], bc(before[:], 1, [128, 2, 8, 8]), ALU.mult))
                link(dve.tensor_tensor(gt[:], gt[:], eq[:], ALU.add))
                link(dve.tensor_reduce(rank[:], gt[:], AX, ALU.add))
                for c in (0, 1):
                    dve.tensor_scalar(oh[:, c], rank[:], float(c), None, ALU.is_equal)
                link(dve.tensor_scalar(sel[:], rank[:], 1.0, None, ALU.is_le))
                dve.tensor_tensor(ohp[:, 0], oh[:, 0], pr[:], ALU.mult).then_inc(sel_ready, 1)
                link(dve.tensor_tensor(ohp[:, 1], oh[:, 1], pr[:], ALU.mult))

            def gates_of(b):
                par = b.par
                link(dve.tensor_reduce(pg[:], ohp[:], AX, ALU.add))
                link(dve.tensor_tensor(den[:], pg[:, 0], pg[:, 1], ALU.add))
                link(dve.tensor_scalar(den[:], den[:], 1e-9, None, ALU.add))
                link(dve.reciprocal(den[:], den[:]))
                link(dve.tensor_tensor(gsel[:], pg[:], bc(den[:], 1, [128, 2, 2]), ALU.mult))
                dve.tensor_copy(row[:, par, :, C + 1:C + 3].rearrange("p t c -> p c t"), gsel[:])
                link(dve.tensor_tensor(ohp[:, 0], ohp[:, 0], ohp[:, 1], ALU.add))
                link(dve.tensor_tensor(gall[:, bass.ds(2 * b.n, 2)], ohp[:, 0], bc(den[:], 2, [128, 2, 8]), ALU.mult))
                link(dve.tensor_tensor(ohp[:, 1], oh[:, 0], bc(iota8[:], 1, [128, 2, 8]), ALU.mult))
                link(dve.tensor_reduce(row[:, par, :, C + 3:C + 4].rearrange("p t a -> p (t a)"), ohp[:, 1], AX, ALU.add))
                link(dve.tensor_copy(row[:, par, :, C], tok_of[:]))
                dve.tensor_copy(idx[:, b.par], idxf[:]).then_inc(idx_ready, 1)
                link(dve.tensor_scalar(tok_of[:], tok_of[:], float(N), None, ALU.add))

            def place(b):
                dve.wait_ge(filled, post_use(b, 4) + 1)
                link(dve.tensor_tensor(pos[:], misc[:, 0:16].rearrange("p (t e) -> p t e", t=2), bc(region_at[:], 1, [128, 2, 8]), ALU.add))
                link(dve.tensor_tensor(seen[:], seen[:], sel[:, 0], ALU.add))
                link(dve.tensor_tensor(seen[:], seen[:], sel[:, 1], ALU.add))
                for c in (0, 1):
                    link(dve.tensor_tensor(ohq[:, c], oh[:, c], pos[:], ALU.mult))
                link(dve.tensor_reduce(idxf[:], ohq[:], AX, ALU.add))

            def body(b, heads, post, pre):
                nb, lb = b.next(), b.prev()
                for h in range(H):
                    if post and h == 3:
                        o_evac(lb, 1)
                    if heads and h == 11:
                        o_evac(b, 0)
                    if bh := head_at(b, h, 2, heads, post, False):
                        ptx_evac(*bh)
                    if bh := head_at(b, h, -1, heads, False, pre):
                        row_max(*bh)
                    if pre and h == 0:
                        dve.wait_ge(s_x[nb.par], 16 * (nb.half + 1))
                        norm_stats(xb[:, nb.par], mv1, ve1, ve1_ready)
                    if pre and h == 2:
                        dve.wait_ge(rs1_ready, nb.n + 1)
                        for t in (0, 1):
                            last = dve.tensor_scalar(xn[:, t], xb[:, nb.par, t], mv1[:, t, 0:1], rs1[:, t:t + 1], ALU.subtract, ALU.mult)
                        last.then_inc(xn_ready, 1)
                    if post and h == 6:
                        dve.wait_ge(rs2_ready, lb.n + 1)
                        wait(dve, s_scat[lb.par], 64 * lb.half)
                        for t in (0, 1):
                            last = dve.tensor_scalar(row[:, lb.par, t, 0:C], xr[:, lb.par, t], mv2[:, t, 0:1], rs2[:, t:t + 1], ALU.subtract, ALU.mult)
                        last.then_inc(row_ready, 1)
                    if post and h == 9:
                        route(lb)
                    if post and h == 11:
                        gates_of(lb)
                    for slot, kind, k in USES:
                        if slot != h or not (post if kind == "post" else pre):
                            continue
                        if kind == "pre":
                            low(nb, k)
                        elif k == 0:
                            dve.wait_ge(ot_hi, lb.n + 1)
                            dve.tensor_tensor(oTl[:].rearrange("p k t -> p (k t)"), misc[:], oTh[:].rearrange("p k t -> p (k t)"),
                                              ALU.subtract).then_inc(emptied, 1)
                        elif k == 1:
                            dve.wait_ge(filled, post_use(lb, 1) + 1)
                            dve.wait_ge(s_xr[lb.par], 16 * (lb.half + 1))
                            xrow = xr[:, lb.par].rearrange("p t c -> p (t c)")
                            dve.scalar_tensor_tensor(xrow, misc[:], tgx[:, 0:1], xrow, ALU.mult, ALU.add).then_inc(x1_ready, 1)
                            dve.wait_ge(x1_ready, lb.n + 1)
                            dve.sem_inc(emptied, 1)
                            norm_stats(xr[:, lb.par], mv2, ve2, ve2_ready)
                        elif k == 3:
                            dve.wait_ge(filled, post_use(lb, 3) + 1)
                            mlg = misc[:, 0:16].rearrange("p (t e) -> p t e", t=2)
                            link(dve.tensor_reduce(lmax[:], mlg, AX, ALU.max))
                            dve.tensor_tensor(lg[:], mlg, bc(lmax[:], 2, [128, 2, 8]), ALU.subtract).then_inc(lg_ready, 1)
                            dve.wait_ge(lg_ready, lb.n + 1)
                            dve.sem_inc(emptied, 1)
                        elif k == 4:
                            place(lb)
                            dve.sem_inc(emptied, 1)
                    if heads and h in W_SLOTS:
                        n = W_SLOTS.index(h)
                        dve.wait_ge(w_high, 3 * b.n + n + 1)
                        dve.scalar_tensor_tensor(wout[:, b.par, 3 + n], wst[:, b.par, n], WS, wout[:, b.par, n],
                                                 ALU.mult, ALU.subtract).then_inc(w_split, 1)

            link.per = 37
            batches(dve, body, link)
            link.rest()

            dve.sem_inc(s_cnt_in, 1)
            dve.wait_ge(s_cnt, 1)
            link(dve.tensor_copy(cnt[:], misc[:, 0:8]))
            for s in (0, 1):
                link(dve.tensor_tensor(padf[:, s], cnt[:], region_at[:], ALU.add))
                link(dve.tensor_scalar(padf[:, s], padf[:, s], slot_num[:, s:s + 1], None, ALU.add))
                dve.tensor_copy(padi[:, s], padf[:, s]).then_inc(s_padi, 1)
            link(dve.tensor_scalar(nti[:], cnt[:], float(TS - 1), None, ALU.add))
            link(dve.tensor_scalar(nti[:], nti[:], TS.bit_length() - 1, None, ALU.logical_shift_right))
            link(dve.tensor_copy(ntf[:], nti[:]))
            link(dve.tensor_tensor_scan(tend[:], ones32[:, 0:8], ntf[:], 0.0, ALU.mult, ALU.add))
            shape = [128, NT + 1, 8]
            link(dve.tensor_tensor(tcmp[:], bc(tnum[:], 2, shape), bc(tend[:], 1, shape), ALU.is_ge))
            link(dve.tensor_tensor(tcmp2[:], tcmp[:], bc(ntf[:], 1, shape), ALU.mult))
            link(dve.tensor_reduce(texp[:], tcmp[:], AX, ALU.add))
            link(dve.tensor_reduce(tbase[:], tcmp2[:], AX, ALU.add))
            link(dve.tensor_tensor(tbase[:], tnum[:], tbase[:], ALU.subtract))
            link(dve.tensor_scalar(tbase[:], tbase[:], float(TS), None, ALU.mult))
            link(dve.tensor_scalar(tscr[:], texp[:], float(REGION), None, ALU.mult))
            link(dve.tensor_tensor(tbase[:], tbase[:], tscr[:], ALU.add))
            link(dve.tensor_scalar(tabs[:, 1], tbase[:], float(E * REGION), None, ALU.min))
            link(dve.tensor_scalar(tscr[:], texp[:], float(E - 1), None, ALU.min))
            link(dve.tensor_copy(tabs[:, 0], tscr[:]))
            link(dve.memset(tabs[:, 2, 0:2], 1))
            dve.tensor_tensor(tabs[:, 2, 2:], tscr[:, 2:], tscr[:, :NT - 1], ALU.not_equal).then_inc(s_tabs, 1)

            dve.wait_ge(s_gt, 1)
            link(dve.tensor_copy(gT[:], o_ps[:]))
            link(dve.memset(thr[:], 0))
            link(dve.memset(bit[:], 1 << 29))
            link(dve.memset(cut[:], 0.0))
            link(dve.memset(stepf[:], float(1 << 13)))
            link.rest()
            start = link.base
            with dve.Fori(0, 30) as i:
                link.base, link.n = start + i * 5, 0
                link(dve.tensor_tensor(cand[:], thr[:], bit[:], ALU.bitwise_or))
                dve.tensor_scalar(gcmp[:], gT[:], cand[:, 0:1].bitcast(F32), 0.0, ALU.is_ge, ALU.add, accum_out=count[:]).then_inc(s_cnt_in, 1)
                dve.wait_ge(s_count, i + 1)
                link(dve.tensor_scalar(keep_i[:], ptx_ps[:, 0:1], float(CAP), -1.0, ALU.is_ge, ALU.mult))
                link(dve.tensor_tensor(keep_i[:], keep_i[:], bit[:], ALU.bitwise_and))
                link(dve.tensor_tensor(thr[:], thr[:], keep_i[:], ALU.bitwise_or))
                link(dve.tensor_scalar(bit[:], bit[:], 1, None, ALU.logical_shift_right))
                assert link.n == 5
            link.base, link.n = start + 150, 0
            thrf = thr[:, 0:1].bitcast(F32)
            dve.tensor_scalar(gcmp[:], gT[:], thrf, 0.0, ALU.is_gt, ALU.add, accum_out=count[:]).then_inc(s_cnt_in, 1)
            dve.wait_ge(s_count, 31)
            link(dve.tensor_scalar(need[:], ptx_ps[:, 0:1], -1.0, float(CAP), ALU.mult, ALU.add))
            link(dve.tensor_scalar(gcmp[:], gT[:], thrf, float(4 * T), ALU.not_equal, ALU.mult))
            link(dve.tensor_tensor(tokT[:], tokT[:], gcmp[:], ALU.add))
            link.rest()
            start = link.base
            with dve.Fori(0, 14) as i:
                link.base, link.n = start + i * 4, 0
                link(dve.tensor_tensor(candf[:], cut[:], stepf[:], ALU.add))
                dve.tensor_scalar(gcmp[:], tokT[:], candf[:, 0:1], 0.0, ALU.is_lt, ALU.add, accum_out=count[:]).then_inc(s_cnt_in, 1)
                dve.wait_ge(s_count, i + 32)
                link(dve.tensor_scalar(candf[:], ptx_ps[:, 0:1], need[:, 0:1], stepf[:, 0:1], ALU.is_le, ALU.mult))
                link(dve.tensor_tensor(cut[:], cut[:], candf[:], ALU.add))
                link(dve.tensor_scalar(stepf[:], stepf[:], 0.5, None, ALU.mult))
                assert link.n == 4
            link.base, link.n = start + 56, 0
            dve.tensor_scalar(diag[:, 0], ident[0:8, 0:8], thr[0:8, 0:1].bitcast(F32), None, ALU.mult)
            dve.tensor_scalar(diag[:, 1], ident[0:8, 0:8], cut[0:8, 0:1], None, ALU.mult).then_inc(s_limin, 1)
            dve.wait_ge(s_lim, 1)
            link(dve.tensor_copy(lim[:].rearrange("p a e -> p (a e)"), ptx_ps[:, 8:24]))
            link(dve.tensor_tensor(tcmp[:], bc(texp[:], 2, shape), bc(iota8[:], 1, shape), ALU.is_equal))
            for a, dst in ((0, thr_t), (1, cut_t)):
                link(dve.tensor_tensor(tcmp2[:], tcmp[:], bc(lim[:, a], 1, shape), ALU.mult))
                link(dve.tensor_reduce(dst[:], tcmp2[:], AX, ALU.add))
            dve.sem_inc(s_limits_ok, 1)
            link.rest()

            def turned_low(t):
                dve.wait_ge(et_hi, t.n + 1)
                dve.tensor_tensor(eTl[:, t.par].rearrange("p k t -> p (k t)"), misc[:], eTh[:, t.par].rearrange("p k t -> p (k t)"),
                                  ALU.subtract).then_inc(et_lo, 1)

            def low_h(t, c):
                dve.wait_ge(hhi_done, t.n * 8 + c + 1)
                dve.tensor_tensor(hl[:, c % 4], h32[:, c % 2], hh[:, c % 4], ALU.subtract).then_inc(hlo_done, 1)

            def y_evac(t):
                dve.wait_ge(y_filled, t.n + 1)
                for s in (0, 1):
                    last = dve.tensor_scalar(y[:, t.par, s], y_ps[t.par][:, s * 256:s * 256 + 256], gf[:, t.par, s:s + 1], None, ALU.mult)
                last.then_inc(y_out, 1)

            y_ps = (ptc_ps, o_ps)

            def gates(t):
                par = t.par
                e_t, th, ct = (a[:, bass.ds(t.n, 1)] for a in (texp, thr_t, cut_t))
                tok, g0, g1, e0 = (xe[:, par, :, C + k] for k in range(4))
                wait(dve, s_add, 32 * (t.n - 1))
                link(dve.tensor_scalar(ga[:], e0, e_t, None, ALU.is_equal))
                dve.tensor_scalar(gb[:], e0, e_t, None, ALU.not_equal)
                link(dve.tensor_tensor(ga[:], ga[:], g0, ALU.mult))
                link(dve.tensor_tensor(gb[:], gb[:], g1, ALU.mult))
                link(dve.tensor_tensor(gg[:], ga[:], gb[:], ALU.add))
                dve.tensor_copy(toki[:, par], tok)
                link(dve.tensor_scalar(ga[:], gg[:], th, None, ALU.is_gt))
                dve.tensor_scalar(gb[:], gg[:], th, None, ALU.is_equal)
                link(dve.tensor_scalar(gk[:], tok, ct, None, ALU.is_lt))
                link(dve.tensor_tensor(gb[:], gb[:], gk[:], ALU.mult))
                link(dve.tensor_tensor(ga[:], ga[:], gb[:], ALU.add))
                link(dve.tensor_tensor(ga[:], ga[:], gg[:], ALU.mult))
                dve.tensor_scalar(gf[:, par], ga[:], tgf[:, 0:1], None, ALU.mult).then_inc(gf_ready, 1)

            def tile(t):
                first = isinstance(t.n, int) and t.n < 0
                last = isinstance(t.n, int) and t.n == NT
                zero = isinstance(t.n, int) and t.n == 0
                if first:
                    return turned_low(t.next())
                for c in range(8):
                    if not last:
                        u = t.n * 8 + c
                        dve.wait_ge(silu_done, u + 1)
                        wait(dve, hlo_done, u - 1)
                        dve.tensor_tensor(h32[:, c % 2], sg[:, c % 2], bank[c % 4 // 2][:, c % 2, TS:2 * TS], ALU.mult).then_inc(mult_done, 1)
                    if c == 0 and not zero:
                        low_h(t.prev(), 7)
                    if c and not last:
                        low_h(t, c - 1)
                    if c == 2 and not zero:
                        y_evac(t.prev())
                    if c == 3 and not last:
                        gates(t)
                    if c == 4 and not last:
                        turned_low(t.next())

            link.per = 9
            tiles(dve, tile, link)


def kernel(x, ctx_2048, g_xattn, g_ffn, L0_xattn_w_qkv, L0_xattn_w_proj, L0_xattn_b_proj,
           L0_ffn_router_gate, L0_ffn_gate_w, L0_ffn_up_w, L0_ffn_down_w):
    import numpy as np
    import concourse.bacc as bacc
    from concourse.bass_utils import run_bass_kernel_spmd as run

    ctx = np.asarray(ctx_2048)
    kT = ctx[:, :, :C].reshape(B, NC, 2, 128).transpose(0, 3, 2, 1)
    arrays = {
        "x": np.asarray(x), "ctx_kT": kT, "ctx": ctx, "g_xattn": np.asarray(g_xattn), "g_ffn": np.asarray(g_ffn),
        "wqkvT": np.asarray(L0_xattn_w_qkv).T, "wprojT": np.asarray(L0_xattn_w_proj).T, "b_proj": np.asarray(L0_xattn_b_proj),
        "router_w": np.asarray(L0_ffn_router_gate), "gate_w": np.asarray(L0_ffn_gate_w), "up_w": np.asarray(L0_ffn_up_w),
        "down_w": np.asarray(L0_ffn_down_w),
    }
    arrays = {n: np.ascontiguousarray(a) for n, a in arrays.items()}
    nc = bacc.Bacc("TRN2", target_bir_lowering=False, num_devices=1)
    args = [nc.dram_tensor(n, a.shape, mybir.dt.from_np(a.dtype), kind="ExternalInput").ap() for n, a in arrays.items()]
    out = nc.dram_tensor("out", (T + TS, C), F32, kind="ExternalOutput").ap()
    flamingo_block(nc, *args, out)
    r = run(nc, [arrays], core_ids=[0])
    return r.results[0]["out"][:T].reshape(B, N, C)
```

```python
import concourse.bass as bass
from concourse import mybir
from contextlib import ExitStack

F32, F16, BF16, I32, U16 = mybir.dt.float32, mybir.dt.float16, mybir.dt.bfloat16, mybir.dt.int32, mybir.dt.uint16
ALU = mybir.AluOpType
ACT = mybir.ActivationFunctionType
AX = mybir.AxisListType.X

B, N, C, NC = 32, 256, 256, 77
H, D = 16, 16
NK = NC + N
T = B * N
E, I, K = 8, 1024, 2
CAP = int(1.25 * ((T * K + E - 1) // E))
TS = 256
REGION = T + TS
NT = T * K // TS + E - 1
HOLD = 6
BITS, CUTS = 30, 14
ROW = C + 4
WPIECE = 3 * I
WS = 64.0
EPS = 1e-5
USES = [(3, "pre", 0), (4, "pre", 1), (5, "post", 0), (6, "post", 1), (7, "pre", 2), (9, "post", 2),
        (10, "post", 3), (12, "pre", 3), (14, "post", 4)]
PRE = sum(u[1] == "pre" for u in USES)
TURN, COPY, VALUES = 2, 3, 4
S_SLOTS = (0, 3, 9, 13)
W_SLOTS = (0, 8, 10)


def uses_of(body):
    return [u for u in USES if (body >= 1 if u[1] == "post" else body < B - 1)]


def use(body, kind, k):
    if isinstance(body, int):
        before = sum(len(uses_of(b)) for b in range(-1, body))
        return before + [u[1:] for u in uses_of(body)].index((kind, k))
    return (body - 1) * len(USES) + len(uses_of(-1)) + len(uses_of(0)) + [u[1:] for u in USES].index((kind, k))


class At:
    def __init__(self, n, half, par):
        self.n, self.half, self.par = n, half, par

    def next(self):
        return At(self.n + 1, self.half + self.par, 1 - self.par)

    def prev(self):
        return At(self.n - 1, self.half - (1 - self.par), 1 - self.par)


def at(n):
    return At(n, n // 2, n % 2)


def settle(eng, waits_over):
    eng.sem_inc(waits_over, 1)


def wait(eng, sem, value):
    if isinstance(value, int) and value <= 0:
        return
    eng.wait_ge(sem, value)


def flamingo_block(nc, x, ctx_kT, ctx, g_xattn, g_ffn, wqkvT, wprojT, b_proj, router_w, gate_w, up_w, down_w, out):
    slots = nc.dram_tensor("slots", [E * REGION + TS, ROW], F32).ap()
    wsplit = nc.dram_tensor("wsplit", [E, 4, 128, WPIECE], F16).ap()
    q_turn = nc.dram_tensor("q_turn", [2, 8, D, 2, 2, 2 * N], F16).ap()
    k_turn = nc.dram_tensor("k_turn", [2, 8, D, 2, 2, 2 * NK], F16).ap()

    ctx_stack = ExitStack()
    with ctx_stack:
        def sb(name, shape, dt=F32):
            return ctx_stack.enter_context(nc.sbuf_tensor(name, shape, dt))

        def sem(name):
            return ctx_stack.enter_context(nc.semaphore(name))

        bank = [ctx_stack.enter_context(nc.psum_tensor(f"pair{i}", [128, 2, 512], F32)) for i in range(2)]
        ptx_ps = ctx_stack.enter_context(nc.psum_tensor("ptx_ps", [128, 512], F32))
        ptc_ps = ctx_stack.enter_context(nc.psum_tensor("ptc_ps", [128, 512], F32))
        o_ps = ctx_stack.enter_context(nc.psum_tensor("o_ps", [128, 512], F32))
        misc = ctx_stack.enter_context(nc.psum_tensor("misc", [128, 512], F32))

        ident = sb("ident", [128, 128])
        tri = sb("tri", [128, 128], F16)
        ones16 = sb("ones16", [128, 128], F16)
        ones32 = sb("ones32", [128, 128])
        same_expert = sb("same_expert", [128, 128])
        iscr = sb("iscr", [128, 512], I32)
        iota8 = sb("iota8", [128, 8])
        region_at = sb("region_at", [128, 8])
        before = sb("before", [128, 8, 8])
        slot_num = sb("slot_num", [128, 2])
        tok_of = sb("tok_of", [128, 2])
        tokTi = sb("tokTi", [128, 512], I32)
        mhalf = sb("mhalf", [128, 2])
        wraw = sb("wraw", [128, 2, 768])
        praw = sb("praw", [128, 2, 256])
        braw = sb("braw", [1, 256])
        rout = sb("rout", [128, 2, 8])
        wq = sb("wq", [128, 2, 2, 256], F16)
        wk = sb("wk", [128, 2, 2, 256], F16)
        wv = sb("wv", [128, 2, 2, 256], F16)
        wp = sb("wp", [128, 2, 2, 256], F16)
        bp = sb("bp", [1, 2, 256], F16)
        tgx = sb("tgx", [128, 1])
        tgf = sb("tgf", [128, 1])

        xb = sb("xb", [128, 2, 2, 256])
        xr = sb("xr", [128, 2, 2, 256])
        ckraw = sb("ckraw", [128, 2, 2, NC])
        cvraw = sb("cvraw", [NC, 2, 256])
        stats = sb("stats", [128, 2, 6])
        mv1 = sb("mv1", [128, 2, 2])
        mv2 = sb("mv2", [128, 2, 2])
        ve1 = sb("ve1", [128, 2])
        ve2 = sb("ve2", [128, 2])
        rs1 = sb("rs1", [128, 2])
        rs2 = sb("rs2", [128, 2])
        xTh = sb("xTh", [128, 2, 256], F16)
        xTl = sb("xTl", [128, 2, 256], F16)
        negmax = sb("negmax", [128, 2, 2])
        ident_b = sb("ident_b", [128, 128], BF16)
        ident_h = sb("ident_h", [128, 128], F16)
        rden = sb("rden", [128, 16])
        o = sb("o", [128, 2, 256])
        oTh = sb("oTh", [128, 2, 256], F16)
        oTl = sb("oTl", [128, 2, 256], F16)
        row = sb("row", [128, 2, 2, ROW])
        xn2T = sb("xn2T", [128, 2, 256])
        lmax = sb("lmax", [128, 2])
        lg = sb("lg", [128, 2, 8])
        ex = sb("ex", [128, 2, 8])
        esum = sb("esum", [128, 2])
        pr = sb("pr", [128, 2, 8])
        gt = sb("gt", [128, 2, 8, 8])
        eq = sb("eq", [128, 2, 8, 8])
        rank = sb("rank", [128, 2, 8])
        oh = sb("oh", [128, 2, 2, 8])
        ohp = sb("ohp", [128, 2, 2, 8])
        pg = sb("pg", [128, 2, 2])
        den = sb("den", [128, 2])
        sel = sb("sel", [128, 2, 8], F16)
        seen = sb("seen", [128, 8], F16)
        pos = sb("pos", [128, 2, 8])
        idxf = sb("idxf", [128, 2, 2])
        idx = sb("idx", [128, 2, 2, 2], I32)
        ohq = sb("ohq", [128, 2, 2, 8])
        ohs = sb("ohs", [128, 2, 8])
        ohe = sb("ohe", [128, 2, 8])
        gall = sb("gall", [128, 2 * B, 8])

        cnt = sb("cnt", [128, 8])
        nti = sb("nti", [128, 8], I32)
        ntf = sb("ntf", [128, 8])
        tend = sb("tend", [128, 8])
        tnum = sb("tnum", [128, NT + 1])
        tcmp = sb("tcmp", [128, NT + 1, 8])
        tcmp2 = sb("tcmp2", [128, NT + 1, 8])
        texp = sb("texp", [128, NT + 1])
        tbase = sb("tbase", [128, NT + 1])
        tscr = sb("tscr", [128, NT + 1])
        tabs = sb("tabs", [128, 3, NT + 1], I32)
        thr_t = sb("thr_t", [128, NT + 1])
        cut_t = sb("cut_t", [128, NT + 1])
        padf = sb("padf", [128, 8])
        padi = sb("padi", [128, 8], I32)
        padrow = sb("padrow", [128, 2, ROW])
        gT = sb("gT", [128, 512])
        tokT = sb("tokT", [128, 512])
        gcmp = sb("gcmp", [128, 512])
        thr = sb("thr", [128, 1], I32)
        cand = sb("cand", [128, 1], I32)
        bit = sb("bit", [128, 1], I32)
        bitf = sb("bitf", [128, 1])
        keep_i = sb("keep_i", [128, 1], I32)
        count = sb("count", [128, 1])
        need = sb("need", [128, 1])
        cut = sb("cut", [128, 1])
        candf = sb("candf", [128, 1])
        stepf = sb("stepf", [128, 1])
        diag = sb("diag", [8, 2, 8])
        lim = sb("lim", [128, 2, 8])

        with ExitStack() as att_stack:
            def att(name, shape, dt=F32):
                return att_stack.enter_context(nc.sbuf_tensor(name, shape, dt))

            xn = att("xn", [128, 2, 256])
            qs = att("qs", [128, 2, 2, N], F16)
            ks = att("ks", [128, 2, 2, NK], F16)
            qst = att("qst", [128, 2, 4, 2, N], F16)
            kst = att("kst", [128, 2, 4, 2, NK], F16)
            vh = att("vh", [128, 2, 3, H, D + 1], F16)
            vl = att("vl", [128, 2, 3, H, D], F16)
            p = att("p", [128, 4, 2, NK])
            pl = att("pl", [128, 4, 2, NK], F16)
            ptx = att("ptx", [128, 2, 2, 2, 2, 128], U16)
            ptc = att("ptc", [NC, 2, 2, 2, 128], U16)
            wst = att("wst", [128, 2, 3, 512])
            wout = att("wout", [128, 2, 6, 512], F16)
            p_high = p[:].bitcast(BF16)[:, :, :, 1:2 * NK:2]

        wb = sb("wb", [128, 2, 4, WPIECE], F16)
        xe = sb("xe", [128, 2, 2, ROW])
        eTh = sb("eTh", [128, 2, 2, TS], F16)
        eTl = sb("eTl", [128, 2, 2, TS], F16)
        sg = sb("sg", [128, 2, TS])
        h32 = sb("h32", [128, 2, TS])
        hh = sb("hh", [128, 4, TS], F16)
        hl = sb("hl", [128, 4, TS], F16)
        gf = sb("gf", [128, 2, 2])
        ga = sb("ga", [128, 2])
        gb = sb("gb", [128, 2])
        gg = sb("gg", [128, 2])
        gk = sb("gk", [128, 2])
        toki = sb("toki", [128, 2, 2], I32)
        y = sb("y", [128, 2, 2, 256])
        held = sb("held", [128, HOLD, 2, 256])
        tails = sb("tails", [128, HOLD, 2, 4])
        ga_h = sb("ga_h", [128, HOLD, 2])
        gb_h = sb("gb_h", [128, HOLD, 2])
        gg_h = sb("gg_h", [128, HOLD, 2])
        gk_h = sb("gk_h", [128, HOLD, 2])
        gf_h = sb("gf_h", [128, HOLD, 2])
        toki_h = sb("toki_h", [128, HOLD, 2], I32)

        s_const = sem("const_loaded")
        s_made = sem("const_made")
        s_pmade = sem("pool_const_made")
        s_tanh = sem("tanh_done")
        sp_waits_over, pool_waits_over, dve_waits_over = sem("sp_waits_over"), sem("pool_waits_over"), sem("dve_waits_over")
        s_padrow = sem("pad_rows_made")
        key_high, value_high = sem("ctx_key_high"), sem("ctx_value_high")
        plow = sem("probs_low")
        w_high = sem("w_high")
        s_dve = sem("dve_order")
        s_pool = sem("pool_order")
        s_x = [sem("x_loaded0"), sem("x_loaded1")]
        s_ck = [sem("ctxk_loaded0"), sem("ctxk_loaded1")]
        s_cv = [sem("ctxv_loaded0"), sem("ctxv_loaded1")]
        q_saved, k_saved = sem("q_saved"), sem("k_saved")
        q_stacked = [sem("q_stacked0"), sem("q_stacked1")]
        k_stacked = [sem("k_stacked0"), sem("k_stacked1")]
        s_w = [sem("w_loaded0"), sem("w_loaded1")]
        s_xr = [sem("residual_loaded0"), sem("residual_loaded1")]
        s_xst = [sem("x1_stored0"), sem("x1_stored1")]
        s_wst = [sem("w_stored0"), sem("w_stored1")]
        s_scat = [sem("rows_scattered0"), sem("rows_scattered1")]
        ve1_ready, rs1_ready, ve2_ready, rs2_ready = sem("ve1_ready"), sem("rs1_ready"), sem("ve2_ready"), sem("rs2_ready")
        xn_ready, row_ready = sem("xn_ready"), sem("row_ready")
        ctx_split, w_split = sem("ctx_split"), sem("w_split")
        filled, emptied = sem("misc_filled"), sem("misc_emptied")
        pre_hi, ot_hi = sem("pre_high"), sem("ot_high")
        scored, maxed, expd = sem("scored"), sem("maxed"), sem("exp_done")
        turned, ptx_out, ptc_out = sem("probs_turned"), sem("ptx_out"), sem("ptc_out")
        pv_done, o_out = sem("pv_done"), sem("o_out")
        ex_ready, sel_ready, idx_ready = sem("router_exp"), sem("sel_ready"), sem("idx_ready")
        s_cnt, s_gt, s_gtc, s_count, s_cnt_in, s_lim, s_limin = (
            sem("counts_done"), sem("gates_turned"), sem("gates_copied"), sem("count_summed"), sem("count_in"),
            sem("limits_done"), sem("limits_in"))
        s_tabs, s_padi, s_pads = sem("tables_ready"), sem("pads_ready"), sem("pads_stored")
        s_dummy = sem("dummy_rows_stored")
        held_scaled = sem("held_scaled")
        s_guess = sem("first_expert_loaded")
        s_wl = [sem("expert_w0"), sem("expert_w1")]
        s_xe = [sem("slots_loaded0"), sem("slots_loaded1")]
        gu_filled, silu_done, mult_done, hhi_done, hlo_done = (
            sem("gu_filled"), sem("silu_done"), sem("mult_done"), sem("hhi_done"), sem("hlo_done"))
        et_filled, et_hi, et_lo = sem("et_filled"), sem("et_high"), sem("et_low")
        y_filled, y_out, gf_ready, s_add = sem("y_filled"), sem("y_out"), sem("gf_ready"), sem("rows_added")

        def pre_use(b, k):
            return use(b.n - 1, "pre", k)

        def post_use(b, k):
            return use(b.n + 1, "post", k)

        def head_at(b, h, lag, heads, post, pre):
            n = h - lag
            if n < 0:
                return (b.prev(), n + H) if post else None
            if n >= H:
                return (b.next(), n - H) if pre else None
            return (b, n) if heads else None

        class Chain:
            def __init__(self, eng, s, after=None):
                self.eng, self.s, self.base, self.n, self.after = eng, s, 0, 0, after

            def __call__(self, ins):
                self.n += 1
                ins.then_inc(self.s, 1)
                self.eng.wait_ge(self.s, self.base + self.n)
                if self.after:
                    settle(self.eng, self.after)

            def note(self, ins):
                self.n += 1
                ins.then_inc(self.s, 1)

            def wait(self):
                self.eng.wait_ge(self.s, self.base + self.n)

            def rest(self):
                self.base, self.n = self.base + self.n, 0

        def batches(eng, body, chain=None):
            def part(*a):
                if chain:
                    chain.rest()
                body(*a)
            part(at(-1), False, False, True)
            part(at(0), True, False, True)
            part(at(1), True, True, True)
            part(at(2), True, True, True)
            if chain:
                chain.rest()
                start = chain.base
            with eng.Fori(1, (B - 2) // 2) as i:
                for j in (1, 2):
                    if chain:
                        chain.n = 0
                        chain.base = start + (i - 1) * (2 * chain.per) + (j - 1) * chain.per
                    body(At(2 * i + j, i + j // 2, j % 2), True, True, True)
                    if chain:
                        assert chain.n == chain.per, (chain.n, chain.per)
            if chain:
                chain.base, chain.n = start + (B - 4) * chain.per, 0
            part(at(B - 1), True, True, False)
            part(at(B), False, True, False)

        def tiles(eng, body, chain=None):
            def part(*a):
                if chain:
                    chain.rest()
                body(*a)
            for n in range(-1, HOLD + 1):
                part(at(n))
            if chain:
                chain.rest()
                start = chain.base
            with eng.Fori(HOLD // 2, (NT - 1) // 2) as i:
                for j in (1, 2):
                    if chain:
                        chain.n = 0
                        chain.base = start + (i - HOLD // 2) * (2 * chain.per) + (j - 1) * chain.per
                    body(At(2 * i + j, i + j // 2, j % 2))
                    if chain:
                        assert chain.n == chain.per, (chain.n, chain.per)
            if chain:
                chain.base, chain.n = start + (NT - 1 - HOLD) * chain.per, 0
            part(at(NT))

        block = ctx_stack.enter_context(nc.Block())

        @block.sync
        def _(sp):
            def load_batch(b):
                par = b.par
                wait(sp, xn_ready, b.n - 1)
                sp.dma_start(xb[:, par], x[bass.ds(b.n, 1)].rearrange("a (t p) c -> p (a t) c", p=128)).then_inc(s_x[par], 16)
                wait(sp, ctx_split, 2 * (b.n - 1))
                sp.dma_start(ckraw[:, par], ctx_kT[bass.ds(b.n, 1)].rearrange("a p c k -> p (a c) k")).then_inc(s_ck[par], 16)
                sp.dma_start(cvraw[:, par], ctx[bass.ds(b.n, 1), :, C:].rearrange("a k c -> k (a c)")).then_inc(s_cv[par], 16)

            def load_weights(b, e, q):
                wait(sp, w_split, 3 * (b.n - 1))
                for k, w in enumerate((gate_w, up_w)):
                    sp.dma_start(wst[:, b.par, k].rearrange("p (k c) -> p k c", k=2),
                                 w[bass.ds(e, 1), :, bass.ds(q * 256, 256)].rearrange("a (k p) c -> p (a k) c", p=128)
                                 ).then_inc(s_w[b.par], 16)
                sp.dma_start(wst[:, b.par, 2].rearrange("p (k c) -> p k c", k=2),
                             down_w[bass.ds(e, 1), bass.ds(q * 256, 256), :].rearrange("a (k p) c -> p (a k) c", p=128)
                             ).then_inc(s_w[b.par], 16)

            def stack(b):
                for step, turn_, made, stacks, saved, stacked in ((1, q_turn, qs, qst, q_saved, q_stacked),
                                                                  (2, k_turn, ks, kst, k_saved, k_stacked)):
                    sp.wait_ge(emptied, pre_use(b, step) + 1)
                    if step == 2:
                        settle(sp, sp_waits_over)
                        sp.wait_ge(ctx_split, 2 * b.n + 1)
                    for s in (0, 1):
                        copies = turn_[b.par].rearrange("h d i j n -> (h d) i j n")
                        copies = copies[:, :, s] if step == 1 else copies[:, s]
                        sp.dma_start(copies, made[:, s].rearrange("p c n -> p (c n)").unsqueeze(1).to_broadcast(
                            [128, 2, 2 * (N if step == 1 else NK)])).then_inc(saved, 16)
                    wait(sp, pv_done, 16 * (b.n - 1))
                    settle(sp, sp_waits_over)
                    sp.wait_ge(saved, 32 * (b.n + 1))
                    sp.dma_start(stacks[:, b.par].rearrange("p a c n -> p a (c n)"),
                                 turn_[b.par].rearrange("(a h) d i j n -> (h d i j) a n", h=2)).then_inc(stacked[b.par], 16)

            def store_weights(b, e, q):
                sp.wait_ge(w_split, 3 * (b.n + 1))
                sp.dma_start(wsplit[bass.ds(e, 1), bass.ds(q, 1)].rearrange("a q p c -> p (a q c)"),
                             wout[:, b.par].rearrange("p s c -> p (s c)")).then_inc(s_wst[b.par], 16)

            def load_residual(b):
                wait(sp, s_xst[b.par], 16 * b.half)
                wait(sp, row_ready, b.n - 1)
                sp.dma_start(xr[:, b.par], x[bass.ds(b.n, 1)].rearrange("a (t p) c -> p (a t) c", p=128)).then_inc(s_xr[b.par], 16)

            def store_x1(b):
                sp.wait_ge(emptied, post_use(b, 1) + 1)
                sp.dma_start(out[bass.ds(b.n * N, N)].rearrange("(t p) c -> p t c", p=128), xr[:, b.par]).then_inc(s_xst[b.par], 16)

            load_batch(at(0))
            sp.dma_start(wraw[:], wqkvT.rearrange("(k p) n -> p k n", p=128)).then_inc(s_const, 16)
            sp.dma_start(praw[:], wprojT.rearrange("(k p) n -> p k n", p=128)).then_inc(s_const, 16)
            sp.dma_start(braw[:], b_proj.rearrange("(a n) -> a n", a=1)).then_inc(s_const, 16)
            sp.dma_start(rout[:], router_w.rearrange("(k p) n -> p k n", p=128)).then_inc(s_const, 16)
            sp.dma_start(tgx[:], g_xattn.rearrange("(a n) -> a n", a=1).to_broadcast([128, 1])).then_inc(s_const, 16)
            sp.dma_start(tgf[:], g_ffn.rearrange("(a n) -> a n", a=1).to_broadcast([128, 1])).then_inc(s_const, 16)
            load_batch(at(1))
            stack(at(0))
            for n in (0, 1):
                load_weights(at(n), 0, n)
                load_residual(at(n))
            load_batch(at(2))
            stack(at(1))
            store_weights(at(0), 0, 0)
            load_weights(at(2), 0, 2)

            def step(b, q0, q2):
                load_batch(b.next().next())
                store_x1(b.prev())
                load_residual(b.next())
                stack(b.next())
                store_weights(b, *q0)
                load_weights(b.next().next(), *q2)
            step(at(1), (0, 1), (0, 3))
            with sp.Fori(1, B // 2 - 1) as i:
                step(At(2 * i, i, 0), (i // 2, (i % 2) * 2), ((i + 1) // 2, ((i + 1) % 2) * 2))
                step(At(2 * i + 1, i, 1), (i // 2, (i % 2) * 2 + 1), ((i + 1) // 2, ((i + 1) % 2) * 2 + 1))
            store_x1(at(B - 3))
            load_residual(at(B - 1))
            stack(at(B - 1))
            for n in (B - 2, B - 1):
                store_weights(at(n), n // 4, n % 4)
                store_x1(at(n))

            sp.wait_ge(s_padrow, 1)
            sp.dma_start(out[T:T + TS].rearrange("(s p) c -> p s c", p=128), padrow[:, :, 0:C]).then_inc(s_dummy, 16)
            sp.dma_start(slots[E * REGION:].rearrange("(s p) c -> p s c", p=128), padrow[:]).then_inc(s_dummy, 16)
            sp.wait_ge(s_dummy, 32)
            for par in (0, 1):
                sp.wait_ge(s_wst[par], 16 * B // 2)
                sp.wait_ge(s_xst[par], 16 * B // 2)
            sp.dma_start(wb[:, 0], wsplit[0].rearrange("q p c -> p q c")).then_inc(s_guess, 16)
            sp.wait_ge(s_padi, 1)
            for e in range(E):
                r0 = nc.values_load(padi[0:1, e:e + 1], engines=(mybir.EngineType.SP,), min_val=0, max_val=E * REGION - TS,
                                    skip_runtime_bounds_check_because="no expert has more than T slots")
                sp.dma_start(slots[bass.ds(r0, TS)].rearrange("(s p) c -> p s c", p=128), padrow[:]).then_inc(s_pads, 16)
            sp.wait_ge(s_tabs, 1)
            sp.wait_ge(s_guess, 16)

            def load_expert(t):
                e = nc.values_load(tabs[0:1, 0, bass.ds(t.n, 1)], engines=(mybir.EngineType.SP,), min_val=0, max_val=E - 1,
                                   skip_runtime_bounds_check_because="the table is clipped")
                new = nc.values_load(tabs[0:1, 2, bass.ds(t.n, 1)], engines=(mybir.EngineType.SP,), min_val=0, max_val=1,
                                     skip_runtime_bounds_check_because="it is a comparison's result")
                wait(sp, y_filled, t.n - 1)
                sp.dma_start(wb[:, t.par], wsplit[bass.ds(e, 1)].rearrange("a q p c -> p (a q) c"),
                             cond=new).then_inc(s_wl[t.par], 16)

            def load_rows(t):
                r0 = nc.values_load(tabs[0:1, 1, bass.ds(t.n, 1)], engines=(mybir.EngineType.SP,), min_val=0, max_val=E * REGION,
                                    skip_runtime_bounds_check_because="the table is clipped")
                wait(sp, gf_ready, t.n - 1)
                sp.dma_start(xe[:, t.par], slots[bass.ds(r0, TS)].rearrange("(s p) c -> p s c", p=128)).then_inc(s_xe[t.par], 16)

            def load_tile(t):
                load_rows(t)
                load_expert(t)

            load_expert(at(0))
            for par in (0, 1):
                sp.wait_ge(s_scat[par], 64 * B // 2)
            sp.wait_ge(s_pads, 16 * E)
            load_rows(at(0))
            load_tile(at(1))
            load_tile(at(2))
            with sp.Fori(1, (NT - 1) // 2) as i:
                for j in (1, 2):
                    load_tile(At(2 * i + j, i + j // 2, j % 2))
            load_tile(at(NT))
            sp.wait_ge(s_wl[1], 16 * ((NT + 1) // 2))
            sp.wait_ge(s_wl[0], 16 * ((NT + 1) // 2))
            sp.wait_ge(s_add, 32 * NT)

        @block.gpsimd
        def _(pool):
            chain = Chain(pool, s_pool)
            pool.memset(ident[:], 0.0).then_inc(s_pmade, 1)
            chain(pool.memset(tri[:], 1.0))
            pool.wait_ge(s_pmade, 1)
            chain(pool.affine_select(out=ident[:], in_=ident[:], compare_op=ALU.not_equal, fill=1.0, base=0,
                                     pattern=[[-1, 128]], channel_multiplier=1))
            chain(pool.affine_select(out=tri[:], in_=tri[:], compare_op=ALU.is_gt, fill=0.0, base=0,
                                     pattern=[[1, 128]], channel_multiplier=-1))
            chain(pool.memset(ones16[:], 1.0))
            chain(pool.memset(ones32[:], 1.0))
            chain(pool.memset(mhalf[:], -0.5))
            chain(pool.memset(seen[:], 0.0))
            for par in (0, 1):
                chain(pool.memset(vh[:, par, :, :, D:D + 1], 1.0))
            chain(pool.memset(before[:], 1.0))
            chain(pool.affine_select(out=before[:], in_=before[:], compare_op=ALU.is_gt, fill=0.0, base=0,
                                     pattern=[[1, 8], [-1, 8]], channel_multiplier=0))
            chain(pool.iota(iscr[:, 0:1], [[0, 1]], base=0, channel_multiplier=1))
            chain(pool.iota(iscr[:, 1:9], [[1, 8]], base=0, channel_multiplier=0))
            chain(pool.iota(iscr[:, 16:16 + NT + 1], [[1, NT + 1]], base=0, channel_multiplier=0))
            chain(pool.iota(iscr[:, 128:256], [[-1, 128]], base=128, channel_multiplier=1))
            chain(pool.iota(tokTi[:], [[16 * 128, 4], [1, 128]], base=0, channel_multiplier=0))
            pool.memset(padrow[:], 0.0).then_inc(s_pmade, 1)

            def scatter(b, c, t):
                if (c, t) == (0, 0):
                    pool.wait_ge(idx_ready, b.n + 1)
                    settle(pool, pool_waits_over)
                pool.indirect_dma_start(out=slots[:], out_offset=bass.IndirectOffsetOnAxis(ap=idx[:, b.par, c, t:t + 1], axis=0),
                                        in_=row[:, b.par, t], in_offset=None).then_inc(s_scat[b.par], 16)

            def body(b, heads, post, pre):
                nb, lb = b.next(), b.prev()
                for h in range(H):
                    if heads:
                        g = b.n * H + h
                        pool.wait_ge(expd, g + 1)
                        wait(pool, turned, g - 3)
                        pool.tensor_tensor(pl[:, h % 4], p[:, h % 4], p_high[:, h % 4], ALU.subtract).then_inc(plow, 1)
                    if pre and h == 1:
                        pool.wait_ge(ve1_ready, nb.n + 1)
                        pool.tensor_tensor(rs1[:], ve1[:], mhalf[:], ALU.pow).then_inc(rs1_ready, 1)
                    if pre and h in (4, 11):
                        if h == 4:
                            wait(pool, k_saved, 32 * nb.n)
                        else:
                            wait(pool, pv_done, 16 * (nb.n - 1))
                        src, high, low_, loaded, made = (
                            (ckraw[:, nb.par], ks[:, 0, :, 0:NC], ks[:, 1, :, 0:NC], s_ck, key_high) if h == 4 else
                            (cvraw[:, nb.par].rearrange("p (h d) -> p h d", h=H), vh[0:NC, nb.par, 0, :, 0:D],
                             vl[0:NC, nb.par, 0], s_cv, value_high))
                        pool.wait_ge(loaded[nb.par], 16 * (nb.half + 1))
                        settle(pool, pool_waits_over)
                        pool.tensor_copy(high, src).then_inc(made, 1)
                        pool.wait_ge(made, nb.n + 1)
                        pool.tensor_tensor(low_, src, high, ALU.subtract).then_inc(ctx_split, 1)
                    if post and h == 7:
                        pool.wait_ge(ve2_ready, lb.n + 1)
                        pool.tensor_tensor(rs2[:], ve2[:], mhalf[:], ALU.pow).then_inc(rs2_ready, 1)
                    if h in S_SLOTS and not (isinstance(b.n, int) and b.n < 2):
                        n = S_SLOTS.index(h)
                        scatter(lb.prev(), n // 2, n % 2)

            batches(pool, body)
            for n in range(4):
                scatter(at(B - 1), n // 2, n % 2)

            pool.wait_ge(s_dummy, 32)
            for par in (0, 1):
                pool.wait_ge(s_xst[par], 16 * B // 2)

            def add_tile(t):
                pool.wait_ge(y_out, t.n + 1)
                wait(pool, s_add, 32 * t.n)
                settle(pool, pool_waits_over)
                for s in (0, 1):
                    pool.indirect_dma_start(out=out[:], out_offset=bass.IndirectOffsetOnAxis(ap=toki[:, t.par, s:s + 1], axis=0),
                                            in_=y[:, t.par, s], in_offset=None, compute_op=ALU.add).then_inc(s_add, 16)

            for n in range(HOLD):
                pool.wait_ge(held_scaled, n + 1)
                wait(pool, s_add, 32 * n)
                for s in (0, 1):
                    pool.indirect_dma_start(out=out[:], out_offset=bass.IndirectOffsetOnAxis(ap=toki_h[:, n, s:s + 1], axis=0),
                                            in_=held[:, n, s], in_offset=None, compute_op=ALU.add).then_inc(s_add, 16)
            add_tile(at(HOLD))
            with pool.Fori(HOLD // 2, (NT - 1) // 2) as i:
                for j in (1, 2):
                    add_tile(At(2 * i + j, i + j // 2, j % 2))

        @block.scalar
        def _(act):
            act.wait_ge(s_const, 96)
            act.activation(tgx[:], tgx[:], ACT.Tanh).then_inc(s_tanh, 1)
            act.activation(tgf[:], tgf[:], ACT.Tanh).then_inc(s_tanh, 1)

            def ctx_out(b, h):
                g = b.n * H + h
                act.wait_ge(turned, g + 1)
                wait(act, pv_done, g - 1)
                act.copy(ptc[:, h % 2].rearrange("p s t q -> p (s t q)"), ptc_ps[0:NC].bitcast(U16)[:, 0:512]).then_inc(ptc_out, 1)

            def body(b, heads, post, pre):
                nb, lb = b.next(), b.prev()
                for h in range(H):
                    if heads:
                        g = b.n * H + h
                        act.wait_ge(maxed, g + 1)
                        wait(act, turned, g - 3)
                        for t in (0, 1):
                            last = act.activation(p[:, h % 4, t], bank[h % 2][:, t, 0:NK], ACT.Exp,
                                                  bias=negmax[:, h % 2, t:t + 1])
                        last.then_inc(expd, 1)
                    if bh := head_at(b, h, COPY, heads, post, False):
                        ctx_out(*bh)
                    for slot, kind, k in USES:
                        if slot != h or not (post if kind == "post" else pre):
                            continue
                        if kind == "post" and k in (0, 2):
                            act.wait_ge(filled, post_use(lb, k) + 1)
                        if kind == "post" and k == 0:
                            act.copy(oTh[:].rearrange("p k t -> p (k t)"), misc[:]).then_inc(ot_hi, 1)
                        if kind == "post" and k == 2:
                            act.copy(xn2T[:].rearrange("p k t -> p (k t)"), misc[:]).then_inc(emptied, 1)
                        if kind == "pre":
                            act.wait_ge(filled, pre_use(nb, k) + 1)
                            if k == 1:
                                wait(act, q_saved, 32 * nb.n)
                            if k == 2:
                                wait(act, k_saved, 32 * nb.n)
                            dst, src = (
                                (xTh[:].rearrange("p k t -> p (k t)"), misc[:]) if k == 0 else
                                (qs[:, 0].rearrange("p c t -> p (c t)"), misc[:]) if k == 1 else
                                (ks[:, 0, :, NC:NK], misc[:].rearrange("p (c t) -> p c t", c=2)) if k == 2 else
                                (vh[:, nb.par, 1:3, :, 0:D], misc[:].rearrange("p (t h d) -> p t h d", t=2, h=H)))
                            act.copy(dst, src).then_inc(pre_hi, 1)
                    if post and h == 11:
                        act.wait_ge(emptied, post_use(lb, 3) + 1)
                        act.activation(ex[:], lg[:], ACT.Exp).then_inc(ex_ready, 1)
                    if heads and h in W_SLOTS:
                        n = W_SLOTS.index(h)
                        if n == 0:
                            act.wait_ge(s_w[b.par], 48 * (b.half + 1))
                            wait(act, s_wst[b.par], 16 * b.half)
                        act.mul(wout[:, b.par, n], wst[:, b.par, n], WS).then_inc(w_high, 1)

            batches(act, body)

            def turned_high(t):
                act.wait_ge(et_filled, t.n + 1)
                act.copy(eTh[:, t.par].rearrange("p k t -> p (k t)"), misc[:]).then_inc(et_hi, 1)

            def high(t, c):
                u = t.n * 8 + c
                act.wait_ge(mult_done, u + 1)
                act.copy(hh[:, c % 4], h32[:, c % 2]).then_inc(hhi_done, 1)

            def tile(t):
                first = isinstance(t.n, int) and t.n < 0
                last = isinstance(t.n, int) and t.n == NT
                if first:
                    return turned_high(t.next())
                for c in range(8):
                    if not last:
                        u = t.n * 8 + c
                        act.wait_ge(gu_filled, u + 1)
                        wait(act, mult_done, u - 1)
                        act.activation(sg[:, c % 2], bank[c % 4 // 2][:, c % 2, 0:TS], ACT.Silu, scale=1.0 / WS).then_inc(silu_done, 1)
                    if c == 0 and not (isinstance(t.n, int) and t.n == 0):
                        high(t.prev(), 7)
                    if c and not last:
                        high(t, c - 1)
                    if c == 4 and not last:
                        turned_high(t.next())

            tiles(act, tile)

        @block.tensor
        def _(pe):
            def mm(out_, l, r, start, stop, **kw):
                return pe.matmul(out_, l, r, start=start, stop=stop, **kw)

            def three(dst, lh, ll, rh, rl):
                for n, (l, r) in enumerate(((lh, rh), (ll, rh), (lh, rl))):
                    for k in (0, 1):
                        last = mm(dst, l(k), r(k), n == 0 and k == 0, n == 2 and k == 1)
                return last

            def turn(src):
                for k in (0, 1):
                    for t in (0, 1):
                        last = pe.transpose(misc[:, k * 256 + t * 128:k * 256 + t * 128 + 128],
                                            src(t, k), ident[:])
                return last

            def scores(b, h):
                g = b.n * H + h
                wait(pe, expd, g - 1)
                c, pair, rows = h // 8, h % 8 // 2, slice(64 * (h % 2), 64 * (h % 2) + 64)
                for t in (0, 1):
                    last = mm(bank[h % 2][:, t, 0:NK], qst[rows, b.par, pair, c, t * 128:t * 128 + 128],
                              kst[rows, b.par, pair, c], True, True)
                last.then_inc(scored, 1)

            def turn_probs(b, h):
                g = b.n * H + h
                pe.wait_ge(plow, g + 1)
                wait(pe, ptx_out, g)
                wait(pe, ptc_out, g)
                for s, (src, i_, dt) in enumerate(((p_high, ident_b, BF16), (pl[:], ident_h, F16))):
                    cdst, xdst = ptc_ps[0:NC].bitcast(dt), ptx_ps[:].bitcast(dt)
                    for t in (0, 1):
                        pe.transpose(cdst[:, (s * 2 + t) * 128:(s * 2 + t) * 128 + 128], src[:, h % 4, t, 0:NC], i_[:])
                        for k in (0, 1):
                            at_ = ((s * 2 + k) * 2 + t) * 128
                            last = pe.transpose(xdst[:, at_:at_ + 128], src[:, h % 4, t, NC + k * 128:NC + k * 128 + 128], i_[:])
                last.then_inc(turned, 1)

            def values(b, h):
                g = b.n * H + h
                pe.wait_ge(ptx_out, g + 1)
                pe.wait_ge(ptc_out, g + 1)
                if h % 8 == 0:
                    wait(pe, o_out, 2 * b.n + h // 8)
                if h == 0:
                    pe.wait_ge(emptied, pre_use(b, 3) + 1)
                par = h % 2
                for t in (0, 1):
                    at_ = ((h % 8) * 2 + t) * 17
                    whole, plain = o_ps[:, at_:at_ + 17], o_ps[:, at_:at_ + 16]
                    for k in range(3):
                        n = NC if k == 0 else 128
                        hi, lo = ((ptc[:, par, s, t] if k == 0 else ptx[:, par, s, k - 1, t]).bitcast(dt)
                                  for s, dt in ((0, BF16), (1, F16)))
                        mm(whole, hi, vh[0:n, b.par, k, h], k == 0, False)
                        mm(plain, hi, vl[0:n, b.par, k, h], False, False)
                        last = mm(whole, lo, vh[0:n, b.par, k, h], False, k == 2)
                last.then_inc(pv_done, 1)

            def pre_step(b, k):
                wait(pe, emptied, pre_use(b, k))
                if k == 0:
                    pe.wait_ge(xn_ready, b.n + 1)
                    last = turn(lambda t, c: xn[:, t, c * 128:c * 128 + 128])
                elif k < 3:
                    w = wq if k == 1 else wk
                    for c in (0, 1):
                        last = three(misc[:, c * 256:c * 256 + 256],
                                     lambda kk: w[:, 0, kk, c * 128:c * 128 + 128],
                                     lambda kk: w[:, 1, kk, c * 128:c * 128 + 128],
                                     lambda kk: xTh[:, kk, :], lambda kk: xTl[:, kk, :])
                else:
                    for t in (0, 1):
                        last = three(misc[:, t * 256:t * 256 + 256],
                                     lambda kk: xTh[:, kk, t * 128:t * 128 + 128],
                                     lambda kk: xTl[:, kk, t * 128:t * 128 + 128],
                                     lambda kk: wv[:, 0, kk, :], lambda kk: wv[:, 1, kk, :])
                last.then_inc(filled, 1)

            def post_step(b, k):
                wait(pe, emptied, post_use(b, k))
                if k == 0:
                    pe.wait_ge(o_out, 2 * b.n + 2)
                    last = turn(lambda t, c: o[:, t, c * 128:c * 128 + 128])
                elif k == 1:
                    for t in (0, 1):
                        dst = misc[:, t * 256:t * 256 + 256]
                        for n, (l, s) in enumerate(((oTh, 0), (oTl, 0), (oTh, 1))):
                            for c in (0, 1):
                                mm(dst, l[:, c, t * 128:t * 128 + 128], wp[:, s, c, :], n == 0 and c == 0, False)
                        mm(dst, ones16[0:1, :], bp[:, 0, :], False, False)
                        last = mm(dst, ones16[0:1, :], bp[:, 1, :], False, True)
                elif k == 2:
                    pe.wait_ge(row_ready, b.n + 1)
                    last = turn(lambda t, c: row[:, b.par, t, c * 128:c * 128 + 128])
                elif k == 3:
                    for t in (0, 1):
                        for c in (0, 1):
                            last = mm(misc[:, t * 8:t * 8 + 8], xn2T[:, c, t * 128:t * 128 + 128], rout[:, c, :], c == 0, c == 1)
                else:
                    pe.wait_ge(sel_ready, b.n + 1)
                    mm(misc[:, 0:8], tri[:], sel[:, 0], True, False)
                    mm(misc[:, 0:8], ones16[:], seen[:], False, True)
                    mm(misc[:, 8:16], tri[:], sel[:, 1], True, False)
                    mm(misc[:, 8:16], ones16[:], seen[:], False, False)
                    last = mm(misc[:, 8:16], ones16[:], sel[:, 0], False, True)
                last.then_inc(filled, 1)

            pe.wait_ge(s_made, 1)
            pe.wait_ge(s_pmade, 2)

            def body(b, heads, post, pre):
                nb, lb = b.next(), b.prev()
                for h in range(H):
                    if bh := head_at(b, h, -1, heads, post, pre):
                        if h + 1 == H:
                            pe.wait_ge(q_stacked[nb.par], 16 * (nb.half + 1))
                            pe.wait_ge(k_stacked[nb.par], 16 * (nb.half + 1))
                            pe.wait_ge(ctx_split, 2 * (nb.n + 1))
                        scores(*bh)
                    for slot, kind, k in USES:
                        if slot == h and kind == "post" and post:
                            post_step(lb, k)
                        if slot == h and kind == "pre" and pre:
                            pre_step(nb, k)
                    if bh := head_at(b, h, VALUES, heads, post, False):
                        values(*bh)
                    if bh := head_at(b, h, TURN, heads, post, False):
                        turn_probs(*bh)

            batches(pe, body)

            pe.wait_ge(s_cnt_in, 1)
            mm(misc[:, 0:8], ones16[:], seen[:], True, True).then_inc(s_cnt, 1)
            pe.wait_ge(idx_ready, B)
            for i in range(4):
                last = pe.transpose(o_ps[:, i * 128:i * 128 + 128], gall[:, i * 16:i * 16 + 16, :].rearrange("p t e -> p (t e)"), ident[:])
            last.then_inc(s_gt, 1)

            def search(u):
                if u <= BITS + CUTS:
                    pe.wait_ge(s_cnt_in, u + 2)
                    mm(ptx_ps[:, 0:1], same_expert[:], count[:], True, True).then_inc(s_count, 1)
                elif u == BITS + CUTS + 1:
                    pe.wait_ge(s_limin, 1)
                    mm(ptx_ps[:, 8:24], ones32[0:8, :], diag[:].rearrange("p a e -> p (a e)"), True, True).then_inc(s_lim, 1)

            def turn_tile(t):
                pe.wait_ge(s_xe[t.par], 16 * (t.half + 1))
                wait(pe, et_lo, t.n)
                turn(lambda s, c: xe[:, t.par, s, c * 128:c * 128 + 128]).then_inc(et_filled, 1)

            def weights(t, part, low, c, k=0):
                off = (low * 3 + part) * 512
                if part < 2:
                    off += k * 256 + (c % 2) * 128
                    return wb[:, t.par, c // 2, off:off + 128]
                off += (c % 2) * 256
                return wb[:, t.par, c // 2, off:off + 256]

            def gate_up(t, c):
                u = t.n * 8 + c
                wait(pe, mult_done, u - 3)
                for part in (0, 1):
                    last = three(bank[c % 4 // 2][:, c % 2, part * TS:part * TS + TS],
                                 lambda k: weights(t, part, 0, c, k), lambda k: weights(t, part, 1, c, k),
                                 lambda k: eTh[:, t.par, k, :], lambda k: eTl[:, t.par, k, :])
                last.then_inc(gu_filled, 1)

            y_ps = (ptc_ps, o_ps)

            def down(t, c):
                u = t.n * 8 + c
                pe.wait_ge(hhi_done, u + 1)
                pe.wait_ge(hlo_done, u + 1)
                if c == 0:
                    wait(pe, y_out, t.n - 1)
                for s in (0, 1):
                    rows = slice(s * 128, s * 128 + 128)
                    dst = y_ps[t.par][:, s * 256:s * 256 + 256]
                    mm(dst, hh[:, c % 4, rows], weights(t, 2, 0, c), c == 0 and s == 0, False, skip_group_check=True)
                    mm(dst, hl[:, c % 4, rows], weights(t, 2, 0, c), False, False, skip_group_check=True)
                    last = mm(dst, hh[:, c % 4, rows], weights(t, 2, 1, c), False, c == 7, skip_group_check=True)
                if c == 7:
                    last.then_inc(y_filled, 1)

            def tile(t):
                first = isinstance(t.n, int) and t.n < 0
                last = isinstance(t.n, int) and t.n == NT
                zero = isinstance(t.n, int) and t.n == 0
                if first:
                    pe.wait_ge(s_tabs, 1)
                    pe.wait_ge(s_gtc, 1)
                    return turn_tile(t.next())
                for c in range(8):
                    if not last:
                        if c == 0:
                            pe.wait_ge(et_lo, t.n + 1)
                            pe.wait_ge(s_wl[t.par], 16 * (t.half + 1))
                            if zero:
                                pe.wait_ge(s_guess, 16)
                        gate_up(t, c)
                    if c < 2 and not zero:
                        down(t.prev(), c + 6)
                    if c >= 2 and not last:
                        down(t, c - 2)
                    if isinstance(t.n, int) and 0 < 8 * t.n + c <= 8 * HOLD:
                        search(8 * t.n + c - 1)
                    if c == 4 and not last:
                        turn_tile(t.next())

            tiles(pe, tile)

        @block.vector
        def _(dve):
            link = Chain(dve, s_dve)
            bc = lambda a, n, shape: a.unsqueeze(n).to_broadcast(shape)
            dve.wait_ge(s_pmade, 2)
            link(dve.tensor_copy(ident_b[:], ident[:]))
            link(dve.tensor_copy(ident_h[:], ident[:]))
            for s in (0, 1):
                link(dve.tensor_scalar(slot_num[:, s:s + 1], iscr[:, 0:1], float(128 * s), None, ALU.add))
            link(dve.tensor_copy(tok_of[:], slot_num[:]))
            link(dve.tensor_scalar(iscr[:, 11:12], iscr[:, 0:1], 3, None, ALU.logical_shift_right))
            link(dve.tensor_copy(candf[:], iscr[:, 11:12]))
            link(dve.tensor_scalar(candf[:], candf[:], 128.0, None, ALU.mult))
            link(dve.tensor_copy(tokT[:], tokTi[:]))
            link(dve.tensor_scalar(tokT[:], tokT[:], candf[:, 0:1], None, ALU.add))
            link(dve.tensor_copy(iota8[:], iscr[:, 1:9]))
            link(dve.tensor_copy(tnum[:], iscr[:, 16:16 + NT + 1]))
            link(dve.tensor_scalar(iscr[:, 256:384], iscr[:, 128:256], 7, None, ALU.bitwise_and))
            link(dve.tensor_scalar(same_expert[:], iscr[:, 256:384], 0.0, None, ALU.is_equal))
            link(dve.tensor_scalar(region_at[:], iota8[:], float(REGION), None, ALU.mult))
            dve.tensor_scalar(padrow[:, :, C], slot_num[:], float(T), None, ALU.add).then_inc(s_padrow, 1)
            dve.wait_ge(s_const, 96)
            link(dve.tensor_scalar(wraw[:, :, 0:256], wraw[:, :, 0:256], D ** -0.5, None, ALU.mult))
            for w, src in ((wq, wraw[:, :, 0:256]), (wk, wraw[:, :, 256:512]), (wv, wraw[:, :, 512:768]), (wp, praw[:])):
                link(dve.tensor_copy(w[:, 0], src))
                link(dve.tensor_tensor(w[:, 1], src, w[:, 0], ALU.subtract))
            link(dve.tensor_copy(bp[:, 0], braw[:]))
            dve.tensor_tensor(bp[:, 1], braw[:], bp[:, 0], ALU.subtract).then_inc(s_made, 1)
            dve.wait_ge(s_tanh, 2)
            link(dve.tensor_scalar(bitf[:], tgf[:], 1.0 / (WS * WS), None, ALU.mult))
            link(dve.tensor_copy(tgf[:], bitf[:]))

            def norm_stats(step, src, mv, ve, ready):
                if step == 0:
                    for t in (0, 1):
                        settle(dve, dve_waits_over)
                        link.note(dve.bn_stats(stats[:, t], src[:, t]))
                    return
                link.wait()
                settle(dve, dve_waits_over)
                if step == 1:
                    for t in (0, 1):
                        link.note(dve.bn_aggr(mv[:, t], stats[:, t]))
                else:
                    dve.tensor_scalar(ve[:], mv[:, :, 1], EPS, None, ALU.add).then_inc(ready, 1)

            def ptx_evac(b, h):
                g = b.n * H + h
                dve.wait_ge(turned, g + 1)
                wait(dve, pv_done, g - 1)
                dve.tensor_copy(ptx[:, h % 2].rearrange("p s k t q -> p (s k t q)"), ptx_ps[:].bitcast(U16)).then_inc(ptx_out, 1)

            def row_max(b, h):
                g = b.n * H + h
                dve.wait_ge(scored, g + 1)
                wait(dve, expd, g - 1)
                dve.tensor_reduce(negmax[:, h % 2], bank[h % 2][:, :, 0:NK], AX, ALU.max, negate=True).then_inc(maxed, 1)

            def o_evac(b, g, step):
                src = o_ps[:, 0:272].rearrange("p (u d) -> p u d", d=17)
                if step == 0:
                    dve.wait_ge(pv_done, b.n * H + 8 * g + 8)
                    link.note(dve.reciprocal(rden[:].unsqueeze(2), src[:, :, 16:17]))
                    return
                link.wait()
                dst = o[:].rearrange("p t (h d) -> p h t d", h=H)[:, 8 * g:8 * g + 8]
                dve.tensor_tensor(dst, src[:, :, 0:16].rearrange("p (h t) d -> p h t d", t=2),
                                  bc(rden[:].rearrange("p (h t) -> p h t", t=2), 3, [128, 8, 2, 16]), ALU.mult).then_inc(o_out, 1)

            def low(b, k):
                dve.wait_ge(pre_hi, b.n * PRE + k + 1)
                pair = misc[:].rearrange("p (c t) -> p c t", c=2)
                lo, src, hi = (
                    (xTl[:], pair, xTh[:]) if k == 0 else
                    (qs[:, 1], pair, qs[:, 0]) if k == 1 else
                    (ks[:, 1, :, NC:NK], pair, ks[:, 0, :, NC:NK]) if k == 2 else
                    (vl[:, b.par, 1:3], misc[:].rearrange("p (t h d) -> p t h d", t=2, h=H), vh[:, b.par, 1:3, :, 0:D]))
                dve.tensor_tensor(lo, src, hi, ALU.subtract).then_inc(emptied, 1)

            logits = misc[:, 0:16].rearrange("p (t e) -> p t e", t=2)
            mine, other = bc(pr[:], 3, [128, 2, 8, 8]), bc(pr[:], 2, [128, 2, 8, 8])

            def route(b, step):
                par = b.par
                link.wait()
                if step == 0:
                    dve.tensor_tensor(lg[:], logits, bc(lmax[:], 2, [128, 2, 8]), ALU.subtract).then_inc(emptied, 1)
                elif step == 1:
                    dve.wait_ge(ex_ready, b.n + 1)
                    link.note(dve.tensor_reduce(esum[:], ex[:], AX, ALU.add))
                elif step == 2:
                    link.note(dve.reciprocal(esum[:], esum[:]))
                elif step == 3:
                    link.note(dve.tensor_tensor(pr[:], ex[:], bc(esum[:], 2, [128, 2, 8]), ALU.mult))
                elif step == 4:
                    link.note(dve.tensor_tensor(gt[:], other, mine, ALU.is_gt))
                    link.note(dve.tensor_tensor(eq[:], other, mine, ALU.is_equal))
                elif step == 5:
                    link.note(dve.tensor_tensor(eq[:], eq[:], bc(before[:], 1, [128, 2, 8, 8]), ALU.mult))
                elif step == 6:
                    link.note(dve.tensor_tensor(gt[:], gt[:], eq[:], ALU.add))
                elif step == 7:
                    link.note(dve.tensor_reduce(rank[:], gt[:], AX, ALU.add))
                elif step == 8:
                    for c in (0, 1):
                        link.note(dve.tensor_scalar(oh[:, c], rank[:], float(c), None, ALU.is_equal))
                    dve.tensor_scalar(sel[:], rank[:], 1.0, None, ALU.is_le).then_inc(sel_ready, 1)
                elif step == 9:
                    for c in (0, 1):
                        link.note(dve.tensor_tensor(ohp[:, c], oh[:, c], pr[:], ALU.mult))
                elif step == 10:
                    link.note(dve.tensor_reduce(pg[:], ohp[:], AX, ALU.add))
                    link.note(dve.tensor_tensor(ohs[:], ohp[:, 0], ohp[:, 1], ALU.add))
                    link.note(dve.tensor_tensor(ohe[:], oh[:, 0], bc(iota8[:], 1, [128, 2, 8]), ALU.mult))
                elif step == 11:
                    link.note(dve.scalar_tensor_tensor(den[:], pg[:, 0], 1e-9, pg[:, 1], ALU.add, ALU.add))
                    link.note(dve.tensor_reduce(row[:, par, :, C + 3:C + 4].rearrange("p t a -> p (t a)"), ohe[:], AX, ALU.add))
                    link.note(dve.tensor_copy(row[:, par, :, C], tok_of[:]))
                elif step == 12:
                    link.note(dve.reciprocal(den[:], den[:]))
                    link.note(dve.tensor_scalar(tok_of[:], tok_of[:], float(N), None, ALU.add))
                elif step == 13:
                    link.note(dve.tensor_tensor(row[:, par, :, C + 1:C + 3].rearrange("p t c -> p c t"), pg[:],
                                                bc(den[:], 1, [128, 2, 2]), ALU.mult))
                    link.note(dve.tensor_tensor(gall[:, bass.ds(2 * b.n, 2)], ohs[:], bc(den[:], 2, [128, 2, 8]), ALU.mult))
                elif step == 14:
                    dve.wait_ge(filled, post_use(b, 4) + 1)
                    dve.tensor_tensor(pos[:], logits, bc(region_at[:], 1, [128, 2, 8]), ALU.add).then_inc(emptied, 1)
                    link.note(dve.tensor_tensor(seen[:], seen[:], sel[:, 0], ALU.add))
                elif step == 15:
                    dve.wait_ge(emptied, post_use(b, 4) + 1)
                    link.note(dve.tensor_tensor(seen[:], seen[:], sel[:, 1], ALU.add))
                    for c in (0, 1):
                        link.note(dve.tensor_tensor(ohq[:, c], oh[:, c], pos[:], ALU.mult))
                elif step == 16:
                    link.note(dve.tensor_reduce(idxf[:], ohq[:], AX, ALU.add))
                else:
                    dve.tensor_copy(idx[:, par], idxf[:]).then_inc(idx_ready, 1)

            def between(b, h, point, heads, post, pre):
                nb, lb = b.next(), b.prev()
                at_ = 4 * h + point
                if pre and at_ in (0, 2, 3):
                    if at_ == 0:
                        dve.wait_ge(s_x[nb.par], 16 * (nb.half + 1))
                    norm_stats((0, 2, 3).index(at_), xb[:, nb.par], mv1, ve1, ve1_ready)
                if post and at_ in (28, 29, 30):
                    if at_ == 28:
                        dve.wait_ge(emptied, post_use(lb, 1) + 1)
                    norm_stats(at_ - 28, xr[:, lb.par], mv2, ve2, ve2_ready)
                if post and at_ in (16, 17):
                    o_evac(lb, 1, at_ - 16)
                if heads and at_ in (48, 49):
                    o_evac(b, 0, at_ - 48)
                if post and at_ == 44:
                    route(lb, 0)
                if post and 48 <= at_:
                    route(lb, at_ - 47)
                if post and at_ == 63:
                    route(lb, 17)

            def body(b, heads, post, pre):
                nb, lb = b.next(), b.prev()
                for h in range(H):
                    between(b, h, 0, heads, post, pre)
                    if bh := head_at(b, h, COPY, heads, post, False):
                        ptx_evac(*bh)
                    between(b, h, 1, heads, post, pre)
                    if bh := head_at(b, h, -1, heads, False, pre):
                        row_max(*bh)
                    between(b, h, 2, heads, post, pre)
                    if pre and h == 2:
                        dve.wait_ge(rs1_ready, nb.n + 1)
                        for t in (0, 1):
                            last = dve.tensor_scalar(xn[:, t], xb[:, nb.par, t], mv1[:, t, 0:1], rs1[:, t:t + 1], ALU.subtract, ALU.mult)
                        last.then_inc(xn_ready, 1)
                    if post and h == 8:
                        dve.wait_ge(rs2_ready, lb.n + 1)
                        wait(dve, s_scat[lb.par], 64 * lb.half)
                        for t in (0, 1):
                            last = dve.tensor_scalar(row[:, lb.par, t, 0:C], xr[:, lb.par, t], mv2[:, t, 0:1], rs2[:, t:t + 1], ALU.subtract, ALU.mult)
                        last.then_inc(row_ready, 1)
                    for slot, kind, k in USES:
                        if slot != h or not (post if kind == "post" else pre):
                            continue
                        if kind == "pre":
                            low(nb, k)
                        elif k == 0:
                            dve.wait_ge(ot_hi, lb.n + 1)
                            dve.tensor_tensor(oTl[:].rearrange("p k t -> p (k t)"), misc[:], oTh[:].rearrange("p k t -> p (k t)"),
                                              ALU.subtract).then_inc(emptied, 1)
                        elif k == 1:
                            dve.wait_ge(filled, post_use(lb, 1) + 1)
                            dve.wait_ge(s_xr[lb.par], 16 * (lb.half + 1))
                            xrow = xr[:, lb.par].rearrange("p t c -> p (t c)")
                            dve.scalar_tensor_tensor(xrow, misc[:], tgx[:, 0:1], xrow, ALU.mult, ALU.add).then_inc(emptied, 1)
                        elif k == 3:
                            dve.wait_ge(filled, post_use(lb, 3) + 1)
                            link.note(dve.tensor_reduce(lmax[:], logits, AX, ALU.max))
                    if heads and h - 1 in W_SLOTS:
                        n = W_SLOTS.index(h - 1)
                        dve.wait_ge(w_high, 3 * b.n + n + 1)
                        dve.scalar_tensor_tensor(wout[:, b.par, 3 + n], wst[:, b.par, n], WS, wout[:, b.par, n],
                                                 ALU.mult, ALU.subtract).then_inc(w_split, 1)
                    between(b, h, 3, heads, post, pre)

            link.per = 38
            batches(dve, body, link)
            link.rest()

            dve.sem_inc(s_cnt_in, 1)
            dve.wait_ge(s_cnt, 1)
            link(dve.tensor_copy(cnt[:], misc[:, 0:8]))
            link(dve.tensor_tensor(padf[:], cnt[:], region_at[:], ALU.add))
            dve.tensor_copy(padi[:], padf[:]).then_inc(s_padi, 1)
            link(dve.tensor_scalar(nti[:], cnt[:], float(TS - 1), None, ALU.add))
            link(dve.tensor_scalar(nti[:], nti[:], TS.bit_length() - 1, None, ALU.logical_shift_right))
            link(dve.tensor_copy(ntf[:], nti[:]))
            link(dve.tensor_tensor_scan(tend[:], ones32[:, 0:8], ntf[:], 0.0, ALU.mult, ALU.add))
            shape = [128, NT + 1, 8]
            link(dve.tensor_tensor(tcmp[:], bc(tnum[:], 2, shape), bc(tend[:], 1, shape), ALU.is_ge))
            link(dve.tensor_tensor(tcmp2[:], tcmp[:], bc(ntf[:], 1, shape), ALU.mult))
            link(dve.tensor_reduce(texp[:], tcmp[:], AX, ALU.add))
            link(dve.tensor_reduce(tbase[:], tcmp2[:], AX, ALU.add))
            link(dve.tensor_tensor(tbase[:], tnum[:], tbase[:], ALU.subtract))
            link(dve.tensor_scalar(tbase[:], tbase[:], float(TS), None, ALU.mult))
            link(dve.tensor_scalar(tscr[:], texp[:], float(REGION), None, ALU.mult))
            link(dve.tensor_tensor(tbase[:], tbase[:], tscr[:], ALU.add))
            link(dve.tensor_scalar(tabs[:, 1], tbase[:], float(E * REGION), None, ALU.min))
            link(dve.tensor_scalar(tscr[:], texp[:], float(E - 1), None, ALU.min))
            link(dve.tensor_copy(tabs[:, 0], tscr[:]))
            link(dve.tensor_scalar(tabs[:, 2, 0:1], tscr[:, 0:1], 0.0, None, ALU.not_equal))
            link(dve.memset(tabs[:, 2, 1:2], 1))
            dve.tensor_tensor(tabs[:, 2, 2:], tscr[:, 2:], tscr[:, :NT - 1], ALU.not_equal).then_inc(s_tabs, 1)

            dve.wait_ge(s_gt, 1)
            dve.tensor_copy(gT[:], o_ps[:]).then_inc(s_gtc, 1)
            dve.wait_ge(s_gtc, 1)
            link(dve.memset(thr[:], 0))
            link(dve.memset(bit[:], 1 << (BITS - 1)))
            link(dve.memset(cut[:], 0.0))
            link(dve.memset(stepf[:], float(1 << (CUTS - 1))))
            link.rest()
            thrf = thr[:, 0:1].bitcast(F32)

            def counted(compare, src, limit):
                dve.tensor_scalar(gcmp[:], src, limit, 0.0, compare, ALU.add, accum_out=count[:]).then_inc(s_cnt_in, 1)

            def search(u, part):
                if not 0 <= u < 8 * HOLD:
                    return
                if part:
                    link.wait()
                elif 0 < u <= BITS + CUTS + 1:
                    dve.wait_ge(s_count, u)
                if 0 < u <= BITS and part == 0:
                    link.note(dve.tensor_scalar(keep_i[:], ptx_ps[:, 0:1], float(CAP), -1.0, ALU.is_ge, ALU.mult))
                elif 0 < u <= BITS and part == 1:
                    link.note(dve.tensor_tensor(keep_i[:], keep_i[:], bit[:], ALU.bitwise_and))
                elif 0 < u <= BITS and part == 2:
                    link.note(dve.tensor_tensor(thr[:], thr[:], keep_i[:], ALU.bitwise_or))
                    link.note(dve.tensor_scalar(bit[:], bit[:], 1, None, ALU.logical_shift_right))
                elif u < BITS and part == 3:
                    link.note(dve.tensor_tensor(cand[:], thr[:], bit[:], ALU.bitwise_or))
                elif u < BITS and part == 4:
                    counted(ALU.is_ge, gT[:], cand[:, 0:1].bitcast(F32))
                elif u == BITS and part == 4:
                    counted(ALU.is_gt, gT[:], thrf)
                elif u == BITS + 1 and part == 0:
                    link.note(dve.tensor_scalar(need[:], ptx_ps[:, 0:1], -1.0, float(CAP), ALU.mult, ALU.add))
                    link.note(dve.tensor_scalar(gcmp[:], gT[:], thrf, float(4 * T), ALU.not_equal, ALU.mult))
                elif u == BITS + 1 and part == 1:
                    link.note(dve.tensor_tensor(tokT[:], tokT[:], gcmp[:], ALU.add))
                elif BITS + 1 < u <= BITS + CUTS + 1 and part == 0:
                    link.note(dve.tensor_scalar(candf[:], ptx_ps[:, 0:1], need[:, 0:1], stepf[:, 0:1], ALU.is_le, ALU.mult))
                elif BITS + 1 < u <= BITS + CUTS + 1 and part == 1:
                    link.note(dve.tensor_tensor(cut[:], cut[:], candf[:], ALU.add))
                    link.note(dve.tensor_scalar(stepf[:], stepf[:], 0.5, None, ALU.mult))
                elif BITS < u <= BITS + CUTS and part == 3:
                    link.note(dve.tensor_tensor(candf[:], cut[:], stepf[:], ALU.add))
                elif BITS < u <= BITS + CUTS and part == 4:
                    counted(ALU.is_lt, tokT[:], candf[:, 0:1])
                elif u == BITS + CUTS + 1 and part == 3:
                    link.note(dve.tensor_scalar(diag[:, 0], ident[0:8, 0:8], thr[0:8, 0:1].bitcast(F32), None, ALU.mult))
                    dve.tensor_scalar(diag[:, 1], ident[0:8, 0:8], cut[0:8, 0:1], None, ALU.mult).then_inc(s_limin, 1)
                elif u == BITS + CUTS + 2 and part == 0:
                    dve.wait_ge(s_lim, 1)
                    link.note(dve.tensor_copy(lim[:].rearrange("p a e -> p (a e)"), ptx_ps[:, 8:24]))
                    link.note(dve.tensor_tensor(tcmp[:], bc(texp[:], 2, shape), bc(iota8[:], 1, shape), ALU.is_equal))
                elif (u, part) in ((BITS + CUTS + 2, 1), (BITS + CUTS + 3, 1)):
                    link.note(dve.tensor_tensor(tcmp2[:], tcmp[:], bc(lim[:, u - BITS - CUTS - 2], 1, shape), ALU.mult))
                elif (u, part) in ((BITS + CUTS + 2, 2), (BITS + CUTS + 3, 2)):
                    dst = (thr_t, cut_t)[u - BITS - CUTS - 2]
                    link.note(dve.tensor_reduce(dst[:], tcmp2[:], AX, ALU.add))

            def turned_low(t):
                dve.wait_ge(et_hi, t.n + 1)
                dve.tensor_tensor(eTl[:, t.par].rearrange("p k t -> p (k t)"), misc[:], eTh[:, t.par].rearrange("p k t -> p (k t)"),
                                  ALU.subtract).then_inc(et_lo, 1)

            def low_h(t, c):
                dve.wait_ge(hhi_done, t.n * 8 + c + 1)
                dve.tensor_tensor(hl[:, c % 4], h32[:, c % 2], hh[:, c % 4], ALU.subtract).then_inc(hlo_done, 1)

            def y_evac(t):
                dve.wait_ge(y_filled, t.n + 1)
                for s in (0, 1):
                    last = dve.tensor_scalar(y[:, t.par, s], y_ps[t.par][:, s * 256:s * 256 + 256], gf[:, t.par, s:s + 1], None, ALU.mult)
                last.then_inc(y_out, 1)

            y_ps = (ptc_ps, o_ps)

            def hold(t):
                dve.wait_ge(y_filled, t.n + 1)
                dve.tensor_copy(held[:, t.n].rearrange("p s c -> p (s c)"), y_ps[t.par][:]).then_inc(y_out, 1)

            def held_gates():
                th, ct, e_t = (bc(a[:, 0:HOLD], 2, [128, HOLD, 2]) for a in (thr_t, cut_t, texp))
                tok, g0, g1, e0 = (tails[:, :, :, k] for k in range(4))
                link.wait()
                link.note(dve.tensor_tensor(ga_h[:], e0, e_t, ALU.is_equal))
                link(dve.tensor_tensor(gb_h[:], e0, e_t, ALU.not_equal))
                link.note(dve.tensor_tensor(ga_h[:], ga_h[:], g0, ALU.mult))
                link(dve.tensor_tensor(gb_h[:], gb_h[:], g1, ALU.mult))
                link.note(dve.tensor_tensor(gg_h[:], ga_h[:], gb_h[:], ALU.add))
                link(dve.tensor_copy(toki_h[:], tok))
                link.note(dve.tensor_tensor(ga_h[:], gg_h[:], th, ALU.is_gt))
                link.note(dve.tensor_tensor(gb_h[:], gg_h[:], th, ALU.is_equal))
                link(dve.tensor_tensor(gk_h[:], tok, ct, ALU.is_lt))
                link(dve.tensor_tensor(gb_h[:], gb_h[:], gk_h[:], ALU.mult))
                link(dve.tensor_tensor(ga_h[:], ga_h[:], gb_h[:], ALU.add))
                link(dve.tensor_tensor(ga_h[:], ga_h[:], gg_h[:], ALU.mult))
                link(dve.tensor_scalar(gf_h[:], ga_h[:], tgf[:, 0:1], None, ALU.mult))

            def scale_held(n):
                for s in (0, 1):
                    last = dve.tensor_scalar(held[:, n, s], held[:, n, s], gf_h[:, n, s:s + 1], None, ALU.mult)
                last.then_inc(held_scaled, 1)

            def gates(t, step):
                par = t.par
                e_t, th, ct = (a[:, bass.ds(t.n, 1)] for a in (texp, thr_t, cut_t))
                tok, g0, g1, e0 = (xe[:, par, :, C + k] for k in range(4))
                link.wait()
                if step == 0:
                    if not (isinstance(t.n, int) and t.n < HOLD + 2):
                        dve.wait_ge(s_add, 32 * (t.n - 1))
                    link.note(dve.tensor_scalar(ga[:], e0, e_t, None, ALU.is_equal))
                    link.note(dve.tensor_scalar(gb[:], e0, e_t, None, ALU.not_equal))
                    link.note(dve.tensor_scalar(gk[:], tok, ct, None, ALU.is_lt))
                    link.note(dve.tensor_copy(toki[:, par], tok))
                elif step == 1:
                    link.note(dve.tensor_tensor(ga[:], ga[:], g0, ALU.mult))
                    link.note(dve.tensor_tensor(gb[:], gb[:], g1, ALU.mult))
                elif step == 2:
                    link.note(dve.tensor_tensor(gg[:], ga[:], gb[:], ALU.add))
                elif step == 3:
                    link.note(dve.tensor_scalar(ga[:], gg[:], th, None, ALU.is_gt))
                    link.note(dve.tensor_scalar(gb[:], gg[:], th, None, ALU.is_equal))
                elif step == 4:
                    link.note(dve.tensor_tensor(gb[:], gb[:], gk[:], ALU.mult))
                elif step == 5:
                    link.note(dve.tensor_tensor(ga[:], ga[:], gb[:], ALU.add))
                elif step == 6:
                    link.note(dve.tensor_tensor(ga[:], ga[:], gg[:], ALU.mult))
                else:
                    dve.tensor_scalar(gf[:, par], ga[:], tgf[:, 0:1], None, ALU.mult).then_inc(gf_ready, 1)

            def tile(t):
                first = isinstance(t.n, int) and t.n < 0
                last = isinstance(t.n, int) and t.n == NT
                zero = isinstance(t.n, int) and t.n == 0
                if first:
                    return turned_low(t.next())
                early = isinstance(t.n, int) and t.n < HOLD
                for c in range(8):
                    if not last:
                        u = t.n * 8 + c
                        dve.wait_ge(silu_done, u + 1)
                        wait(dve, hlo_done, u - 1)
                        dve.tensor_tensor(h32[:, c % 2], sg[:, c % 2], bank[c % 4 // 2][:, c % 2, TS:2 * TS], ALU.mult).then_inc(mult_done, 1)
                    if early:
                        search(u, 0)
                    elif 3 <= c < 7 and not last:
                        gates(t, 2 * c - 6)
                    if c == 0 and not zero:
                        low_h(t.prev(), 7)
                    if c and not last:
                        low_h(t, c - 1)
                    if early:
                        search(u, 1)
                    if c == 2 and not zero:
                        if isinstance(t.n, int) and t.n <= HOLD:
                            hold(t.prev())
                        else:
                            y_evac(t.prev())
                    if c == 3 and early:
                        dve.tensor_copy(tails[:, t.n], xe[:, t.par, :, C:ROW]).then_inc(gf_ready, 1)
                    elif 3 <= c < 7 and not early and not last:
                        gates(t, 2 * c - 5)
                    if early:
                        search(u, 2)
                    if c == 4 and not last:
                        turned_low(t.next())
                    if early:
                        search(u, 3)
                        search(u, 4)
                    if isinstance(t.n, int) and t.n == HOLD:
                        if c == 0:
                            held_gates()
                        elif c <= HOLD:
                            scale_held(c - 1)

            link.per = 12
            tiles(dve, tile, link)


def kernel(x, ctx_2048, g_xattn, g_ffn, L0_xattn_w_qkv, L0_xattn_w_proj, L0_xattn_b_proj,
           L0_ffn_router_gate, L0_ffn_gate_w, L0_ffn_up_w, L0_ffn_down_w):
    import numpy as np
    import concourse.bacc as bacc
    from concourse.bass_utils import run_bass_kernel_spmd as run

    ctx = np.asarray(ctx_2048)
    kT = ctx[:, :, :C].reshape(B, NC, 2, 128).transpose(0, 3, 2, 1)
    arrays = {
        "x": np.asarray(x), "ctx_kT": kT, "ctx": ctx, "g_xattn": np.asarray(g_xattn), "g_ffn": np.asarray(g_ffn),
        "wqkvT": np.asarray(L0_xattn_w_qkv).T, "wprojT": np.asarray(L0_xattn_w_proj).T, "b_proj": np.asarray(L0_xattn_b_proj),
        "router_w": np.asarray(L0_ffn_router_gate), "gate_w": np.asarray(L0_ffn_gate_w), "up_w": np.asarray(L0_ffn_up_w),
        "down_w": np.asarray(L0_ffn_down_w),
    }
    arrays = {n: np.ascontiguousarray(a) for n, a in arrays.items()}
    nc = bacc.Bacc("TRN2", target_bir_lowering=False, num_devices=1)
    args = [nc.dram_tensor(n, a.shape, mybir.dt.from_np(a.dtype), kind="ExternalInput").ap() for n, a in arrays.items()]
    out = nc.dram_tensor("out", (T + TS, C), F32, kind="ExternalOutput").ap()
    flamingo_block(nc, *args, out)
    r = run(nc, [arrays], core_ids=[0])
    return r.results[0]["out"][:T].reshape(B, N, C)
```
